# Optimizing a Trainium2 kernel written in Bass

```python
import numpy as np
import jax
import jax.numpy as jnp

def _softmax(x, axis=-1):
    return jax.nn.softmax(x, axis=axis)

def _gelu(x):
    return jax.nn.gelu(x, approximate=True)

def _silu(x):
    return jax.nn.silu(x)

def _sigmoid(x):
    return jax.nn.sigmoid(x)

def _layernorm(x, axis=-1, eps=1e-05):
    m = jnp.mean(x, axis=axis, keepdims=True)
    v = jnp.var(x, axis=axis, keepdims=True)
    return (x - m) / jnp.sqrt(v + eps)

def _scatter_add(tgt, idx, src, axis=0):
    return tgt.at[idx].add(src)

def _segment_sum(src, seg, n):
    return jax.ops.segment_sum(src, seg, n)
kernel_name = 'mk_xattn_ffn_d4_seqx_r4_aeaf82'

def setup_inputs(seed: int=0):
    np.random.seed(seed)
    _w = jnp.asarray

    def _rec_inputs():
        import jax
        import jax.numpy as jnp
        _rk = jax.random.key(seed)
        x = -0.0003929 + 0.9999 * jax.random.normal(jax.random.fold_in(_rk, 1), (8, 112, 256), jnp.float32)
        _lenS = 112 - jax.random.randint(jax.random.fold_in(_rk, 7), (8,), 0, max(1, 112 // 4) + 1, jnp.int32)
        _lenS2 = 375 - jax.random.randint(jax.random.fold_in(_rk, 8), (8,), 0, max(1, 375 // 4) + 1, jnp.int32)
        _ctx_768P = jax.random.normal(jax.random.fold_in(_rk, 11), (8, 16, 192), jnp.float32)
        _ctx_768c = jax.random.dirichlet(jax.random.fold_in(_rk, 511), 0.3 * jnp.ones((16,), jnp.float32), (8, 375))
        _ctx_768t = jnp.einsum('bsk,bkd->bsd', _ctx_768c, _ctx_768P)
        _ctx_768t = _ctx_768t * jax.lax.rsqrt(jnp.mean(jnp.square(_ctx_768t)) + 1e-12) * 0.953939
        ctx_768 = -7.36909e-05 + 0.999899 * (_ctx_768t + 0.3 * jax.random.normal(jax.random.fold_in(_rk, 611), (8, 375, 192), jnp.float32))
        return (x, ctx_768)
    x, ctx_768 = _rec_inputs()

    def _L0_xattn_setup():
        import jax, jax.numpy as jnp
        import numpy as np
        EPS = 1e-05

        def layernorm(x, g, b):
            mu = jnp.mean(x, axis=-1, keepdims=True)
            var = jnp.mean(jnp.square(x - mu), axis=-1, keepdims=True)
            return (x - mu) * jax.lax.rsqrt(var + EPS) * g + b
        key = jax.random.key(seed)
        ks = jax.random.split(key, 12)
        B, L1, L2 = (8, 512, 512)
        D1, D2, E = (256, 192, 256)
        s1, s2, se = (D1 ** (-0.5), D2 ** (-0.5), E ** (-0.5))
        return {'modality1': jax.random.normal(ks[0], (B, L1, D1), jnp.float32), 'modality2': jax.random.normal(ks[1], (B, L2, D2), jnp.float32), 'ln1_g': jnp.ones((D1,), jnp.float32), 'ln1_b': jnp.zeros((D1,), jnp.float32), 'ln2_g': jnp.ones((D2,), jnp.float32), 'ln2_b': jnp.zeros((D2,), jnp.float32), 'Wq': jax.random.normal(ks[2], (D1, E), jnp.float32) * s1, 'bq': jax.random.normal(ks[3], (E,), jnp.float32) * 0.01, 'Wk': jax.random.normal(ks[4], (D2, E), jnp.float32) * s2, 'bk': jax.random.normal(ks[5], (E,), jnp.float32) * 0.01, 'Wv': jax.random.normal(ks[6], (D2, E), jnp.float32) * s2, 'bv': jax.random.normal(ks[7], (E,), jnp.float32) * 0.01, 'Wo': jax.random.normal(ks[8], (E, D1), jnp.float32) * se, 'bo': jax.random.normal(ks[9], (D1,), jnp.float32) * 0.01}
    _L0_xattn_all = _L0_xattn_setup()
    _L0_xattn_in = {k: v for k, v in _L0_xattn_all.items() if k in ('ln1_g', 'ln1_b', 'ln2_g', 'ln2_b', 'Wq', 'bq', 'Wk', 'bk', 'Wv', 'bv', 'Wo', 'bo')}
    del _L0_xattn_all

    def _L0_ffn_setup():
        import jax, jax.numpy as jnp
        import numpy as np
        B, S, D, E = (4, 1024, 256, 8)
        key = jax.random.key(seed)
        ks = jax.random.split(key, 6)
        scale = 1.0 / np.sqrt(D)
        return {'tokens': jax.random.normal(ks[0], (B, S, D), dtype=jnp.float32), 'gate_w': jax.random.normal(ks[1], (D, E), dtype=jnp.float32) * scale, 'w0': jax.random.normal(ks[2], (D, D), dtype=jnp.float32) * scale, 'b0': jax.random.normal(ks[3], (D,), dtype=jnp.float32) * 0.01, 'w1': jax.random.normal(ks[4], (D, D), dtype=jnp.float32) * scale, 'b1': jax.random.normal(ks[5], (D,), dtype=jnp.float32) * 0.01}
    _L0_ffn_all = _L0_ffn_setup()
    _L0_ffn_in = {k: v for k, v in _L0_ffn_all.items() if k in ('gate_w', 'w0', 'b0', 'w1', 'b1')}
    del _L0_ffn_all

    def _L1_xattn_setup():
        import jax, jax.numpy as jnp
        import numpy as np
        HEADS = 8
        DIM_HEAD = 128
        ATTN_MATRIX_SCALE = 1.5
        SCALE = DIM_HEAD ** (-0.5)

        def _split_heads(t):
            b, n, _ = t.shape
            t = t.reshape(b, n, HEADS, DIM_HEAD)
            return t.transpose(2, 0, 1, 3).reshape(HEADS, b * n, DIM_HEAD)
        key = jax.random.key(seed)
        ks = jax.random.split(key, 7)
        b, n, m = (2, 512, 512)
        qd, cd, inner = (256, 192, HEADS * DIM_HEAD)
        x = jax.random.normal(ks[0], (b, n, qd), dtype=jnp.float32)
        context = jax.random.normal(ks[1], (b, m, cd), dtype=jnp.float32)
        Wq = jax.random.normal(ks[2], (qd, inner), dtype=jnp.float32) * qd ** (-0.5)
        Wk = jax.random.normal(ks[3], (cd, inner), dtype=jnp.float32) * cd ** (-0.5)
        Wv = jax.random.normal(ks[4], (cd, inner), dtype=jnp.float32) * cd ** (-0.5)
        Wout = jax.random.normal(ks[5], (inner, qd), dtype=jnp.float32) * inner ** (-0.5)
        bout = jnp.zeros((qd,), dtype=jnp.float32)
        return {'x': x, 'context': context, 'Wq': Wq, 'Wk': Wk, 'Wv': Wv, 'Wout': Wout, 'bout': bout}
    _L1_xattn_all = _L1_xattn_setup()
    _L1_xattn_in = {k: v for k, v in _L1_xattn_all.items() if k in ('Wq', 'Wk', 'Wv', 'Wout', 'bout')}
    del _L1_xattn_all

    def _L1_ffn_setup():
        import jax, jax.numpy as jnp
        import numpy as np
        HIDDEN = 256
        INNER = 1024

        def _weight_quant(w):
            scale = 1.0 / jnp.clip(jnp.mean(jnp.abs(w)), 1e-05)
            wq = jnp.clip(jnp.round(w * scale), -1.0, 1.0) / scale
            return w + jax.lax.stop_gradient(wq - w)

        def _act_quant(x):
            scale = 127.0 / jnp.clip(jnp.max(jnp.abs(x), axis=-1, keepdims=True), 1e-05)
            xq = jnp.clip(jnp.round(x * scale), -128.0, 127.0) / scale
            return x + jax.lax.stop_gradient(xq - x)

        def _bitlinear(x, w):
            return jnp.einsum('bsi,oi->bso', _act_quant(x), _weight_quant(w))
        key = jax.random.key(seed)
        k0, k1, k2, k3 = jax.random.split(key, 4)
        x = jax.random.normal(k0, (4, 512, HIDDEN), dtype=jnp.float32)
        w_gate = jax.random.normal(k1, (INNER, HIDDEN), dtype=jnp.float32) / np.sqrt(HIDDEN)
        w_up = jax.random.normal(k2, (INNER, HIDDEN), dtype=jnp.float32) / np.sqrt(HIDDEN)
        w_down = jax.random.normal(k3, (HIDDEN, INNER), dtype=jnp.float32) / np.sqrt(INNER)
        return {'x': x, 'w_gate': w_gate, 'w_up': w_up, 'w_down': w_down}
    _L1_ffn_all = _L1_ffn_setup()
    _L1_ffn_in = {k: v for k, v in _L1_ffn_all.items() if k in ('w_gate', 'w_up', 'w_down')}
    del _L1_ffn_all

    def _L2_xattn_setup():
        import jax, jax.numpy as jnp
        import numpy as np
        HEADS = 16
        DIM_HEAD = 64
        SCALE = DIM_HEAD ** (-0.5)
        key = jax.random.key(seed)
        ks = jax.random.split(key, 6)
        B, N, C = (4, 1024, 256)
        M, Cc = (128, 192)
        inner = HEADS * DIM_HEAD
        s = lambda d: d ** (-0.5)
        return {'x': jax.random.normal(ks[0], (B, N, C), jnp.float32), 'context': jax.random.normal(ks[1], (B, M, Cc), jnp.float32), 'Wq': jax.random.normal(ks[2], (C, inner), jnp.float32) * s(C), 'Wk': jax.random.normal(ks[3], (Cc, inner), jnp.float32) * s(Cc), 'Wv': jax.random.normal(ks[4], (Cc, inner), jnp.float32) * s(Cc), 'Wo': jax.random.normal(ks[5], (inner, C), jnp.float32) * s(inner), 'bo': jnp.zeros((C,), jnp.float32)}
    _L2_xattn_all = _L2_xattn_setup()
    _L2_xattn_in = {k: v for k, v in _L2_xattn_all.items() if k in ('Wq', 'Wk', 'Wv', 'Wo', 'bo')}
    del _L2_xattn_all

    def _L2_ffn_setup():
        import jax, jax.numpy as jnp
        import numpy as np
        D_MODEL = 256
        HIDDEN = 1024
        NUM_EXPERTS = 8
        TOP_K = 2
        key = jax.random.key(seed)
        k_x, k_g, k_in, k_out = jax.random.split(key, 4)
        bound_in = 1.0 / HIDDEN
        bound_out = 1.0 / D_MODEL
        x = jax.random.normal(k_x, (2, 512, D_MODEL), dtype=jnp.float32)
        w_gate = jax.random.uniform(k_g, (NUM_EXPERTS, D_MODEL), dtype=jnp.float32, minval=-D_MODEL ** (-0.5), maxval=D_MODEL ** (-0.5))
        w_in = jax.random.uniform(k_in, (NUM_EXPERTS, HIDDEN, D_MODEL), dtype=jnp.float32, minval=-bound_in, maxval=bound_in)
        w_out = jax.random.uniform(k_out, (NUM_EXPERTS, D_MODEL, HIDDEN), dtype=jnp.float32, minval=-bound_out, maxval=bound_out)
        return {'x': x, 'w_gate': w_gate, 'w_in': w_in, 'w_out': w_out}
    _L2_ffn_all = _L2_ffn_setup()
    _L2_ffn_in = {k: v for k, v in _L2_ffn_all.items() if k in ('w_gate', 'w_in', 'w_out')}
    del _L2_ffn_all

    def _L3_xattn_setup():
        import jax, jax.numpy as jnp
        import numpy as np
        HEADS = 16
        DIM_HEAD = 64
        key = jax.random.key(seed)
        ks = jax.random.split(key, 8)
        B, S, D = (16, 1024, 256)
        K, DE = (77, 192)
        inner = HEADS * DIM_HEAD
        hidden_states = jax.random.normal(ks[0], (B, S, D), dtype=jnp.float32)
        encoder_hidden_states = jax.random.normal(ks[1], (B, K, DE), dtype=jnp.float32)
        sc_q = 1.0 / np.sqrt(D)
        sc_kv = 1.0 / np.sqrt(DE)
        sc_o = 1.0 / np.sqrt(inner)
        Wq = jax.random.normal(ks[2], (D, inner), dtype=jnp.float32) * sc_q
        Wk = jax.random.normal(ks[3], (DE, inner), dtype=jnp.float32) * sc_kv
        Wv = jax.random.normal(ks[4], (DE, inner), dtype=jnp.float32) * sc_kv
        Wo = jax.random.normal(ks[5], (inner, D), dtype=jnp.float32) * sc_o
        bo = jax.random.normal(ks[6], (D,), dtype=jnp.float32) * 0.01
        return {'hidden_states': hidden_states, 'encoder_hidden_states': encoder_hidden_states, 'Wq': Wq, 'Wk': Wk, 'Wv': Wv, 'Wo': Wo, 'bo': bo}
    _L3_xattn_all = _L3_xattn_setup()
    _L3_xattn_in = {k: v for k, v in _L3_xattn_all.items() if k in ('Wq', 'Wk', 'Wv', 'Wo', 'bo')}
    del _L3_xattn_all

    def _L3_ffn_setup():
        import jax, jax.numpy as jnp
        import numpy as np
        D_MODEL = 256
        HIDDEN = 256
        NUM_EXPERTS = 8
        TOP_K = 2
        key = jax.random.key(seed)
        ks = jax.random.split(key, 10)
        s = 0.02
        return {'x': jax.random.normal(ks[0], (2, 512, D_MODEL), dtype=jnp.float32), 'gate_w': jax.random.normal(ks[1], (NUM_EXPERTS, D_MODEL), dtype=jnp.float32) * s, 'up_w': jax.random.normal(ks[2], (NUM_EXPERTS, D_MODEL, HIDDEN), dtype=jnp.float32) * s, 'up_b': jnp.zeros((NUM_EXPERTS, HIDDEN), dtype=jnp.float32), 'down_w': jax.random.normal(ks[3], (NUM_EXPERTS, HIDDEN, D_MODEL), dtype=jnp.float32) * s, 'down_b': jnp.zeros((NUM_EXPERTS, D_MODEL), dtype=jnp.float32), 'sh_up_w': jax.random.normal(ks[4], (D_MODEL, HIDDEN), dtype=jnp.float32) * s, 'sh_up_b': jnp.zeros((HIDDEN,), dtype=jnp.float32), 'sh_down_w': jax.random.normal(ks[5], (HIDDEN, D_MODEL), dtype=jnp.float32) * s, 'sh_down_b': jnp.zeros((D_MODEL,), dtype=jnp.float32)}
    _L3_ffn_all = _L3_ffn_setup()
    _L3_ffn_in = {k: v for k, v in _L3_ffn_all.items() if k in ('gate_w', 'up_w', 'up_b', 'down_w', 'down_b', 'sh_up_w', 'sh_up_b', 'sh_down_w', 'sh_down_b')}
    del _L3_ffn_all
    return {'x': x, 'ctx_768': ctx_768, 'L0_xattn_ln1_g': _L0_xattn_in['ln1_g'], 'L0_xattn_ln1_b': _L0_xattn_in['ln1_b'], 'L0_xattn_ln2_g': _L0_xattn_in['ln2_g'], 'L0_xattn_ln2_b': _L0_xattn_in['ln2_b'], 'L0_xattn_Wq': _L0_xattn_in['Wq'], 'L0_xattn_bq': _L0_xattn_in['bq'], 'L0_xattn_Wk': _L0_xattn_in['Wk'], 'L0_xattn_bk': _L0_xattn_in['bk'], 'L0_xattn_Wv': _L0_xattn_in['Wv'], 'L0_xattn_bv': _L0_xattn_in['bv'], 'L0_xattn_Wo': _L0_xattn_in['Wo'], 'L0_xattn_bo': _L0_xattn_in['bo'], 'L0_ffn_gate_w': _L0_ffn_in['gate_w'], 'L0_ffn_w0': _L0_ffn_in['w0'], 'L0_ffn_b0': _L0_ffn_in['b0'], 'L0_ffn_w1': _L0_ffn_in['w1'], 'L0_ffn_b1': _L0_ffn_in['b1'], 'L1_xattn_Wq': _L1_xattn_in['Wq'], 'L1_xattn_Wk': _L1_xattn_in['Wk'], 'L1_xattn_Wv': _L1_xattn_in['Wv'], 'L1_xattn_Wout': _L1_xattn_in['Wout'], 'L1_xattn_bout': _L1_xattn_in['bout'], 'L1_ffn_w_gate': _L1_ffn_in['w_gate'], 'L1_ffn_w_up': _L1_ffn_in['w_up'], 'L1_ffn_w_down': _L1_ffn_in['w_down'], 'L2_xattn_Wq': _L2_xattn_in['Wq'], 'L2_xattn_Wk': _L2_xattn_in['Wk'], 'L2_xattn_Wv': _L2_xattn_in['Wv'], 'L2_xattn_Wo': _L2_xattn_in['Wo'], 'L2_xattn_bo': _L2_xattn_in['bo'], 'L2_ffn_w_gate': _L2_ffn_in['w_gate'], 'L2_ffn_w_in': _L2_ffn_in['w_in'], 'L2_ffn_w_out': _L2_ffn_in['w_out'], 'L3_xattn_Wq': _L3_xattn_in['Wq'], 'L3_xattn_Wk': _L3_xattn_in['Wk'], 'L3_xattn_Wv': _L3_xattn_in['Wv'], 'L3_xattn_Wo': _L3_xattn_in['Wo'], 'L3_xattn_bo': _L3_xattn_in['bo'], 'L3_ffn_gate_w': _L3_ffn_in['gate_w'], 'L3_ffn_up_w': _L3_ffn_in['up_w'], 'L3_ffn_up_b': _L3_ffn_in['up_b'], 'L3_ffn_down_w': _L3_ffn_in['down_w'], 'L3_ffn_down_b': _L3_ffn_in['down_b'], 'L3_ffn_sh_up_w': _L3_ffn_in['sh_up_w'], 'L3_ffn_sh_up_b': _L3_ffn_in['sh_up_b'], 'L3_ffn_sh_down_w': _L3_ffn_in['sh_down_w'], 'L3_ffn_sh_down_b': _L3_ffn_in['sh_down_b']}

def reference(x, ctx_768, L0_xattn_ln1_g, L0_xattn_ln1_b, L0_xattn_ln2_g, L0_xattn_ln2_b, L0_xattn_Wq, L0_xattn_bq, L0_xattn_Wk, L0_xattn_bk, L0_xattn_Wv, L0_xattn_bv, L0_xattn_Wo, L0_xattn_bo, L0_ffn_gate_w, L0_ffn_w0, L0_ffn_b0, L0_ffn_w1, L0_ffn_b1, L1_xattn_Wq, L1_xattn_Wk, L1_xattn_Wv, L1_xattn_Wout, L1_xattn_bout, L1_ffn_w_gate, L1_ffn_w_up, L1_ffn_w_down, L2_xattn_Wq, L2_xattn_Wk, L2_xattn_Wv, L2_xattn_Wo, L2_xattn_bo, L2_ffn_w_gate, L2_ffn_w_in, L2_ffn_w_out, L3_xattn_Wq, L3_xattn_Wk, L3_xattn_Wv, L3_xattn_Wo, L3_xattn_bo, L3_ffn_gate_w, L3_ffn_up_w, L3_ffn_up_b, L3_ffn_down_w, L3_ffn_down_b, L3_ffn_sh_up_w, L3_ffn_sh_up_b, L3_ffn_sh_down_w, L3_ffn_sh_down_b):
    import jax
    import jax.numpy as jnp

    def _L0_xattn_ref(modality1, modality2, ln1_g, ln1_b, ln2_g, ln2_b, Wq, bq, Wk, bk, Wv, bv, Wo, bo):
        import jax, jax.numpy as jnp
        import numpy as np
        EPS = 1e-05

        def layernorm(x, g, b):
            mu = jnp.mean(x, axis=-1, keepdims=True)
            var = jnp.mean(jnp.square(x - mu), axis=-1, keepdims=True)
            return (x - mu) * jax.lax.rsqrt(var + EPS) * g + b
        E = Wq.shape[1]
        scaling = E ** (-0.5)
        x1 = layernorm(modality1, ln1_g, ln1_b)
        x2 = layernorm(modality2, ln2_g, ln2_b)
        q = x1 @ Wq + bq
        k = x2 @ Wk + bk
        v = x2 @ Wv + bv
        scores = jnp.einsum('bqe,bke->bqk', q, k) * scaling
        attn = jax.nn.softmax(scores, axis=-1)
        ctx = jnp.einsum('bqk,bke->bqe', attn, v)
        return ctx @ Wo + bo

    def _L0_ffn_ref(tokens, gate_w, w0, b0, w1, b1):
        import jax, jax.numpy as jnp
        import numpy as np
        B, S, D, E = (4, 1024, 256, 8)
        b, s, d = tokens.shape
        logits = jnp.einsum('bsd,de->bse', tokens, gate_w)
        weights = jax.nn.softmax(logits, axis=-1)
        topk_w, topk_idx = jax.lax.top_k(weights, 2)
        x = tokens.reshape(b * s, d)
        fw = topk_w.reshape(b * s, 2)
        fidx = topk_idx.reshape(b * s, 2)
        e0 = jax.nn.silu(x @ w0.T + b0)
        e1 = jax.nn.silu(x @ w1.T + b1)
        m0 = (fidx[:, 0:1] == 0).astype(x.dtype)
        m1 = (fidx[:, 1:2] == 1).astype(x.dtype)
        out = e0 * fw[:, 0:1] * m0 + e1 * fw[:, 1:2] * m1
        return out.reshape(b, s, d)

    def _L1_xattn_ref(x, context, Wq, Wk, Wv, Wout, bout):
        import jax, jax.numpy as jnp
        import numpy as np
        HEADS = 8
        DIM_HEAD = 128
        ATTN_MATRIX_SCALE = 1.5
        SCALE = DIM_HEAD ** (-0.5)

        def _split_heads(t):
            b, n, _ = t.shape
            t = t.reshape(b, n, HEADS, DIM_HEAD)
            return t.transpose(2, 0, 1, 3).reshape(HEADS, b * n, DIM_HEAD)
        b, n, _ = x.shape
        qh = _split_heads(jnp.einsum('bnq,qi->bni', x, Wq))
        kh = _split_heads(jnp.einsum('bmc,ci->bmi', context, Wk))
        vh = _split_heads(jnp.einsum('bmc,ci->bmi', context, Wv))
        sim = jnp.einsum('hid,hjd->hij', qh, kh) * SCALE
        mean = jnp.mean(sim, axis=-1, keepdims=True)
        sim = (sim - mean) * ATTN_MATRIX_SCALE + mean
        attn = jax.nn.softmax(sim, axis=-1)
        out = jnp.einsum('hij,hjd->hid', attn, vh)
        out = out.reshape(HEADS, b, n, DIM_HEAD).transpose(1, 2, 0, 3)
        out = out.reshape(b, n, HEADS * DIM_HEAD)
        return jnp.einsum('bni,iq->bnq', out, Wout) + bout

    def _L1_ffn_ref(x, w_gate, w_up, w_down):
        import jax, jax.numpy as jnp
        import numpy as np
        HIDDEN = 256
        INNER = 1024

        def _weight_quant(w):
            scale = 1.0 / jnp.clip(jnp.mean(jnp.abs(w)), 1e-05)
            wq = jnp.clip(jnp.round(w * scale), -1.0, 1.0) / scale
            return w + jax.lax.stop_gradient(wq - w)

        def _act_quant(x):
            scale = 127.0 / jnp.clip(jnp.max(jnp.abs(x), axis=-1, keepdims=True), 1e-05)
            xq = jnp.clip(jnp.round(x * scale), -128.0, 127.0) / scale
            return x + jax.lax.stop_gradient(xq - x)

        def _bitlinear(x, w):
            return jnp.einsum('bsi,oi->bso', _act_quant(x), _weight_quant(w))
        gate = jax.nn.silu(_bitlinear(x, w_gate))
        up = _bitlinear(x, w_up)
        return _bitlinear(gate * up, w_down)

    def _L2_xattn_ref(x, context, Wq, Wk, Wv, Wo, bo):
        import jax, jax.numpy as jnp
        import numpy as np
        HEADS = 16
        DIM_HEAD = 64
        SCALE = DIM_HEAD ** (-0.5)
        B, N, _ = x.shape
        M = context.shape[1]
        q = (x @ Wq).reshape(B, N, HEADS, DIM_HEAD).transpose(0, 2, 1, 3)
        k = (context @ Wk).reshape(B, M, HEADS, DIM_HEAD).transpose(0, 2, 1, 3)
        v = (context @ Wv).reshape(B, M, HEADS, DIM_HEAD).transpose(0, 2, 1, 3)
        dots = jnp.einsum('bhnd,bhmd->bhnm', q, k) * SCALE
        attn = jax.nn.softmax(dots, axis=-1)
        out = jnp.einsum('bhnm,bhmd->bhnd', attn, v)
        out = out.transpose(0, 2, 1, 3).reshape(B, N, HEADS * DIM_HEAD)
        return out @ Wo + bo

    def _L2_ffn_ref(x, w_gate, w_in, w_out):
        import jax, jax.numpy as jnp
        import numpy as np
        D_MODEL = 256
        HIDDEN = 1024
        NUM_EXPERTS = 8
        TOP_K = 2
        B, S, D = x.shape
        E = w_in.shape[0]
        xt = x.reshape(-1, D)
        logits = (xt @ w_gate.T).astype(jnp.float32)
        top_logits, top_idx = jax.lax.top_k(logits, TOP_K)
        top_gates = jax.nn.softmax(top_logits, axis=-1).astype(x.dtype)
        gates = (jax.nn.one_hot(top_idx, E, dtype=x.dtype) * top_gates[..., None]).sum(axis=1)
        y = jnp.zeros_like(xt)
        for e in range(E):
            h = xt @ w_in[e].T
            y = y + gates[:, e:e + 1] * (h @ w_out[e].T)
        return y.reshape(B, S, D)

    def _L3_xattn_ref(hidden_states, encoder_hidden_states, Wq, Wk, Wv, Wo, bo):
        import jax, jax.numpy as jnp
        import numpy as np
        HEADS = 16
        DIM_HEAD = 64
        B, S, D = hidden_states.shape
        K = encoder_hidden_states.shape[1]
        H, Dh = (HEADS, DIM_HEAD)
        scale = 1.0 / np.sqrt(Dh)
        q = hidden_states @ Wq
        k = encoder_hidden_states @ Wk
        v = encoder_hidden_states @ Wv
        q = q.reshape(B, S, H, Dh).transpose(0, 2, 1, 3)
        k = k.reshape(B, K, H, Dh).transpose(0, 2, 1, 3)
        v = v.reshape(B, K, H, Dh).transpose(0, 2, 1, 3)
        scores = jnp.einsum('bhsd,bhkd->bhsk', q, k) * scale
        probs = jax.nn.softmax(scores, axis=-1)
        out = jnp.einsum('bhsk,bhkd->bhsd', probs, v)
        out = out.transpose(0, 2, 1, 3).reshape(B, S, H * Dh)
        out = out @ Wo + bo
        return out

    def _L3_ffn_ref(x, gate_w, up_w, up_b, down_w, down_b, sh_up_w, sh_up_b, sh_down_w, sh_down_b):
        import jax, jax.numpy as jnp
        import numpy as np
        D_MODEL = 256
        HIDDEN = 256
        NUM_EXPERTS = 8
        TOP_K = 2
        b, s, d = x.shape
        xf = x.reshape(-1, d)
        shared = jax.nn.silu(x @ sh_up_w + sh_up_b) @ sh_down_w + sh_down_b
        logits = xf @ gate_w.T
        scores = jax.nn.softmax(logits, axis=-1)
        topk_w, topk_i = jax.lax.top_k(scores, TOP_K)
        topk_w = topk_w / (topk_w.sum(axis=-1, keepdims=True) + 1e-20)
        comb = (jax.nn.one_hot(topk_i, NUM_EXPERTS, dtype=xf.dtype) * topk_w[..., None]).sum(axis=1)
        h = jnp.einsum('nd,edh->neh', xf, up_w) + up_b
        h = jax.nn.silu(h)
        ye = jnp.einsum('neh,ehd->ned', h, down_w) + down_b
        y = jnp.einsum('ned,ne->nd', ye, comb).reshape(b, s, d)
        return y + shared
    x = x + _L0_xattn_ref(_layernorm(x, axis=-1), ctx_768, L0_xattn_ln1_g, L0_xattn_ln1_b, L0_xattn_ln2_g, L0_xattn_ln2_b, L0_xattn_Wq, L0_xattn_bq, L0_xattn_Wk, L0_xattn_bk, L0_xattn_Wv, L0_xattn_bv, L0_xattn_Wo, L0_xattn_bo)
    x = x + _L0_ffn_ref(_layernorm(x, axis=-1), L0_ffn_gate_w, L0_ffn_w0, L0_ffn_b0, L0_ffn_w1, L0_ffn_b1)
    x = x + _L1_xattn_ref(_layernorm(x, axis=-1), ctx_768, L1_xattn_Wq, L1_xattn_Wk, L1_xattn_Wv, L1_xattn_Wout, L1_xattn_bout)
    x = x + _L1_ffn_ref(_layernorm(x, axis=-1), L1_ffn_w_gate, L1_ffn_w_up, L1_ffn_w_down)
    x = x + _L2_xattn_ref(_layernorm(x, axis=-1), ctx_768, L2_xattn_Wq, L2_xattn_Wk, L2_xattn_Wv, L2_xattn_Wo, L2_xattn_bo)
    x = x + _L2_ffn_ref(_layernorm(x, axis=-1), L2_ffn_w_gate, L2_ffn_w_in, L2_ffn_w_out)
    x = x + _L3_xattn_ref(_layernorm(x, axis=-1), ctx_768, L3_xattn_Wq, L3_xattn_Wk, L3_xattn_Wv, L3_xattn_Wo, L3_xattn_bo)
    x = x + _L3_ffn_ref(_layernorm(x, axis=-1), L3_ffn_gate_w, L3_ffn_up_w, L3_ffn_up_b, L3_ffn_down_w, L3_ffn_down_b, L3_ffn_sh_up_w, L3_ffn_sh_up_b, L3_ffn_sh_down_w, L3_ffn_sh_down_b)
    return x

_drawn_inputs = setup_inputs


def setup_inputs(seed=0):
    import zlib

    import numpy as np

    out = dict(_drawn_inputs(seed))
    spreads = {'L0_xattn_ln1_g': (1.0, 0.2),
     'L0_xattn_ln1_b': (0.0, 0.427),
     'L0_xattn_ln2_g': (1.0, 0.2),
     'L0_xattn_ln2_b': (0.0, 0.1),
     'L1_xattn_bout': (0.0, 0.1),
     'L2_xattn_bo': (0.0, 0.1),
     'L3_ffn_up_b': (0.0, 0.8),
     'L3_ffn_down_b': (0.0, 0.1),
     'L3_ffn_sh_up_b': (0.0, 0.8),
     'L3_ffn_sh_down_b': (0.0, 0.1)}
    factors = {'L0_xattn_bq': 34.797,
     'L0_xattn_bk': 200.0,
     'L0_xattn_bv': 6.873,
     'L0_xattn_bo': 5.995,
     'L0_ffn_b0': 64.0,
     'L0_ffn_b1': 64.0,
     'L2_ffn_w_gate': 21.838,
     'L2_ffn_w_in': 8.0,
     'L2_ffn_w_out': 8.0,
     'L3_xattn_bo': 7.844}
    for name, (base, spread) in spreads.items():
        noise = np.random.default_rng([zlib.crc32(name.encode()), seed]).standard_normal(out[name].shape)
        drawn = base * np.exp(spread * noise) if base else spread * noise
        out[name] = jnp.asarray(drawn.astype(out[name].dtype))
    for name, factor in factors.items():
        out[name] = (out[name] * factor).astype(out[name].dtype)
    return out
```

```python
from contextlib import ExitStack, contextmanager

import concourse.bass as bass
from concourse import mybir

F32 = mybir.dt.float32
F32R = mybir.dt.float32r
BF16 = mybir.dt.bfloat16
ALU = mybir.AluOpType
ACT = mybir.ActivationFunctionType
AX = mybir.AxisListType

P = 128
BATCH, SEQ, D = 8, 112, 256
KEYS, DC = 375, 192
TOK = BATCH * SEQ
TILES = TOK // P
KT = D // P
NK = BATCH * KEYS
KB = 125
KTILES = NK // KB
TAIL = DC - P
CHUNK = 500
CHUNKS = NK // CHUNK
GROUPS = (TILES + 1) // 2
HEADS = 8
EPS = 1e-5
EXPERTS = 8
MAGIC = 1.5 * 2.0 ** 23


def need(eng, semaphore, value):
    if not (isinstance(value, int) and value <= 0):
        eng.wait_ge(semaphore, value)


@contextmanager
def phase_semaphores(nc, prefix=""):
    taken = []

    def sem(name):
        taken.append(nc.alloc_semaphore(name=prefix + name))
        return taken[-1]

    yield sem
    nc.clear_and_free_semaphores(taken)
    nc.all_engine_barrier()


class Names:
    pass


def layer_norm_buffers(sb, tag, width=TILES, rows=P):
    b = Names()
    b.stats = sb(f"{tag}_stats", [rows, width, 6])
    b.mean_var = sb(f"{tag}_mean_var", [rows, width, 2])
    b.root = sb(f"{tag}_root", [rows, 6, width])
    return b


def layer_norm_semaphores(sem, tag):
    q = Names()
    q.stats = sem(f"{tag}_stats_done")
    q.aggr = sem(f"{tag}_aggr_done")
    q.var = sem(f"{tag}_var_ready")
    q.std = sem(f"{tag}_std_ready")
    q.newton = sem(f"{tag}_newton_step")
    q.normed = sem(f"{tag}_normed")
    q.turned = sem(f"{tag}_turned")
    q.high = sem(f"{tag}_high_done")
    q.done = sem(f"{tag}_low_done")
    return q


def layer_norm_vector(dve, b, q, src, dst, width=TILES, ready=None):
    for i in range(width):
        if ready is not None:
            dve.wait_ge(*ready(i))
        dve.bn_stats(b.stats[:, i, :], src[:, i, :]).then_inc(q.stats, 1)
    dve.wait_ge(q.stats, width)
    for i in range(width):
        dve.bn_aggr(b.mean_var[:, i, :], b.stats[:, i, :]).then_inc(q.aggr, 1)
    dve.wait_ge(q.aggr, width)
    var, std, y0, t, u, y = (b.root[:, k, :] for k in range(6))
    dve.tensor_scalar(var, b.mean_var[:, :, 1], EPS, None, ALU.add).then_inc(q.var, 1)
    dve.wait_ge(q.std, 1)
    dve.reciprocal(y0, std).then_inc(q.newton, 1)
    dve.wait_ge(q.newton, 1)
    dve.tensor_tensor(t, y0, y0, ALU.mult).then_inc(q.newton, 1)
    dve.wait_ge(q.newton, 2)
    dve.scalar_tensor_tensor(u, t, -0.5, var, ALU.mult, ALU.mult).then_inc(q.newton, 1)
    dve.wait_ge(q.newton, 3)
    dve.scalar_tensor_tensor(y, u, 1.5, y0, ALU.add, ALU.mult).then_inc(q.newton, 1)
    dve.wait_ge(q.newton, 4)
    for i in range(width):
        dve.tensor_scalar(dst[:, i, :], src[:, i, :], b.mean_var[:, i, 0:1], y[:, i:i + 1],
                          ALU.subtract, ALU.mult).then_inc(q.normed, 1)


def layer_norm_scalar(act, b, q):
    act.wait_ge(q.var, 1)
    act.activation(b.root[:, 1, :], b.root[:, 0, :], ACT.Sqrt).then_inc(q.std, 1)


def turn_tensor(pe, q, src, banks, ident):
    for g in range(GROUPS):
        tiles = range(2 * g, min(2 * g + 2, TILES))
        pe.wait_ge(q.normed, tiles[-1] + 1)
        for i in tiles:
            for k in range(KT):
                at = k * 2 * P + (i % 2) * P
                last = pe.transpose(banks[g][:, at:at + P], src[:, i, k * P:(k + 1) * P], ident)
        last.then_inc(q.turned, 1)


def turned_view(bank, g):
    width = min(2 * P, TOK - g * 2 * P)
    return bank[:, :].rearrange("p (k c) -> p k c", k=KT)[:, :, 0:width], slice(g * 2 * P, g * 2 * P + width)


def turn_scalar(act, q, banks, TH):
    for g in range(GROUPS):
        view, cols = turned_view(banks[g], g)
        act.wait_ge(q.turned, g + 1)
        act.activation(TH[:, :, cols], view, ACT.Copy).then_inc(q.high, 1)


def turn_vector(dve, q, banks, TH, TL):
    for g in range(GROUPS):
        view, cols = turned_view(banks[g], g)
        dve.wait_ge(q.high, g + 1)
        dve.tensor_tensor(TL[:, :, cols], view, TH[:, :, cols].bitcast(F32), ALU.subtract).then_inc(q.done, 1)


def split_products(pe, out, terms, start=True, stop=True):
    for n, (a, b) in enumerate(terms):
        last = pe.matmul(out, a, b, start=start and n == 0, stop=stop and n == len(terms) - 1)
    return last


def layer0_attention(nc, s, dram):
    with ExitStack() as ctx:
        def sb(name, shape, dt=F32):
            return ctx.enter_context(nc.sbuf_tensor(name, shape, dt))

        sem = ctx.enter_context(phase_semaphores(nc))

        ctx_rows = sb("a0_ctx_rows", [KB, KTILES, DC])
        raw_main = sb("a0_raw_main", [P, NK])
        raw_tail = sb("a0_raw_tail", [P, NK])
        c_main = sb("a0_c_main", [P, NK])
        c_tail = sb("a0_c_tail", [TAIL, NK])
        kT = sb("a0_kT", [P, KT, NK])
        v = sb("a0_v", [KB, KTILES, D])
        xa = sb("a0_xa", [P, TILES, D])
        xT = sb("a0_xT", [P, KT, TOK])
        qT = sb("a0_qT", [P, KT, TOK])
        w_k = sb("a0_w_k", [P, 2, D])
        w_v = sb("a0_w_v", [P, 2, D])
        w_q = sb("a0_w_q", [P, KT, D])
        w_o = sb("a0_w_o", [P, KT, D])
        cols = sb("a0_cols", [P, 12])
        rows = sb("a0_rows", [P, 2, D])
        prob = sb("a0_prob", [SEQ, 2, KEYS])
        pT = sb("a0_pT", [KB, 2, 3, SEQ])
        nmax = sb("a0_nmax", [SEQ, 2])
        rsum = sb("a0_rsum", [SEQ, 2])
        rinv = sb("a0_rinv", [SEQ, 2])
        tail_high = sb("a0_tail_high", [P, NK // 2], F32R)
        oT = xT
        ln_c = layer_norm_buffers(sb, "a0_ln_c", KTILES, KB)
        ln_x = layer_norm_buffers(sb, "a0_ln_x")
        ln_y = layer_norm_buffers(sb, "a0_ln_y")
        qc = layer_norm_semaphores(sem, "a0_lc")
        qx = layer_norm_semaphores(sem, "a0_lx")
        qy = layer_norm_semaphores(sem, "a0_ly")
        g1, b1 = cols[:, 0:2], cols[:, 2:4]
        g2, b2 = cols[:, 4:6], cols[:, 6:8]
        bq, bk = cols[:, 8:10], cols[:, 10:12]

        LOADS = 4
        PER = KTILES // LOADS
        ctx_loaded = [sem(f"a0_ctx_loaded{n}") for n in range(LOADS)]
        x_loaded = sem("a0_x_loaded")
        small_loaded = sem("a0_small_loaded")
        w_loaded = sem("a0_w_loaded")
        raw_loaded = sem("a0_raw_loaded")
        c_main_done, c_tail_done = sem("a0_c_main_done"), sem("a0_c_tail_done")
        c_turned = sem("a0_c_turned")
        k_filled, k_done = sem("a0_k_filled"), sem("a0_k_done")
        v_filled, v_done = sem("a0_v_filled"), sem("a0_v_done")
        q_filled, q_done = sem("a0_q_filled"), sem("a0_q_done")
        xT_done = sem("a0_xT_done")
        s_filled, max_ready, exp_done, p_normed = (sem("a0_s_filled"), sem("a0_max_ready"),
                                                   sem("a0_exp_done"), sem("a0_p_normed"))
        rinv_ready = sem("a0_rinv_ready")
        t_filled, t_done, o_filled, o_done = (sem("a0_t_filled"), sem("a0_t_done"),
                                              sem("a0_o_filled"), sem("a0_o_done"))
        y_filled, y_added, bias_added = sem("a0_y_filled"), sem("a0_y_added"), sem("a0_bias_added")
        cut_high, cut_done = sem("a0_cut_high"), sem("a0_cut_done")
        B = s.banks
        GRP = 4
        NG = KTILES // GRP

        block = ctx.enter_context(nc.Block())

        @block.sync
        def _(sp):
            c_dram = dram["ctx_rows"].rearrange("(j p) d -> p j d", p=KB)
            for n in range(LOADS):
                sp.dma_start(ctx_rows[:, n * PER:(n + 1) * PER, :],
                             c_dram[:, n * PER:(n + 1) * PER, :]).then_inc(ctx_loaded[n], 16)
            sp.dma_start(s.x[:], dram["x"].rearrange("(t p) d -> p t d", p=P)).then_inc(x_loaded, 16)
            sp.dma_start(s.ident[:], dram["ident"]).then_inc(small_loaded, 16)
            sp.dma_start(s.ones[:], dram["ones"]).then_inc(small_loaded, 16)
            sp.dma_start(s.earlier[:], dram["earlier"]).then_inc(small_loaded, 16)
            sp.dma_start(cols[:], dram["a0_cols"]).then_inc(small_loaded, 16)
            sp.dma_start(rows[:], dram["a0_rows"]).then_inc(small_loaded, 16)
            for w, name in ((w_k, "a0_wk"), (w_v, "a0_wv")):
                sp.dma_start(w[:, 0, :], dram[name][0:P, :]).then_inc(w_loaded, 16)
                sp.dma_start(w[0:TAIL, 1, :], dram[name][P:DC, :]).then_inc(w_loaded, 16)
            for w, name in ((w_q, "a0_wq"), (w_o, "a0_wo")):
                sp.dma_start(w[:], dram[name].rearrange("(k p) n -> p k n", p=P)).then_inc(w_loaded, 16)
            sp.dma_start(raw_main[:], dram["ctx_cols"][0:P, :]).then_inc(raw_loaded, 16)
            sp.dma_start(raw_tail[0:TAIL, :], dram["ctx_cols"][P:DC, :]).then_inc(raw_loaded, 16)
            sp.dma_start(raw_tail[TAIL:P, :], dram["ctx_cols"][P:DC, :]).then_inc(raw_loaded, 16)

        @block.gpsimd
        def _(pool):
            pool.wait_ge(raw_loaded, 48)
            pool.tensor_copy(s.ctxH[:], raw_main[:]).then_inc(cut_high, 1)
            pool.wait_ge(cut_high, 1)
            pool.tensor_tensor(s.ctxL[:], raw_main[:], s.ctxH[:].bitcast(F32), ALU.subtract).then_inc(cut_done, 1)
            pool.wait_ge(cut_done, 1)
            pool.tensor_copy(s.ctxT[0:TAIL, :], raw_tail[0:TAIL, :]).then_inc(cut_done, 1)
            for n in range(2):
                half = slice(n * NK // 2, (n + 1) * NK // 2)
                pool.wait_ge(cut_done, n + 2)
                pool.tensor_copy(tail_high[TAIL:P, :], raw_tail[TAIL:P, half]).then_inc(cut_high, 1)
                pool.wait_ge(cut_high, n + 2)
                pool.tensor_tensor(s.ctxT[TAIL:P, half], raw_tail[TAIL:P, half],
                                   tail_high[TAIL:P, :].bitcast(F32), ALU.subtract).then_inc(cut_done, 1)

        @block.vector
        def _(dve):
            layer_norm_vector(dve, ln_c, qc, ctx_rows, ctx_rows, KTILES,
                              ready=lambda i: (ctx_loaded[i // PER], 16))
            dve.wait_ge(x_loaded, 16)
            layer_norm_vector(dve, ln_x, qx, s.x, xa)
            dve.wait_ge(small_loaded, 80)
            for g in range(NG):
                dve.wait_ge(c_turned, g + 1)
                dve.tensor_scalar(c_tail[:, g * CHUNK:(g + 1) * CHUNK], B[2 + g % 2][0:TAIL, 0:CHUNK],
                                  g2[0:TAIL, 1:2], b2[0:TAIL, 1:2], ALU.mult, ALU.add).then_inc(c_tail_done, 1)
            dve.wait_ge(qx.normed, TILES)
            layer_norm_vector(dve, ln_y, qy, xa, xa)
            dve.tensor_tensor(s.x[:], s.x[:], rows[:, 1:2, :].to_broadcast([P, TILES, D]),
                              ALU.add).then_inc(bias_added, 1)
            for n in range(4):
                dve.wait_ge(q_filled, n + 1)
                e, half = n // 2, slice((n % 2) * 448, (n % 2) * 448 + 448)
                dve.tensor_scalar(qT[:, e, half], B[4 + n][:, 0:448], bq[:, e:e + 1], D ** -0.5,
                                  ALU.add, ALU.mult).then_inc(q_done, 1)
            for n in range(KTILES // 2):
                dve.wait_ge(v_filled, n + 1)
                dve.tensor_tensor(v[:, 2 * n:2 * n + 2, :],
                                  B[2 + n % 2][0:KB, :].rearrange("p (t d) -> p t d", t=2),
                                  rows[0:KB, 0:1, :].to_broadcast([KB, 2, D]), ALU.add).then_inc(v_done, 1)

            def soft_max(b):
                dve.wait_ge(s_filled, b + 1)
                dve.tensor_reduce(nmax[:, b % 2:b % 2 + 1], B[b % 2][0:SEQ, 0:KEYS], AX.X, ALU.max,
                                  negate=True).then_inc(max_ready, 1)

            soft_max(0)
            for b in range(BATCH):
                if b + 1 < BATCH:
                    soft_max(b + 1)
                dve.wait_ge(exp_done, b + 1)
                dve.reciprocal(rinv[:, b % 2:b % 2 + 1], rsum[:, b % 2:b % 2 + 1]).then_inc(rinv_ready, 1)
                dve.wait_ge(rinv_ready, b + 1)
                dve.tensor_scalar(prob[:, b % 2, :], prob[:, b % 2, :], rinv[:, b % 2:b % 2 + 1], None,
                                  ALU.mult).then_inc(p_normed, 1)
                dve.wait_ge(o_filled, b + 1)
                dve.tensor_copy(oT[:, :, b * SEQ:(b + 1) * SEQ],
                                B[4 + b % 2][:, 0:KT * SEQ].rearrange("p (k c) -> p k c", k=KT)).then_inc(o_done, 1)
            dve.wait_ge(bias_added, 1)
            for i in range(TILES):
                dve.wait_ge(y_filled, i + 1)
                dve.tensor_tensor(s.x[:, i, :], s.x[:, i, :], B[6 + i % 2][:, 0:D], ALU.add).then_inc(y_added, 1)

        @block.scalar
        def _(act):
            layer_norm_scalar(act, ln_c, qc)
            layer_norm_scalar(act, ln_x, qx)
            act.wait_ge(small_loaded, 80)
            for g in range(NG):
                act.wait_ge(c_turned, g + 1)
                act.activation(c_main[:, g * CHUNK:(g + 1) * CHUNK], B[g % 2][:, 0:CHUNK], ACT.Identity,
                               scale=g2[:, 0:1], bias=b2[:, 0:1]).then_inc(c_main_done, 1)
            layer_norm_scalar(act, ln_y, qy)
            for g in range(GROUPS):
                view, c = turned_view(B[4 + g], g)
                act.wait_ge(qy.turned, g + 1)
                for k in range(KT):
                    act.activation(xT[:, k, c], view[:, k, :], ACT.Identity,
                                   scale=g1[:, k:k + 1], bias=b1[:, k:k + 1]).then_inc(xT_done, 1)
            for n in range(KT * CHUNKS):
                act.wait_ge(k_filled, n + 1)
                e, c = n // CHUNKS, n % CHUNKS
                act.activation(kT[:, e, c * CHUNK:(c + 1) * CHUNK], B[n % 2][:, 0:CHUNK], ACT.Identity,
                               bias=bk[:, e:e + 1]).then_inc(k_done, 1)
            for b in range(BATCH):
                act.wait_ge(max_ready, b + 1)
                act.activation(prob[:, b % 2, :], B[b % 2][0:SEQ, 0:KEYS], ACT.Exp, bias=nmax[:, b % 2:b % 2 + 1],
                               accum_out=rsum[:, b % 2:b % 2 + 1]).then_inc(exp_done, 1)
                act.wait_ge(t_filled, b + 1)
                act.activation(pT[:, b % 2, :, :], B[2 + b % 2][0:KB, 0:3 * SEQ].rearrange("p (t c) -> p t c", t=3),
                               ACT.Copy).then_inc(t_done, 1)

        @block.tensor
        def _(pe):
            pe.wait_ge(small_loaded, 80)
            pe.wait_ge(qc.normed, KTILES)
            for g in range(NG):
                need(pe, c_main_done, g - 1)
                need(pe, c_tail_done, g - 1)
                for j in range(GRP):
                    t, at = g * GRP + j, j * KB
                    pe.transpose(B[g % 2][:, at:at + KB], ctx_rows[:, t, 0:P], s.ident[0:KB, 0:KB])
                    last = pe.transpose(B[2 + g % 2][0:TAIL, at:at + KB], ctx_rows[:, t, P:DC], s.ident[0:KB, 0:KB])
                last.then_inc(c_turned, 1)
            turn_tensor(pe, qy, xa, B[4:8], s.ident[:])
            pe.wait_ge(w_loaded, 96)
            pe.wait_ge(c_main_done, NG)
            pe.wait_ge(c_tail_done, NG)
            for n in range(KT * CHUNKS):
                e, c = n // CHUNKS, n % CHUNKS
                need(pe, k_done, n - 1)
                split_products(pe, B[n % 2][:, 0:CHUNK], [
                    (w_k[:, 0, e * P:(e + 1) * P], c_main[:, c * CHUNK:(c + 1) * CHUNK]),
                    (w_k[0:TAIL, 1, e * P:(e + 1) * P], c_tail[:, c * CHUNK:(c + 1) * CHUNK])]).then_inc(k_filled, 1)
            pe.wait_ge(xT_done, KT * GROUPS)
            for n in range(4):
                e, half = n // 2, slice((n % 2) * 448, (n % 2) * 448 + 448)
                split_products(pe, B[4 + n][:, 0:448], [
                    (w_q[:, k, e * P:(e + 1) * P], xT[:, k, half]) for k in range(KT)]).then_inc(q_filled, 1)
            for n in range(KTILES // 2):
                need(pe, v_done, n - 1)
                for j in range(2):
                    t = 2 * n + j
                    last = split_products(pe, B[2 + n % 2][0:KB, j * D:(j + 1) * D], [
                        (c_main[:, t * KB:(t + 1) * KB], w_v[:, 0, :]),
                        (c_tail[:, t * KB:(t + 1) * KB], w_v[0:TAIL, 1, :])])
                last.then_inc(v_filled, 1)

            def scores(b):
                if b == 0:
                    pe.wait_ge(k_done, KT * CHUNKS)
                    pe.wait_ge(q_done, 4)
                need(pe, exp_done, b - 1)
                split_products(pe, B[b % 2][0:SEQ, 0:KEYS], [
                    (qT[:, k, b * SEQ:(b + 1) * SEQ], kT[:, k, b * KEYS:(b + 1) * KEYS])
                    for k in range(KT)]).then_inc(s_filled, 1)

            scores(0)
            for b in range(BATCH):
                if b + 1 < BATCH:
                    scores(b + 1)
                if b == 0:
                    pe.wait_ge(v_done, KTILES // 2)
                need(pe, t_done, b - 1)
                pe.wait_ge(p_normed, b + 1)
                for t in range(3):
                    last = pe.transpose(B[2 + b % 2][0:KB, t * SEQ:(t + 1) * SEQ], prob[:, b % 2, t * KB:(t + 1) * KB],
                                        s.ident[0:SEQ, 0:SEQ])
                last.then_inc(t_filled, 1)
                need(pe, o_done, b - 1)
                pe.wait_ge(t_done, b + 1)
                for e in range(KT):
                    last = split_products(pe, B[4 + b % 2][:, e * SEQ:(e + 1) * SEQ], [
                        (v[:, 3 * b + t, e * P:(e + 1) * P], pT[:, b % 2, t, :]) for t in range(3)])
                last.then_inc(o_filled, 1)
            pe.wait_ge(o_done, BATCH)
            for i in range(TILES):
                need(pe, y_added, i - 1)
                split_products(pe, B[6 + i % 2][:, 0:D], [
                    (oT[:, k, i * P:(i + 1) * P], w_o[:, k, :]) for k in range(KT)]).then_inc(y_filled, 1)


def router_buffers(sb, tag):
    r = Names()
    r.raw = sb(f"{tag}_gate_raw", [P, KT, EXPERTS])
    r.gH = sb(f"{tag}_gateH", [P, KT, EXPERTS], F32R)
    r.gL = sb(f"{tag}_gateL", [P, KT, EXPERTS], F32R)
    r.logits = sb(f"{tag}_logits", [P, TILES, EXPERTS])
    r.shifted = sb(f"{tag}_shifted", [P, TILES, EXPERTS])
    r.exps = sb(f"{tag}_exps", [P, TILES, EXPERTS])
    r.probs = sb(f"{tag}_probs", [P, TILES, EXPERTS])
    r.rank = sb(f"{tag}_rank", [P, TILES, EXPERTS])
    r.kept = sb(f"{tag}_kept", [P, TILES, EXPERTS])
    r.above = sb(f"{tag}_above", [P, TILES, EXPERTS, EXPERTS])
    r.ties = sb(f"{tag}_ties", [P, TILES, EXPERTS, EXPERTS])
    r.sums = sb(f"{tag}_sums", [P, 5, TILES])
    return r


def router_semaphores(sem, tag):
    q = Names()
    q.loaded = sem(f"{tag}_gate_loaded")
    q.cut = sem(f"{tag}_gate_cut")
    q.filled = sem(f"{tag}_logits_filled")
    q.step = sem(f"{tag}_route_step")
    q.shifted = sem(f"{tag}_logits_shifted")
    q.exps = sem(f"{tag}_exps_done")
    q.kept = sem(f"{tag}_route_ready")
    return q


def router_cut(pool, r, q):
    pool.wait_ge(q.loaded, 16)
    pool.tensor_copy(r.gH[:], r.raw[:]).then_inc(q.cut, 1)
    pool.wait_ge(q.cut, 1)
    pool.tensor_tensor(r.gL[:], r.raw[:], r.gH[:].bitcast(F32), ALU.subtract).then_inc(q.cut, 1)


def router_tensor(pe, s, r, q, bank):
    pe.wait_ge(q.cut, 2)
    for i in range(TILES):
        tok = slice(i * P, (i + 1) * P)
        last = split_products(pe, bank[:, i * EXPERTS:(i + 1) * EXPERTS], [
            pair for k in range(KT) for pair in (
                (s.xnTH[:, k, tok], r.gH[:, k, :]), (s.xnTH[:, k, tok], r.gL[:, k, :]),
                (s.xnTL[:, k, tok], r.gH[:, k, :]))])
    last.then_inc(q.filled, 1)


def router_scalar(act, r, q):
    act.wait_ge(q.shifted, 1)
    act.activation(r.exps[:], r.shifted[:], ACT.Exp).then_inc(q.exps, 1)


def over_experts(row):
    return row.unsqueeze(2).to_broadcast([P, TILES, EXPERTS])


def router_ranks(dve, s, r, q, key, at):
    every = [P, TILES, EXPERTS, EXPERTS]
    mine, others = key.unsqueeze(3).to_broadcast(every), key.unsqueeze(2).to_broadcast(every)
    dve.tensor_tensor(r.above[:], others, mine, ALU.is_gt).then_inc(q.step, 1)
    dve.tensor_tensor(r.ties[:], others, mine, ALU.is_equal).then_inc(q.step, 1)
    dve.wait_ge(q.step, at + 2)
    dve.tensor_tensor(r.ties[:], r.ties[:], s.earlier[:].unsqueeze(1).to_broadcast(every), ALU.mult).then_inc(q.step, 1)
    dve.wait_ge(q.step, at + 3)
    dve.tensor_tensor(r.above[:], r.above[:], r.ties[:], ALU.add).then_inc(q.step, 1)
    dve.wait_ge(q.step, at + 4)
    dve.tensor_reduce(r.rank[:], r.above[:], AX.X, ALU.add).then_inc(q.step, 1)
    dve.wait_ge(q.step, at + 5)
    return at + 5


def router_exps(dve, r, q, bank):
    dve.wait_ge(q.filled, 1)
    dve.tensor_copy(r.logits[:], bank[:, 0:TILES * EXPERTS].rearrange("p (t e) -> p t e", e=EXPERTS)).then_inc(q.step, 1)
    dve.wait_ge(q.step, 1)
    dve.tensor_reduce(r.sums[:, 0, :], r.logits[:], AX.X, ALU.max).then_inc(q.step, 1)
    dve.wait_ge(q.step, 2)
    dve.tensor_tensor(r.shifted[:], r.logits[:], over_experts(r.sums[:, 0, :]), ALU.subtract).then_inc(q.shifted, 1)
    return 2


def router_softmax(dve, r, q, at):
    dve.wait_ge(q.exps, 1)
    dve.tensor_reduce(r.sums[:, 1, :], r.exps[:], AX.X, ALU.add).then_inc(q.step, 1)
    dve.wait_ge(q.step, at + 1)
    dve.reciprocal(r.sums[:, 2, :], r.sums[:, 1, :]).then_inc(q.step, 1)
    dve.wait_ge(q.step, at + 2)
    dve.tensor_tensor(r.probs[:], r.exps[:], over_experts(r.sums[:, 2, :]), ALU.mult).then_inc(q.step, 1)
    dve.wait_ge(q.step, at + 3)
    return at + 3


def router_keep_two(dve, r, q, at, values, out, tiny):
    dve.scalar_tensor_tensor(r.kept[:], r.rank[:], 1.5, values, ALU.is_lt, ALU.mult).then_inc(q.step, 1)
    dve.wait_ge(q.step, at + 1)
    dve.tensor_reduce(r.sums[:, 3, :], r.kept[:], AX.X, ALU.add).then_inc(q.step, 1)
    dve.wait_ge(q.step, at + 2)
    dve.tensor_scalar(r.sums[:, 4, :], r.sums[:, 3, :], tiny, None, ALU.add).then_inc(q.step, 1)
    dve.wait_ge(q.step, at + 3)
    dve.reciprocal(r.sums[:, 2, :], r.sums[:, 4, :]).then_inc(q.step, 1)
    dve.wait_ge(q.step, at + 4)
    dve.tensor_tensor(out, r.kept[:], over_experts(r.sums[:, 2, :]), ALU.mult).then_inc(q.kept, 1)


def layer0_ffn(nc, s, dram):
    with ExitStack() as ctx:
        def sb(name, shape, dt=F32):
            return ctx.enter_context(nc.sbuf_tensor(name, shape, dt))

        sem = ctx.enter_context(phase_semaphores(nc))

        WIDE = 2 * D
        xn = sb("f0_xn", [P, TILES, D])
        w_raw = sb("f0_w_raw", [P, KT, WIDE])
        wH = sb("f0_wH", [P, KT, WIDE], F32R)
        wL = sb("f0_wL", [P, KT, WIDE], F32R)
        bias = sb("f0_bias", [P, WIDE])
        pre = sb("f0_pre", [P, 2, WIDE])
        post = sb("f0_post", [P, 2, WIDE])
        coef = sb("f0_coef", [P, 2, TILES])
        quant_raw = sb("f0_quant_raw", [P, 3, 2048])
        quant_work = sb("f0_quant_work", [P, 2048])
        ln = layer_norm_buffers(sb, "f0_ln")
        r = router_buffers(sb, "f0")
        ql = layer_norm_semaphores(sem, "f0_ln")
        q = router_semaphores(sem, "f0_r")
        w_loaded, w_cut = sem("f0_w_loaded"), sem("f0_w_cut")
        e_filled, pre_ready, post_ready, x_added = (sem("f0_e_filled"), sem("f0_pre_ready"),
                                                    sem("f0_post_ready"), sem("f0_x_added"))
        first_added = sem("f0_first_added")
        quant_loaded, abs_summed, abs_total = sem("f0_quant_loaded"), sem("f0_abs_summed"), sem("f0_abs_total")
        scale_step, scale_ready = sem("f0_scale_step"), sem("f0_scale_ready")
        quant_step, quant_done = sem("f0_quant_step"), sem("f0_quant_done")
        abs_sum = sb("f0_abs_sum", [P, 3])
        w_scale = sb("f0_w_scale", [P, 3])
        B = s.banks
        block = ctx.enter_context(nc.Block())

        @block.sync
        def _(sp):
            sp.dma_start(r.raw[:], dram["f0_gate"]).then_inc(q.loaded, 16)
            sp.dma_start(w_raw[:], dram["f0_w"]).then_inc(w_loaded, 16)
            sp.dma_start(bias[:], dram["f0_bias"]).then_inc(w_loaded, 16)
            sp.dma_start(quant_raw[:], dram["f1_w"]).then_inc(quant_loaded, 16)

        @block.gpsimd
        def _(pool):
            router_cut(pool, r, q)
            pool.wait_ge(w_loaded, 32)
            pool.tensor_copy(wH[:], w_raw[:]).then_inc(w_cut, 1)
            pool.wait_ge(w_cut, 1)
            pool.tensor_tensor(wL[:], w_raw[:], wH[:].bitcast(F32), ALU.subtract).then_inc(w_cut, 1)
            pool.wait_ge(scale_ready, 1)
            for m in range(3):
                need(pool, quant_done, m)
                pool.tensor_scalar(quant_work[:], quant_raw[:, m, :], w_scale[:, m:m + 1], MAGIC,
                                   ALU.mult, ALU.add).then_inc(quant_step, 1)
                pool.wait_ge(quant_step, 2 * m + 1)
                pool.tensor_scalar(quant_work[:], quant_work[:], MAGIC + 1.0, MAGIC - 1.0,
                                   ALU.min, ALU.max).then_inc(quant_step, 1)
                pool.wait_ge(quant_step, 2 * m + 2)
                pool.tensor_scalar(s.w_quant[:, m, :], quant_work[:], -MAGIC, 1.0,
                                   ALU.add, ALU.mult).then_inc(quant_done, 1)

        @block.vector
        def _(dve):
            layer_norm_vector(dve, ln, ql, s.x, xn)
            turn_vector(dve, ql, B[4:8], s.xnTH, s.xnTL)
            at = router_exps(dve, r, q, B[0])
            at = router_softmax(dve, r, q, at)
            at = router_ranks(dve, s, r, q, r.probs[:], at)
            for e in range(2):
                dve.scalar_tensor_tensor(coef[:, e, :], r.rank[:, :, e], float(e), r.probs[:, :, e],
                                         ALU.is_equal, ALU.mult).then_inc(q.kept, 1)
            dve.wait_ge(w_loaded, 32)

            def bias_add(i):
                dve.wait_ge(e_filled, i + 1)
                dve.tensor_tensor(pre[:, i % 2, :], B[1 + i % 2][:, :], bias[:], ALU.add).then_inc(pre_ready, 1)

            bias_add(0)
            for i in range(TILES):
                if i + 1 < TILES:
                    bias_add(i + 1)
                if i == 0:
                    dve.wait_ge(q.kept, 2)
                dve.wait_ge(post_ready, i + 1)
                dve.scalar_tensor_tensor(s.x[:, i, :], post[:, i % 2, 0:D], coef[:, 0, i:i + 1], s.x[:, i, :],
                                         ALU.mult, ALU.add).then_inc(first_added, 1)
                dve.wait_ge(first_added, i + 1)
                dve.scalar_tensor_tensor(s.x[:, i, :], post[:, i % 2, D:WIDE], coef[:, 1, i:i + 1], s.x[:, i, :],
                                         ALU.mult, ALU.add).then_inc(x_added, 1)
            dve.wait_ge(quant_loaded, 16)
            for m in range(3):
                dve.tensor_reduce(abs_sum[:, m:m + 1], quant_raw[:, m, :], AX.X, ALU.add,
                                  apply_absolute_value=True).then_inc(abs_summed, 1)
            dve.wait_ge(abs_total, 1)
            dve.tensor_scalar(s.w_mean[:], B[3][:, 0:3], 1.0 / (P * 2048), EPS, ALU.mult, ALU.max).then_inc(scale_step, 1)
            dve.wait_ge(scale_step, 1)
            dve.reciprocal(w_scale[:], s.w_mean[:]).then_inc(scale_ready, 1)

        @block.scalar
        def _(act):
            layer_norm_scalar(act, ln, ql)
            turn_scalar(act, ql, B[4:8], s.xnTH)
            router_scalar(act, r, q)
            for i in range(TILES):
                act.wait_ge(pre_ready, i + 1)
                need(act, x_added, i - 1)
                act.activation(post[:, i % 2, :], pre[:, i % 2, :], ACT.Silu).then_inc(post_ready, 1)

        @block.tensor
        def _(pe):
            turn_tensor(pe, ql, xn, B[4:8], s.ident[:])
            pe.wait_ge(ql.done, GROUPS)
            router_tensor(pe, s, r, q, B[0])
            pe.wait_ge(w_cut, 2)
            for i in range(TILES):
                tok = slice(i * P, (i + 1) * P)
                need(pe, pre_ready, i - 1)
                split_products(pe, B[1 + i % 2][:, :], [
                    pair for k in range(KT) for pair in (
                        (s.xnTH[:, k, tok], wH[:, k, :]), (s.xnTH[:, k, tok], wL[:, k, :]),
                        (s.xnTL[:, k, tok], wH[:, k, :]))]).then_inc(e_filled, 1)
            pe.wait_ge(abs_summed, 3)
            pe.matmul(B[3][:, 0:3], s.ones[:], abs_sum[:], start=True, stop=True).then_inc(abs_total, 1)
Q_W, K_W, V_W, O_W = slice(0, 2), slice(2, 4), slice(4, 6), slice(6, 8)


class HeadBuffers:

    def __init__(self, sb, tag):
        self.w_raw = sb(f"{tag}_w_raw", [P, 8, P])
        self.wH = sb(f"{tag}_wH", [P, 6, P], F32R)
        self.wL = sb(f"{tag}_wL", [P, 6, P], F32R)
        self.woH = sb(f"{tag}_woH", [P, D], F32R)
        self.woL = sb(f"{tag}_woL", [P, D], F32R)
        self.kH = sb(f"{tag}_kH", [P, NK], F32R)
        self.kL = sb(f"{tag}_kL", [P, NK], F32R)
        self.vH = sb(f"{tag}_vH", [KB, KTILES, P], F32R)
        self.vL = sb(f"{tag}_vL", [KB, KTILES, P], F32R)
        self.qH = sb(f"{tag}_qH", [P, TOK], F32R)
        self.qL = sb(f"{tag}_qL", [P, TOK], F32R)
        self.o = sb(f"{tag}_o", [P, TOK])
        self.oH = sb(f"{tag}_oH", [P, TOK], F32R)
        self.oL = sb(f"{tag}_oL", [P, TOK], F32R)


class HeadSemaphores:
    def __init__(self, sem, tag):
        self.loaded = sem(f"{tag}_w_loaded")
        self.qkv_high = sem(f"{tag}_qkv_high")
        self.qkv_cut = sem(f"{tag}_qkv_cut")
        self.wo_high = sem(f"{tag}_wo_high")
        self.wo_cut = sem(f"{tag}_wo_cut")
        self.v_issued = sem(f"{tag}_v_issued")
        self.o_issued = sem(f"{tag}_o_issued")
        self.filled = sem(f"{tag}_g_filled")
        self.high = sem(f"{tag}_g_high")
        self.done = sem(f"{tag}_g_done")
        self.bias_loaded = sem(f"{tag}_bias_loaded")
        self.bias_added = sem(f"{tag}_bias_added")
        self.o_high = sem(f"{tag}_o_high")
        self.o_cut = sem(f"{tag}_o_cut")
        self.o_written = sem(f"{tag}_o_written")


def head_loads(sp, w, q, dram_w):
    sp.dma_start(w.w_raw[:], dram_w[0]).then_inc(q.loaded, 16)
    with sp.Fori(1, HEADS) as h:
        sp.wait_ge(q.wo_cut, h)
        sp.dma_start(w.w_raw[:], dram_w[bass.ds(h, 1)].rearrange("o p t c -> p (o t) c")).then_inc(q.loaded, 16)


def cut_qkv(pool, s, w, q, h):
    need(pool, q.v_issued, h)
    pool.wait_ge(q.loaded, 16 * h + 16)
    pool.tensor_tensor(w.wH[:], w.w_raw[:, 0:6, :], s.ones[:].unsqueeze(1).to_broadcast([P, 6, P]), ALU.mult).then_inc(q.qkv_high, 1)
    pool.wait_ge(q.qkv_high, h + 1)
    pool.tensor_tensor(w.wL[:], w.w_raw[:, 0:6, :], w.wH[:].bitcast(F32), ALU.subtract).then_inc(q.qkv_cut, 1)


def cut_wo(pool, s, w, q, h):
    wo, high, low = w.w_raw[:, O_W, :], w.woH[:].rearrange("p (t c) -> p t c", c=P), w.woL[:].rearrange("p (t c) -> p t c", c=P)
    need(pool, q.o_issued, h)
    pool.tensor_tensor(high, wo, s.ones[:].unsqueeze(1).to_broadcast([P, 2, P]), ALU.mult).then_inc(q.wo_high, 1)
    pool.wait_ge(q.wo_high, h + 1)
    pool.tensor_tensor(low, wo, high.bitcast(F32), ALU.subtract).then_inc(q.wo_cut, 1)


def key_terms(s, w, c):
    cols = slice(c * CHUNK, (c + 1) * CHUNK)
    return [(w.wH[:, 2, :], s.ctxH[:, cols]), (w.wH[:, 2, :], s.ctxL[:, cols]), (w.wL[:, 2, :], s.ctxH[:, cols]),
            (w.wH[:, 3, :], s.ctxT[:, cols]), (w.wL[:, 3, :], s.ctxT[:, cols])]


def value_terms(s, w, t):
    cols = slice(t * KB, (t + 1) * KB)
    return [(s.ctxH[:, cols], w.wH[:, 4, :]), (s.ctxL[:, cols], w.wH[:, 4, :]), (s.ctxH[:, cols], w.wL[:, 4, :]),
            (s.ctxT[:, cols], w.wH[:, 5, :]), (s.ctxT[:, cols], w.wL[:, 5, :])]


def query_terms(s, w, half):
    return [pair for k in range(KT) for pair in (
        (w.wH[:, k, :], s.xnTH[:, k, half]), (w.wH[:, k, :], s.xnTL[:, k, half]),
        (w.wL[:, k, :], s.xnTH[:, k, half]))]


HALVES = [slice(0, TOK // 2), slice(TOK // 2, TOK)]
VGROUP = 4
VGROUPS = KTILES // VGROUP


def project_keys(pe, s, w, q, banks, h, use):
    pe.wait_ge(q.qkv_cut, h + 1)
    for c in range(CHUNKS):
        need(pe, q.done, use + c - 1)
        split_products(pe, banks[c % 2][:, 0:CHUNK], key_terms(s, w, c)).then_inc(q.filled, 1)


def project_queries(pe, s, w, q, banks, use):
    for n, half in enumerate(HALVES):
        need(pe, q.done, use + n - 1)
        split_products(pe, banks[n % 2][:, 0:TOK // 2], query_terms(s, w, half)).then_inc(q.filled, 1)


def project_values(pe, s, w, q, banks, use):
    for n in range(VGROUPS):
        need(pe, q.done, use + n - 1)
        for j in range(VGROUP):
            last = split_products(pe, banks[n % 2][0:KB, j * P:(j + 1) * P], value_terms(s, w, n * VGROUP + j))
        last.then_inc(q.filled, 1)
    pe.wait_ge(q.filled, use + VGROUPS)
    pe.sem_inc(q.v_issued, 1)


def project_outputs(pe, w, q, banks, h, use, parts):
    pe.wait_ge(q.o_cut, parts * (h + 1))
    pe.wait_ge(q.wo_cut, h + 1)
    for g in range(GROUPS):
        need(pe, q.done, use + g - 1)
        for i in range(2 * g, min(2 * g + 2, TILES)):
            tok = slice(i * P, (i + 1) * P)
            last = split_products(pe, banks[g % 2][:, (i % 2) * D:(i % 2 + 1) * D], [
                (w.oH[:, tok], w.woH[:]), (w.oH[:, tok], w.woL[:]), (w.oL[:, tok], w.woH[:])])
        last.then_inc(q.filled, 1)
    pe.wait_ge(q.filled, use + GROUPS)
    pe.sem_inc(q.o_issued, 1)


def high_keys(act, w, q, banks, use, highs):
    for c in range(CHUNKS):
        act.wait_ge(q.filled, use + c + 1)
        act.activation(w.kH[:, c * CHUNK:(c + 1) * CHUNK], banks[c % 2][:, 0:CHUNK], ACT.Copy).then_inc(q.high, 1)


def high_queries(act, w, q, banks, use, highs, scale):
    for n, half in enumerate(HALVES):
        act.wait_ge(q.filled, use + n + 1)
        act.activation(w.qH[:, half], banks[n % 2][:, 0:TOK // 2], ACT.Copy, scale=scale).then_inc(q.high, 1)


def high_values(act, w, q, banks, use, highs):
    for n in range(VGROUPS):
        act.wait_ge(q.filled, use + n + 1)
        act.activation(w.vH[:, n * VGROUP:(n + 1) * VGROUP, :],
                       banks[n % 2][0:KB, :].rearrange("p (t c) -> p t c", t=VGROUP), ACT.Copy).then_inc(q.high, 1)


def low_keys(dve, w, q, banks, highs):
    for c in range(CHUNKS):
        cols = slice(c * CHUNK, (c + 1) * CHUNK)
        dve.wait_ge(q.high, highs + c + 1)
        dve.tensor_tensor(w.kL[:, cols], banks[c % 2][:, 0:CHUNK], w.kH[:, cols].bitcast(F32),
                          ALU.subtract).then_inc(q.done, 1)


def low_queries(dve, w, q, banks, highs, scale):
    for n, half in enumerate(HALVES):
        dve.wait_ge(q.high, highs + n + 1)
        dve.scalar_tensor_tensor(w.qL[:, half], banks[n % 2][:, 0:TOK // 2], scale, w.qH[:, half].bitcast(F32),
                                 ALU.mult, ALU.subtract).then_inc(q.done, 1)


def low_values(dve, w, q, banks, highs):
    for n in range(VGROUPS):
        tiles = slice(n * VGROUP, (n + 1) * VGROUP)
        dve.wait_ge(q.high, highs + n + 1)
        dve.tensor_tensor(w.vL[:, tiles, :], banks[n % 2][0:KB, :].rearrange("p (t c) -> p t c", t=VGROUP),
                          w.vH[:, tiles, :].bitcast(F32), ALU.subtract).then_inc(q.done, 1)


def add_outputs(dve, s, q, banks, use):
    for g in range(GROUPS):
        tiles = slice(2 * g, min(2 * g + 2, TILES))
        wide = (tiles.stop - tiles.start) * D
        dve.wait_ge(q.filled, use + g + 1)
        dve.tensor_tensor(s.x[:, tiles, :], s.x[:, tiles, :],
                          banks[g % 2][:, 0:wide].rearrange("p (t d) -> p t d", d=D), ALU.add).then_inc(q.done, 1)


def layer1_attention(nc, s, dram):
    SCALE = 1.5 * P ** -0.5
    TCH = 4
    TCHUNKS = KTILES // TCH
    RING = 3
    AHEAD = 3
    with ExitStack() as ctx:
        def sb(name, shape, dt=F32):
            return ctx.enter_context(nc.sbuf_tensor(name, shape, dt))

        sem = ctx.enter_context(phase_semaphores(nc))

        w = HeadBuffers(sb, "a1")
        prob = sb("a1_prob", [P, 2, NK])
        xn = prob[:, 0, 0:TILES * D].rearrange("p (t d) -> p t d", d=D)
        pH = sb("a1_pH", [KB, RING, TCH, P], F32R)
        pL = sb("a1_pL", [KB, RING, TCH, P], F32R)
        bias = sb("a1_bias", [P, D])
        chunk_max = sb("a1_chunk_max", [P, 2, CHUNKS])
        nmax = sb("a1_nmax", [P, 2])
        rsum = sb("a1_rsum", [P, 2])
        rinv = sb("a1_rinv", [P, 2])
        spread = sb("a1_spread", [P, P])
        rinv_all = sb("a1_rinv_all", [P, P])
        ln = layer_norm_buffers(sb, "a1_ln")
        ql = layer_norm_semaphores(sem, "a1_ln")
        q = HeadSemaphores(sem, "a1")
        s_filled, s_out, max_ready, exp_done = (sem("a1_s_filled"), sem("a1_s_out"), sem("a1_max_ready"),
                                                sem("a1_exp_done"))
        rinv_ready, spread_ready = sem("a1_rinv_ready"), sem("a1_spread_ready")
        t_filled, t_high, t_done, pv_done = sem("a1_t_filled"), sem("a1_t_high"), sem("a1_t_done"), sem("a1_pv_done")
        sums_filled, rinv_out = sem("a1_sums_filled"), sem("a1_rinv_out")
        SB, OB, GB = s.banks[0:3], s.banks[5], s.banks[6:8]
        TB = [s.banks[3], s.banks[4], *GB]
        LNB = [*SB, OB]
        FIRST, EACH = CHUNKS + 2 + VGROUPS, CHUNKS + 2 + VGROUPS + GROUPS
        HIGHS = CHUNKS + 2 + VGROUPS

        def base(h):
            return 0 if isinstance(h, int) and h == 0 else EACH * h - (EACH - FIRST)

        block = ctx.enter_context(nc.Block())

        @block.sync
        def _(sp):
            sp.dma_start(bias[:], dram["a1_bias"]).then_inc(q.bias_loaded, 16)
            head_loads(sp, w, q, dram["a1_w"])

        @block.gpsimd
        def _(pool):
            def cut_outputs(h):
                for t in range(TILES):
                    tok = slice(t * P, (t + 1) * P)
                    n = TILES * h + t
                    pool.wait_ge(q.o_written, n + 1)
                    pool.tensor_tensor(w.oH[:, tok], w.o[:, tok], s.ones[:], ALU.mult).then_inc(q.o_high, 1)
                    pool.wait_ge(q.o_high, n + 1)
                    pool.tensor_tensor(w.oL[:, tok], w.o[:, tok], w.oH[:, tok].bitcast(F32),
                                       ALU.subtract).then_inc(q.o_cut, 1)

            cut_qkv(pool, s, w, q, 0)
            cut_wo(pool, s, w, q, 0)
            with pool.Fori(1, HEADS) as h:
                cut_qkv(pool, s, w, q, h)
                cut_outputs(h - 1)
                cut_wo(pool, s, w, q, h)
            cut_outputs(HEADS - 1)

        @block.tensor
        def _(pe):
            def scores(h, t):
                for c in range(CHUNKS):
                    n = CHUNKS * (TILES * h + t) + c
                    need(pe, s_out, n - 2)
                    cols, tok = slice(c * CHUNK, (c + 1) * CHUNK), slice(t * P, (t + 1) * P)
                    split_products(pe, SB[c % 3][:, 0:CHUNK], [
                        (w.qH[:, tok], w.kH[:, cols]), (w.qH[:, tok], w.kL[:, cols]),
                        (w.qL[:, tok], w.kH[:, cols])]).then_inc(s_filled, 1)

            def turn(h, t, c):
                n = TCHUNKS * (TILES * h + t) + c
                if c >= len(TB):
                    pe.wait_ge(t_done, n - len(TB) + 1)
                if c == 3:
                    need(pe, rinv_out, TILES * h + t)
                for j in range(TCH):
                    key = (c * TCH + j) * KB
                    last = pe.transpose(TB[c % 4][0:KB, j * P:(j + 1) * P], prob[:, t % 2, key:key + KB], s.ident[:])
                last.then_inc(t_filled, 1)

            def mix(h, t, c):
                n = TCHUNKS * (TILES * h + t) + c
                pe.wait_ge(t_done, n + 1)
                terms = []
                for j in range(TCH):
                    k = c * TCH + j
                    terms += [(w.vH[:, k, :], pH[:, c % RING, j, :]), (w.vL[:, k, :], pH[:, c % RING, j, :]),
                              (w.vH[:, k, :], pL[:, c % RING, j, :])]
                split_products(pe, OB[:, 0:P], terms, c == 0, c == TCHUNKS - 1).then_inc(pv_done, 1)

            def turn_and_mix(h, t):
                tile = TILES * h + t
                pe.wait_ge(exp_done, tile + 1)
                need(pe, q.o_written, tile)
                for c in range(AHEAD):
                    turn(h, t, c)
                for c in range(TCHUNKS):
                    if c + AHEAD < TCHUNKS:
                        turn(h, t, c + AHEAD)
                    if c == TCHUNKS - 2:
                        pe.wait_ge(spread_ready, tile + 1)
                        pe.matmul(TB[3][:, 0:P], s.ones[:], spread[:], start=True, stop=True).then_inc(sums_filled, 1)
                    mix(h, t, c)

            def head(h, first):
                use = base(h)
                if not first:
                    pe.wait_ge(rinv_out, TILES * h - 1)
                project_keys(pe, s, w, q, GB, h, use)
                if not first:
                    pe.wait_ge(q.done, use + CHUNKS)
                    turn_and_mix(h - 1, TILES - 1)
                    pe.wait_ge(rinv_out, TILES * h)
                project_queries(pe, s, w, q, GB, use + CHUNKS)
                pe.wait_ge(q.done, use + CHUNKS + 2)
                scores(h, 0)
                values = use + CHUNKS + 2
                if not first:
                    project_outputs(pe, w, q, GB, h - 1, values, TILES)
                    values = values + GROUPS
                project_values(pe, s, w, q, GB, values)
                scores(h, 1)
                pe.wait_ge(q.done, values + VGROUPS)
                for t in range(TILES - 1):
                    turn_and_mix(h, t)
                    if t + 2 < TILES:
                        scores(h, t + 2)

            turn_tensor(pe, ql, xn, LNB, s.ident[:])
            pe.wait_ge(ql.done, GROUPS)
            head(0, True)
            with pe.Fori(1, HEADS) as h:
                head(h, False)
            turn_and_mix(HEADS - 1, TILES - 1)
            pe.wait_ge(rinv_out, TILES * HEADS)
            project_outputs(pe, w, q, GB, HEADS - 1, base(HEADS), TILES)

        @block.scalar
        def _(act):
            def exps(h, t):
                act.wait_ge(max_ready, TILES * h + t + 1)
                act.activation(prob[:, t % 2, :], prob[:, t % 2, :], ACT.Exp, bias=nmax[:, t % 2:t % 2 + 1],
                               accum_out=rsum[:, t % 2:t % 2 + 1]).then_inc(exp_done, 1)

            def highs(h, t):
                for c in range(TCHUNKS):
                    n = TCHUNKS * (TILES * h + t) + c
                    act.wait_ge(t_filled, n + 1)
                    need(act, pv_done, n + 1 - RING)
                    act.activation(pH[:, c % RING, :, :], TB[c % 4][0:KB, :].rearrange("p (j c) -> p j c", j=TCH),
                                   ACT.Copy).then_inc(t_high, 1)
                act.wait_ge(sums_filled, TILES * h + t + 1)
                need(act, q.o_written, TILES * h + t)
                act.activation(rinv_all[:], TB[3][:, 0:P], ACT.Copy).then_inc(rinv_out, 1)

            def head(h, first):
                use, high = base(h), HIGHS * h
                high_keys(act, w, q, GB, use, high)
                if not first:
                    highs(h - 1, TILES - 1)
                high_queries(act, w, q, GB, use + CHUNKS, high + CHUNKS, 1.0)
                exps(h, 0)
                high_values(act, w, q, GB, use + CHUNKS + 2 + (0 if first else GROUPS), high + CHUNKS + 2)
                for t in range(TILES - 1):
                    highs(h, t)
                    exps(h, t + 1)

            layer_norm_scalar(act, ln, ql)
            turn_scalar(act, ql, LNB, s.xnTH)
            head(0, True)
            with act.Fori(1, HEADS) as h:
                head(h, False)
            highs(HEADS - 1, TILES - 1)

        @block.vector
        def _(dve):
            def scores_out(h, t, between=None):
                for c in range(CHUNKS):
                    dve.wait_ge(s_filled, CHUNKS * (TILES * h + t) + c + 1)
                    dve.tensor_scalar(prob[:, t % 2, c * CHUNK:(c + 1) * CHUNK], SB[c % 3][:, 0:CHUNK], SCALE, None,
                                      ALU.mult, ALU.max, accum_out=chunk_max[:, t % 2, c:c + 1]).then_inc(s_out, 1)
                    if c == 1 and between is not None:
                        outputs(h, between)
                dve.wait_ge(s_out, CHUNKS * (TILES * h + t + 1))
                dve.tensor_reduce(nmax[:, t % 2:t % 2 + 1], chunk_max[:, t % 2, :], AX.X, ALU.max,
                                  negate=True).then_inc(max_ready, 1)

            def one_over_sums(h, t):
                tile = TILES * h + t
                dve.wait_ge(exp_done, tile + 1)
                dve.reciprocal(rinv[:, t % 2:t % 2 + 1], rsum[:, t % 2:t % 2 + 1]).then_inc(rinv_ready, 1)
                dve.wait_ge(rinv_ready, tile + 1)
                dve.tensor_scalar(spread[:], s.ident[:], rinv[:, t % 2:t % 2 + 1], None, ALU.mult).then_inc(spread_ready, 1)

            def lows(h, t):
                tile = TILES * h + t
                for c in range(TCHUNKS):
                    dve.wait_ge(t_high, TCHUNKS * tile + c + 1)
                    dve.tensor_tensor(pL[:, c % RING, :, :], TB[c % 4][0:KB, :].rearrange("p (j c) -> p j c", j=TCH),
                                      pH[:, c % RING, :, :].bitcast(F32), ALU.subtract).then_inc(t_done, 1)

            def outputs(h, t):
                tile = TILES * h + t
                dve.wait_ge(pv_done, TCHUNKS * (tile + 1))
                dve.wait_ge(rinv_out, tile + 1)
                dve.tensor_tensor(w.o[:, t * P:(t + 1) * P], OB[:, 0:P], rinv_all[:], ALU.mult).then_inc(q.o_written, 1)

            def head(h, first):
                use, high = base(h), HIGHS * h
                low_keys(dve, w, q, GB, high)
                if not first:
                    one_over_sums(h - 1, TILES - 1)
                    lows(h - 1, TILES - 1)
                    outputs(h - 1, TILES - 1)
                low_queries(dve, w, q, GB, high + CHUNKS, 1.0)
                scores_out(h, 0)
                if not first:
                    add_outputs(dve, s, q, GB, use + CHUNKS + 2)
                low_values(dve, w, q, GB, high + CHUNKS + 2)
                scores_out(h, 1)
                for t in range(TILES - 1):
                    one_over_sums(h, t)
                    lows(h, t)
                    if t + 2 < TILES:
                        scores_out(h, t + 2, between=t)
                    else:
                        outputs(h, t)

            layer_norm_vector(dve, ln, ql, s.x, xn)
            turn_vector(dve, ql, LNB, s.xnTH, s.xnTL)
            dve.wait_ge(q.bias_loaded, 16)
            dve.tensor_tensor(s.x[:], s.x[:], bias[:].unsqueeze(1).to_broadcast([P, TILES, D]), ALU.add)\
               .then_inc(q.bias_added, 1)
            dve.wait_ge(q.bias_added, 1)
            head(0, True)
            with dve.Fori(1, HEADS) as h:
                head(h, False)
            one_over_sums(HEADS - 1, TILES - 1)
            lows(HEADS - 1, TILES - 1)
            outputs(HEADS - 1, TILES - 1)
            add_outputs(dve, s, q, GB, base(HEADS))
def layer1_ffn(nc, s, dram):
    INNER = 1024
    IT = INNER // P
    with ExitStack() as ctx:
        def sb(name, shape, dt=F32):
            return ctx.enter_context(nc.sbuf_tensor(name, shape, dt))

        sem = ctx.enter_context(phase_semaphores(nc))

        xn = sb("f1_xn", [P, TILES, D])
        big = sb("f1_big", [P, TILES, D])
        xq = sb("f1_xq", [P, TILES, D], BF16)
        xqT = sb("f1_xqT", [P, KT, TOK], BF16)
        ident = sb("f1_ident", [P, P], BF16)
        xa = sb("f1_xa", [P, 6, TILES])
        gate = sb("f1_gate", [P, 2, INNER])
        hid = sb("f1_hid", [P, 2, INNER])
        hbig = sb("f1_hbig", [P, 2, INNER])
        hq = sb("f1_hq", [P, 2, INNER], BF16)
        hqT = sb("f1_hqT", [P, 2, IT, P], BF16)
        ha = sb("f1_ha", [P, 4, TILES])
        ln = layer_norm_buffers(sb, "f1_ln")
        ql = layer_norm_semaphores(sem, "f1_ln")
        const_ready, x_step, x_scaled, x_rounded = (sem("f1_const_ready"), sem("f1_x_step"), sem("f1_x_scaled"),
                                                    sem("f1_x_rounded"))
        scales_ready = sem("f1_scales_ready")
        xt_filled, xt_done = sem("f1_xt_filled"), sem("f1_xt_done")
        g_filled, g_done, u_filled, h_done = sem("f1_g_filled"), sem("f1_g_done"), sem("f1_u_filled"), sem("f1_h_done")
        h_step, h_scaled, h_big, h_rounded = sem("f1_h_step"), sem("f1_h_scaled"), sem("f1_h_big"), sem("f1_h_rounded")
        ht_filled, ht_done, y_filled, y_added = (sem("f1_ht_filled"), sem("f1_ht_done"), sem("f1_y_filled"),
                                                 sem("f1_y_added"))
        B = s.banks
        w_gate = s.w_quant[:, 0, :].rearrange("p (k n) -> p k n", k=KT)
        w_up = s.w_quant[:, 1, :].rearrange("p (k n) -> p k n", k=KT)
        w_down = s.w_quant[:, 2, :].rearrange("p (k n) -> p k n", k=IT)
        turned = [B[n][:, :].bitcast(BF16) for n in (4, 5)]
        top, room, scale, inv, inv_gate, inv_up = (xa[:, n, :] for n in range(6))
        block = ctx.enter_context(nc.Block())

        @block.vector
        def _(dve):
            dve.tensor_copy(ident[:], s.ident[:]).then_inc(const_ready, 1)
            layer_norm_vector(dve, ln, ql, s.x, xn)
            dve.wait_ge(ql.normed, TILES)
            dve.tensor_reduce(top, xn[:], AX.X, ALU.max, apply_absolute_value=True).then_inc(x_step, 1)
            dve.wait_ge(x_step, 1)
            dve.tensor_scalar(room, top, EPS, None, ALU.max).then_inc(x_step, 1)
            dve.wait_ge(x_step, 2)
            dve.reciprocal(top, room).then_inc(x_step, 1)
            dve.tensor_scalar(inv, room, 1.0 / 127.0, None, ALU.mult).then_inc(x_step, 1)
            dve.wait_ge(x_step, 4)
            dve.tensor_scalar(scale, top, 127.0, None, ALU.mult).then_inc(x_step, 1)
            dve.wait_ge(x_step, 5)
            for i in range(TILES):
                dve.tensor_scalar(big[:, i, :], xn[:, i, :], scale[:, i:i + 1], MAGIC, ALU.mult, ALU.add)\
                   .then_inc(x_scaled, 1)
                dve.wait_ge(x_scaled, i + 1)
                dve.tensor_scalar(xq[:, i, :], big[:, i, :], MAGIC, 127.0, ALU.subtract, ALU.min)\
                   .then_inc(x_rounded, 1)
            dve.tensor_scalar(inv_gate, inv, s.w_mean[:, 0:1], None, ALU.mult).then_inc(scales_ready, 1)
            dve.tensor_scalar(inv_up, inv, s.w_mean[:, 1:2], None, ALU.mult).then_inc(scales_ready, 1)
            dve.wait_ge(scales_ready, 2)

            def hidden(i):
                for n in range(2):
                    part = slice(n * 512, n * 512 + 512)
                    dve.wait_ge(g_done, 2 * i + n + 1)
                    dve.wait_ge(u_filled, 2 * i + n + 1)
                    dve.scalar_tensor_tensor(hid[:, i % 2, part], B[2 + n][:, :], inv_up[:, i:i + 1],
                                             gate[:, i % 2, part], ALU.mult, ALU.mult).then_inc(h_done, 1)
                dve.wait_ge(h_done, 2 * i + 2)
                dve.tensor_reduce(ha[:, 0, i:i + 1], hid[:, i % 2, :], AX.X, ALU.max,
                                  apply_absolute_value=True).then_inc(h_step, 1)
                dve.wait_ge(h_step, 4 * i + 1)
                dve.tensor_scalar(ha[:, 1, i:i + 1], ha[:, 0, i:i + 1], EPS, None, ALU.max).then_inc(h_step, 1)
                dve.wait_ge(h_step, 4 * i + 2)
                dve.reciprocal(ha[:, 0, i:i + 1], ha[:, 1, i:i + 1]).then_inc(h_step, 1)
                dve.wait_ge(h_step, 4 * i + 3)
                dve.tensor_scalar(ha[:, 2, i:i + 1], ha[:, 0, i:i + 1], 127.0, None, ALU.mult).then_inc(h_scaled, 1)
                dve.tensor_scalar(ha[:, 3, i:i + 1], ha[:, 1, i:i + 1], 1.0 / 127.0, s.w_mean[:, 2:3],
                                  ALU.mult, ALU.mult).then_inc(h_step, 1)

            def rounded(i):
                dve.wait_ge(h_big, i + 1)
                dve.tensor_scalar(hq[:, i % 2, :], hbig[:, i % 2, :], MAGIC, 127.0, ALU.subtract, ALU.min)\
                   .then_inc(h_rounded, 1)

            def into_x(i):
                dve.wait_ge(y_filled, i + 1)
                dve.scalar_tensor_tensor(s.x[:, i, :], B[6 + i % 2][:, 0:D], ha[:, 3, i:i + 1], s.x[:, i, :],
                                         ALU.mult, ALU.add).then_inc(y_added, 1)

            hidden(0)
            for i in range(TILES):
                if i + 1 < TILES:
                    hidden(i + 1)
                rounded(i)
                if i >= 1:
                    into_x(i - 1)
            into_x(TILES - 1)

        @block.scalar
        def _(act):
            layer_norm_scalar(act, ln, ql)
            for i in range(TILES):
                act.wait_ge(xt_filled, i + 1)
                act.activation(xqT[:, :, i * P:(i + 1) * P], turned[i % 2][:, 0:D].rearrange("p (k c) -> p k c", k=KT),
                               ACT.Copy).then_inc(xt_done, 1)
            act.wait_ge(scales_ready, 2)

            def gates(i):
                for n in range(2):
                    act.wait_ge(g_filled, 2 * i + n + 1)
                    act.activation(gate[:, i % 2, n * 512:n * 512 + 512], B[n][:, :], ACT.Silu,
                                   scale=inv_gate[:, i:i + 1]).then_inc(g_done, 1)

            def scaled(i):
                act.wait_ge(h_scaled, i + 1)
                act.activation(hbig[:, i % 2, :], hid[:, i % 2, :], ACT.Copy, scale=ha[:, 2, i:i + 1],
                               bias=MAGIC).then_inc(h_big, 1)

            def turned_out(i):
                act.wait_ge(ht_filled, i + 1)
                act.activation(hqT[:, i % 2, :, :], turned[i % 2].rearrange("p (k c) -> p k c", k=IT),
                               ACT.Copy).then_inc(ht_done, 1)

            gates(0)
            for i in range(TILES):
                if i + 1 < TILES:
                    gates(i + 1)
                scaled(i)
                if i >= 1:
                    turned_out(i - 1)
            turned_out(TILES - 1)

        @block.tensor
        def _(pe):
            pe.wait_ge(const_ready, 1)
            for i in range(TILES):
                pe.wait_ge(x_rounded, i + 1)
                need(pe, xt_done, i - 1)
                for k in range(KT):
                    last = pe.transpose(turned[i % 2][:, k * P:(k + 1) * P], xq[:, i, k * P:(k + 1) * P], ident[:])
                last.then_inc(xt_filled, 1)
            pe.wait_ge(xt_done, TILES)

            def up(i):
                tok = slice(i * P, (i + 1) * P)
                for bank, weights, filled, read in ((0, w_gate, g_filled, g_done), (2, w_up, u_filled, h_done)):
                    for n in range(2):
                        need(pe, read, 2 * (i - 1) + n + 1)
                        split_products(pe, B[bank + n][:, :], [
                            (xqT[:, k, tok], weights[:, k, n * 512:n * 512 + 512]) for k in range(KT)]).then_inc(filled, 1)

            def down(i):
                pe.wait_ge(h_rounded, i + 1)
                need(pe, ht_done, i - 1)
                for k in range(IT):
                    last = pe.transpose(turned[i % 2][:, k * P:(k + 1) * P], hq[:, i % 2, k * P:(k + 1) * P], ident[:])
                last.then_inc(ht_filled, 1)
                pe.wait_ge(ht_done, i + 1)
                need(pe, y_added, i - 1)
                split_products(pe, B[6 + i % 2][:, 0:D], [
                    (hqT[:, i % 2, k, :], w_down[:, k, :]) for k in range(IT)]).then_inc(y_filled, 1)

            up(0)
            for i in range(TILES):
                if i + 1 < TILES:
                    up(i + 1)
                if i >= 1:
                    down(i - 1)
            down(TILES - 1)
def attention_heads64(nc, s, dram, layer, experts=False):
    HD = 64
    SCALE = HD ** -0.5
    BKT = KEYS // KB
    PAIR = 2 * SEQ
    EVEN = KEYS + 1

    def first_key(b):
        return min(b * KEYS, NK - EVEN)

    def own_keys(b):
        skip = b * KEYS - first_key(b)
        return slice(skip, skip + KEYS)

    with ExitStack() as ctx:
        def sb(name, shape, dt=F32):
            return ctx.enter_context(nc.sbuf_tensor(f"a{layer}_{name}", shape, dt))

        sem = ctx.enter_context(phase_semaphores(nc, f"a{layer}_"))

        w = HeadBuffers(sb, "head")
        prob = sb("prob", [SEQ, 2, 2, KEYS])
        pH = sb("pH", [KB, 2, BKT, PAIR], F32R)
        pL = sb("pL", [KB, 2, BKT, PAIR], F32R)
        xn = sb("xn", [P, TILES, D])
        bias = sb("bias", [P, D])
        nmax = sb("nmax", [SEQ, 2, 2])
        rsum = sb("rsum", [SEQ, 2, 2])
        rinv = sb("rinv", [SEQ, 2, 2])
        ln = layer_norm_buffers(sb, "ln")
        ql = layer_norm_semaphores(sem, "ln")
        q = HeadSemaphores(sem, "head")
        s_filled, max_ready, exp_done = sem("s_filled"), sem("max_ready"), sem("exp_done")
        rinv_ready, p_normed = sem("rinv_ready"), sem("p_normed")
        t_filled, t_high, t_done, pv_done = sem("t_filled"), sem("t_high"), sem("t_done"), sem("pv_done")
        expert_loaded = sem("expert_loaded")
        if experts:
            expert = sb("expert", [P, 2 * EXPERTS, D])
        B = s.banks
        SB = [B[0:2], B[2:4]]
        TB = [B[4:6], B[6:8]]
        GB = TB[1]
        OUT = slice(PAIR, 2 * PAIR)
        HIGHS = CHUNKS + 2 + VGROUPS
        EACH = HIGHS + GROUPS + (1 if experts else 0)

        def base(h):
            return 0 if isinstance(h, int) and h == 0 else EACH * h - GROUPS

        block = ctx.enter_context(nc.Block())

        @block.sync
        def _(sp):
            sp.dma_start(bias[:], dram[f"a{layer}_bias"]).then_inc(q.bias_loaded, 16)
            head_loads(sp, w, q, dram[f"a{layer}_w"])

        @block.gpsimd
        def _(pool):
            def norm(h, b):
                pool.wait_ge(rinv_ready, BATCH * h + b + 1)
                pool.tensor_tensor(prob[:, b % 2, :, :], prob[:, b % 2, :, :],
                                   rinv[:, b % 2, :].unsqueeze(2).to_broadcast([SEQ, 2, KEYS]), ALU.mult).then_inc(p_normed, 1)

            def cut_outputs(h, b):
                tok = slice(b * SEQ, (b + 1) * SEQ)
                n = BATCH * h + b
                pool.wait_ge(q.o_written, n + 1)
                pool.tensor_tensor(w.oH[:, tok], w.o[:, tok], s.ones[:, 0:SEQ], ALU.mult).then_inc(q.o_high, 1)
                pool.wait_ge(q.o_high, n + 1)
                pool.tensor_tensor(w.oL[:, tok], w.o[:, tok], w.oH[:, tok].bitcast(F32), ALU.subtract).then_inc(q.o_cut, 1)

            def first_half(h):
                norm(h, 0)
                norm(h, 1)
                cut_wo(pool, s, w, q, h)
                for b in range(2, BATCH // 2):
                    norm(h, b)
                    cut_outputs(h, b - 2)

            def second_half(h):
                for b in range(BATCH // 2, BATCH):
                    norm(h, b)
                    cut_outputs(h, b - 2)
                cut_outputs(h, BATCH - 2)
                cut_outputs(h, BATCH - 1)

            cut_qkv(pool, s, w, q, 0)
            first_half(0)
            with pool.Fori(1, HEADS) as h:
                cut_qkv(pool, s, w, q, h)
                second_half(h - 1)
                first_half(h)
            second_half(HEADS - 1)

        @block.tensor
        def _(pe):
            def scores(h, b):
                n = BATCH * h + b
                need(pe, exp_done, n - 1)
                tok, keys = slice(b * SEQ, (b + 1) * SEQ), slice(first_key(b), first_key(b) + EVEN)
                for i in range(2):
                    rows = slice(i * HD, (i + 1) * HD)
                    last = split_products(pe, SB[b % 2][i][0:SEQ, 0:EVEN], [
                        (w.qH[rows, tok], w.kH[rows, keys]), (w.qH[rows, tok], w.kL[rows, keys]),
                        (w.qL[rows, tok], w.kH[rows, keys])])
                last.then_inc(s_filled, 1)

            def turn(h, b):
                n = BATCH * h + b
                pe.wait_ge(p_normed, n + 1)
                need(pe, q.o_written, n - 1)
                for k in range(BKT):
                    for i in range(2):
                        at = (k % 2) * PAIR + i * SEQ
                        last = pe.transpose(TB[b % 2][k // 2][0:KB, at:at + SEQ],
                                            prob[:, b % 2, i, k * KB:(k + 1) * KB], s.ident[0:SEQ, 0:SEQ])
                last.then_inc(t_filled, 1)

            def mix(h, b):
                pe.wait_ge(t_done, BATCH * h + b + 1)
                terms = []
                for k in range(BKT):
                    t = BKT * b + k
                    terms += [(w.vH[:, t, :], pH[:, b % 2, k, :]), (w.vL[:, t, :], pH[:, b % 2, k, :]),
                              (w.vH[:, t, :], pL[:, b % 2, k, :])]
                split_products(pe, TB[b % 2][1][:, OUT], terms).then_inc(pv_done, 1)

            def combine(h, use):
                pe.wait_ge(expert_loaded, 16 * h + 16)
                need(pe, q.done, use - 1)
                for j in range(KT):
                    last = split_products(pe, GB[0][:, j * D:(j + 1) * D], [
                        (expert[:, k, j * P:(j + 1) * P], expert[:, EXPERTS + k, :]) for k in range(EXPERTS)])
                last.then_inc(q.filled, 1)

            def pair(h, first):
                use = base(h)
                if not first:
                    pe.wait_ge(q.o_written, BATCH * h - 2)
                project_keys(pe, s, w, q, GB, h, use)
                project_queries(pe, s, w, q, SB[0], use + CHUNKS)
                if not first:
                    mix(h - 1, BATCH - 2)
                    pe.wait_ge(q.done, use + CHUNKS)
                    turn(h - 1, BATCH - 1)
                pe.wait_ge(q.done, use + CHUNKS + 2)
                scores(h, 0)
                if not first:
                    mix(h - 1, BATCH - 1)
                scores(h, 1)
                if not first:
                    pe.wait_ge(q.o_written, BATCH * h)
                project_values(pe, s, w, q, GB, use + CHUNKS + 2)
                use = use + HIGHS
                if not first:
                    project_outputs(pe, w, q, GB, h - 1, use, BATCH)
                    use = use + GROUPS
                if experts:
                    combine(h, use)
                    use = use + 1
                turn(h, 0)
                for b in range(BATCH - 2):
                    scores(h, b + 2)
                    if b == 0:
                        pe.wait_ge(q.done, use)
                    turn(h, b + 1)
                    mix(h, b)

            turn_tensor(pe, ql, xn, B[0:4], s.ident[:])
            pe.wait_ge(ql.done, GROUPS)
            pair(0, True)
            with pe.Fori(1, HEADS) as h:
                pair(h, False)
            mix(HEADS - 1, BATCH - 2)
            turn(HEADS - 1, BATCH - 1)
            mix(HEADS - 1, BATCH - 1)
            pe.wait_ge(q.o_written, BATCH * HEADS)
            project_outputs(pe, w, q, GB, HEADS - 1, base(HEADS), BATCH)

        @block.scalar
        def _(act):
            def exps(h, b):
                act.wait_ge(max_ready, BATCH * h + b + 1)
                for i in range(2):
                    last = act.activation(prob[:, b % 2, i, :], SB[b % 2][i][0:SEQ, own_keys(b)], ACT.Exp,
                                          bias=nmax[:, b % 2, i:i + 1], accum_out=rsum[:, b % 2, i:i + 1])
                last.then_inc(exp_done, 1)

            def highs(h, b):
                act.wait_ge(t_filled, BATCH * h + b + 1)
                act.activation(pH[:, b % 2, 0:2, :], TB[b % 2][0][0:KB, 0:2 * PAIR].rearrange("p (k c) -> p k c", k=2),
                               ACT.Copy).then_inc(t_high, 1)
                act.activation(pH[:, b % 2, 2, :], TB[b % 2][1][0:KB, 0:PAIR], ACT.Copy).then_inc(t_high, 1)

            def pair(h, first):
                use, high = base(h), HIGHS * h
                high_keys(act, w, q, GB, use, high)
                high_queries(act, w, q, SB[0], use + CHUNKS, high + CHUNKS, SCALE)
                if not first:
                    highs(h - 1, BATCH - 1)
                exps(h, 0)
                exps(h, 1)
                high_values(act, w, q, GB, use + CHUNKS + 2, high + CHUNKS + 2)
                highs(h, 0)
                for b in range(BATCH - 2):
                    exps(h, b + 2)
                    highs(h, b + 1)

            if experts:
                act.dma_start(expert[:], dram["f2_w"][0]).then_inc(expert_loaded, 16)
            layer_norm_scalar(act, ln, ql)
            turn_scalar(act, ql, B[0:4], s.xnTH)
            pair(0, True)
            with act.Fori(1, HEADS) as h:
                if experts:
                    act.wait_ge(q.filled, base(h))
                    act.dma_start(expert[:], dram["f2_w"][bass.ds(h, 1)].rearrange("o p t c -> p (o t) c"))\
                       .then_inc(expert_loaded, 16)
                pair(h, False)
            highs(HEADS - 1, BATCH - 1)

        @block.vector
        def _(dve):
            def maxima(h, b):
                dve.wait_ge(s_filled, BATCH * h + b + 1)
                for i in range(2):
                    last = dve.tensor_reduce(nmax[:, b % 2, i:i + 1], SB[b % 2][i][0:SEQ, own_keys(b)], AX.X, ALU.max, negate=True)
                last.then_inc(max_ready, 1)

            def one_over_sums(h, b):
                dve.wait_ge(exp_done, BATCH * h + b + 1)
                dve.reciprocal(rinv[:, b % 2, :], rsum[:, b % 2, :]).then_inc(rinv_ready, 1)

            def lows(h, b):
                n = 2 * (BATCH * h + b)
                dve.wait_ge(t_high, n + 1)
                dve.tensor_tensor(pL[:, b % 2, 0:2, :], TB[b % 2][0][0:KB, 0:2 * PAIR].rearrange("p (k c) -> p k c", k=2),
                                  pH[:, b % 2, 0:2, :].bitcast(F32), ALU.subtract)
                dve.wait_ge(t_high, n + 2)
                dve.tensor_tensor(pL[:, b % 2, 2, :], TB[b % 2][1][0:KB, 0:PAIR], pH[:, b % 2, 2, :].bitcast(F32),
                                  ALU.subtract).then_inc(t_done, 1)

            def outputs(h, b):
                tok = slice(b * SEQ, (b + 1) * SEQ)
                dve.wait_ge(pv_done, BATCH * h + b + 1)
                for i in range(2):
                    rows = slice(i * HD, (i + 1) * HD)
                    last = dve.tensor_copy(w.o[rows, tok], TB[b % 2][1][rows, PAIR + i * SEQ:PAIR + (i + 1) * SEQ])
                last.then_inc(q.o_written, 1)

            def pair(h, first):
                use, high = base(h), HIGHS * h
                low_keys(dve, w, q, GB, high)
                low_queries(dve, w, q, SB[0], high + CHUNKS, SCALE)
                if not first:
                    outputs(h - 1, BATCH - 2)
                    lows(h - 1, BATCH - 1)
                maxima(h, 0)
                if not first:
                    outputs(h - 1, BATCH - 1)
                maxima(h, 1)
                one_over_sums(h, 0)
                low_values(dve, w, q, GB, high + CHUNKS + 2)
                one_over_sums(h, 1)
                use = use + HIGHS
                if not first:
                    add_outputs(dve, s, q, GB, use)
                    use = use + GROUPS
                if experts:
                    dve.wait_ge(q.filled, use + 1)
                    dve.tensor_copy(s.combined[:, h:h + 1, :] if first else s.combined[:, bass.ds(h, 1), :],
                                    GB[0][:, :].unsqueeze(1)).then_inc(q.done, 1)
                lows(h, 0)
                for b in range(BATCH - 2):
                    maxima(h, b + 2)
                    lows(h, b + 1)
                    one_over_sums(h, b + 2)
                    outputs(h, b)

            layer_norm_vector(dve, ln, ql, s.x, xn)
            turn_vector(dve, ql, B[0:4], s.xnTH, s.xnTL)
            dve.wait_ge(q.bias_loaded, 16)
            dve.tensor_tensor(s.x[:], s.x[:], bias[:].unsqueeze(1).to_broadcast([P, TILES, D]), ALU.add)\
               .then_inc(q.bias_added, 1)
            dve.wait_ge(q.bias_added, 1)
            pair(0, True)
            with dve.Fori(1, HEADS) as h:
                pair(h, False)
            outputs(HEADS - 1, BATCH - 2)
            lows(HEADS - 1, BATCH - 1)
            outputs(HEADS - 1, BATCH - 1)
            add_outputs(dve, s, q, GB, base(HEADS))


def layer2_ffn(nc, s, dram):
    PAIRS = EXPERTS // 2
    with ExitStack() as ctx:
        def sb(name, shape, dt=F32):
            return ctx.enter_context(nc.sbuf_tensor(f"f2_{name}", shape, dt))

        sem = ctx.enter_context(phase_semaphores(nc, "f2_"))
        xn = sb("xn", [P, TILES, D])
        cH = sb("cH", [P, KT, PAIRS, 2 * D], F32R)
        cL = sb("cL", [P, KT, PAIRS, 2 * D], F32R)
        gates = sb("gates", [P, PAIRS, 2, TILES])
        ln = layer_norm_buffers(sb, "ln")
        r = router_buffers(sb, "r")
        ql = layer_norm_semaphores(sem, "ln")
        q = router_semaphores(sem, "r")
        c_high, c_cut = sem("c_high"), sem("c_cut")
        y_filled, first_added, x_added = sem("y_filled"), sem("first_added"), sem("x_added")
        B = s.banks
        block = ctx.enter_context(nc.Block())

        @block.sync
        def _(sp):
            sp.dma_start(r.raw[:], dram["f2_gate"]).then_inc(q.loaded, 16)

        @block.gpsimd
        def _(pool):
            router_cut(pool, r, q)
            for e in range(EXPERTS):
                whole = s.combined[:, e, :].rearrange("p (k d) -> p k d", k=KT)
                mine = slice((e % 2) * D, (e % 2) * D + D)
                pool.tensor_copy(cH[:, :, e // 2, mine], whole).then_inc(c_high, 1)
                pool.wait_ge(c_high, e + 1)
                pool.tensor_tensor(cL[:, :, e // 2, mine], whole, cH[:, :, e // 2, mine].bitcast(F32),
                                   ALU.subtract).then_inc(c_cut, 1)

        @block.vector
        def _(dve):
            def add_pair(p):
                for i in range(TILES):
                    n = TILES * p + i
                    dve.wait_ge(y_filled, n + 1)
                    for j in range(2):
                        gate = gates[:, p:p + 1, j, i:i + 1] if isinstance(p, int) else gates[:, bass.ds(p, 1), j, i:i + 1]
                        if j == 1:
                            dve.wait_ge(first_added, n + 1)
                        dve.scalar_tensor_tensor(s.x[:, i, :], B[i][:, j * D:(j + 1) * D], gate.rearrange("p a b -> p (a b)"),
                                                 s.x[:, i, :], ALU.mult, ALU.add).then_inc(x_added if j else first_added, 1)

            layer_norm_vector(dve, ln, ql, s.x, xn)
            turn_vector(dve, ql, B[3:7], s.xnTH, s.xnTL)
            at = router_exps(dve, r, q, B[7])
            at = router_ranks(dve, s, r, q, r.logits[:], at)
            dve.wait_ge(q.exps, 1)
            router_keep_two(dve, r, q, at, r.exps[:], gates[:].rearrange("p a b t -> p t (a b)"), 0.0)
            dve.wait_ge(q.kept, 1)
            add_pair(0)
            with dve.Fori(1, PAIRS) as p:
                add_pair(p)

        @block.scalar
        def _(act):
            layer_norm_scalar(act, ln, ql)
            turn_scalar(act, ql, B[3:7], s.xnTH)
            router_scalar(act, r, q)

        @block.tensor
        def _(pe):
            def two_experts(p):
                pe.wait_ge(c_cut, 2 * p + 2)
                here = slice(p, p + 1) if isinstance(p, int) else bass.ds(p, 1)
                for i in range(TILES):
                    tok = slice(i * P, (i + 1) * P)
                    need(pe, x_added, TILES * (p - 1) + i + 1)
                    split_products(pe, B[i][:, :], [
                        pair for k in range(KT) for pair in (
                            (s.xnTH[:, k, tok], cH[:, k, here, :].rearrange("p a d -> p (a d)")),
                            (s.xnTH[:, k, tok], cL[:, k, here, :].rearrange("p a d -> p (a d)")),
                            (s.xnTL[:, k, tok], cH[:, k, here, :].rearrange("p a d -> p (a d)")))]).then_inc(y_filled, 1)

            turn_tensor(pe, ql, xn, B[3:7], s.ident[:])
            pe.wait_ge(ql.done, GROUPS)
            router_tensor(pe, s, r, q, B[7])
            two_experts(0)
            with pe.Fori(1, PAIRS) as p:
                two_experts(p)


def layer3_ffn(nc, s, dram, out):
    ALL = EXPERTS + 1
    WIDE = KT * D
    HALF = TOK // 2
    with ExitStack() as ctx:
        def sb(name, shape, dt=F32):
            return ctx.enter_context(nc.sbuf_tensor(f"f3_{name}", shape, dt))

        sem = ctx.enter_context(phase_semaphores(nc, "f3_"))
        xn = sb("xn", [P, TILES, D])
        raw = [sb(f"raw{n}", [P, 2 * WIDE + KT]) for n in range(2)]
        uH = [sb(f"u{n}H", [P, KT, D], F32R) for n in range(2)]
        uL = [sb(f"u{n}L", [P, KT, D], F32R) for n in range(2)]
        dH = [sb(f"d{n}H", [P, KT, D], F32R) for n in range(2)]
        dL = [sb(f"d{n}L", [P, KT, D], F32R) for n in range(2)]
        hid = sb("hid", [P, 2, HALF])
        hH = [sb(f"h{n}H", [P, KT, TOK], F32R) for n in range(2)]
        hL = [sb(f"h{n}L", [P, KT, TOK], F32R) for n in range(2)]
        comb = sb("comb", [P, ALL, TILES])
        combT = sb("combT", [ALL, TOK])
        down_b = sb("down_b", [ALL, D])
        ln = layer_norm_buffers(sb, "ln")
        r = router_buffers(sb, "r")
        ql = layer_norm_semaphores(sem, "ln")
        q = router_semaphores(sem, "r")
        w_loaded = [sem(f"w_loaded{n}") for n in range(2)]
        down_b_loaded, shared_set = sem("down_b_loaded"), sem("shared_set")
        w_high, w_cut = sem("w_high"), sem("w_cut")
        up_filled, silu_done, h_high, h_cut = sem("up_filled"), sem("silu_done"), sem("h_high"), sem("h_cut")
        y_filled, x_added = sem("y_filled"), sem("x_added")
        c_turned, c_out, b_filled, b_added = sem("c_turned"), sem("c_out"), sem("b_filled"), sem("b_added")
        B = s.banks
        UB, YB = B[0:4], B[4:8]
        UPS = KT * 2
        block = ctx.enter_context(nc.Block())

        def one(e):
            return slice(e, e + 1) if isinstance(e, int) else bass.ds(e, 1)

        @block.sync
        def _(sp):
            sp.dma_start(r.raw[:], dram["f3_gate"]).then_inc(q.loaded, 16)
            for e in range(2):
                sp.dma_start(raw[e][:], dram["f3_w"][e]).then_inc(w_loaded[e], 16)
            sp.dma_start(down_b[:], dram["f3_down_b"]).then_inc(down_b_loaded, 16)

            def load(e, n):
                sp.wait_ge(w_cut, 2 * e - 2)
                sp.wait_ge(silu_done, UPS * e - UPS)
                source = dram["f3_w"][e] if isinstance(e, int) else dram["f3_w"][bass.ds(e, 1)].rearrange("a p c -> p (a c)")
                sp.dma_start(raw[n][:], source).then_inc(w_loaded[n], 16)

            load(2, 0)
            with sp.Fori(2, EXPERTS // 2 + 1) as pair:
                load(2 * pair - 1, 1)
                load(2 * pair, 0)
            for i in range(TILES):
                sp.wait_ge(x_added, TILES * (ALL - 1) + i + 1)
                sp.dma_start(out[i * P:(i + 1) * P, :], s.x[:, i, :]).then_inc(s.stored, 16)
            sp.wait_ge(s.stored, 16 * TILES)

        @block.gpsimd
        def _(pool):
            def cut(e, n):
                pool.wait_ge(w_loaded[n], 8 * (e - n) + 16)
                need(pool, y_filled, TILES * (e - 1))
                for at, (high, low) in enumerate(((uH[n], uL[n]), (dH[n], dL[n]))):
                    whole = raw[n][:, at * WIDE:(at + 1) * WIDE].rearrange("p (k d) -> p k d", k=KT)
                    step = 2 * e + at + 1
                    pool.tensor_tensor(high[:], whole, s.ones[:, 0:1].unsqueeze(2).to_broadcast([P, KT, D]),
                                       ALU.mult).then_inc(w_high, 1)
                    pool.wait_ge(w_high, step)
                    pool.tensor_tensor(low[:], whole, high[:].bitcast(F32), ALU.subtract).then_inc(w_cut, 1)

            router_cut(pool, r, q)
            pool.tensor_copy(comb[:, EXPERTS, :], s.ones[:, 0:TILES]).then_inc(shared_set, 1)
            cut(0, 0)
            cut(1, 1)
            cut(2, 0)
            with pool.Fori(2, EXPERTS // 2 + 1) as pair:
                cut(2 * pair - 1, 1)
                cut(2 * pair, 0)

        @block.tensor
        def _(pe):
            def up(e, n):
                pe.wait_ge(w_cut, 2 * e + 1)
                for u in range(UPS):
                    j, half = u // 2, HALVES[u % 2]
                    cols = slice(j * P, (j + 1) * P)
                    need(pe, silu_done, UPS * (e - 1) + u + 1)
                    split_products(pe, UB[u][:, 0:HALF], [
                        pair for k in range(KT) for pair in (
                            (uH[n][:, k, cols], s.xnTH[:, k, half]), (uH[n][:, k, cols], s.xnTL[:, k, half]),
                            (uL[n][:, k, cols], s.xnTH[:, k, half]))]).then_inc(up_filled, 1)

            def down(e, n, last=False):
                pe.wait_ge(h_cut, UPS * (e + 1))
                pe.wait_ge(w_cut, 2 * e + 2)
                for i in range(TILES):
                    tok = slice(i * P, (i + 1) * P)
                    before = i - 4 if i >= 4 else (i + 4 if i + 4 < TILES else i) - TILES
                    need(pe, x_added, TILES * e + before + 1)
                    if isinstance(e, int) and e == 0 and i in (2, 3):
                        pe.wait_ge(c_out, i - 1)
                    terms = [pair for k in range(KT) for pair in (
                        (hH[n][:, k, tok], dH[n][:, k, :]), (hH[n][:, k, tok], dL[n][:, k, :]),
                        (hL[n][:, k, tok], dH[n][:, k, :]))]
                    if last:
                        terms += [(combT[:, tok], down_b[:])]
                    split_products(pe, YB[i % 4][:, 0:D], terms).then_inc(y_filled, 1)

            turn_tensor(pe, ql, xn, B[0:4], s.ident[:])
            pe.wait_ge(ql.done, GROUPS)
            router_tensor(pe, s, r, q, B[7])
            up(0, 0)
            pe.wait_ge(q.kept, 1)
            pe.wait_ge(shared_set, 1)
            for i in range(TILES):
                last = pe.transpose(YB[2 + i // 4][0:ALL, (i % 4) * P:(i % 4 + 1) * P], comb[:, :, i], s.ident[:])
                if i in (3, TILES - 1):
                    last.then_inc(c_turned, 1)
            up(1, 1)
            down(0, 0)
            up(2, 0)
            down(1, 1)
            with pe.Fori(2, EXPERTS // 2 + 1) as pair:
                up(2 * pair - 1, 1)
                down(2 * pair - 2, 0)
                up(2 * pair, 0)
                down(2 * pair - 1, 1)
            pe.wait_ge(down_b_loaded, 16)
            down(EXPERTS, 0, True)

        @block.scalar
        def _(act):
            def hidden(e, n):
                act.wait_ge(w_loaded[n], 8 * (e - n) + 16)
                for u in range(UPS):
                    step = UPS * e + u
                    act.wait_ge(up_filled, step + 1)
                    need(act, h_cut, step - 1)
                    col = raw[n][:, 2 * WIDE + u // 2:2 * WIDE + u // 2 + 1]
                    act.activation(hid[:, u % 2, :], UB[u][:, 0:HALF], ACT.Silu, bias=col).then_inc(silu_done, 1)

            layer_norm_scalar(act, ln, ql)
            turn_scalar(act, ql, B[0:4], s.xnTH)
            router_scalar(act, r, q)
            hidden(0, 0)
            for n in range(2):
                cols = slice(4 * P * n, min(4 * P * (n + 1), TOK))
                act.wait_ge(c_turned, n + 1)
                act.activation(combT[:, cols], YB[2 + n][0:ALL, 0:cols.stop - cols.start], ACT.Copy).then_inc(c_out, 1)
            hidden(1, 1)
            hidden(2, 0)
            with act.Fori(2, EXPERTS // 2 + 1) as pair:
                hidden(2 * pair - 1, 1)
                hidden(2 * pair, 0)

        @block.vector
        def _(dve):
            def cut_hidden(e, n):
                for u in range(UPS):
                    step = UPS * e + u
                    at = (slice(None), u // 2, HALVES[u % 2])
                    dve.wait_ge(silu_done, step + 1)
                    dve.tensor_copy(hH[n][at], hid[:, u % 2, :]).then_inc(h_high, 1)
                    dve.wait_ge(h_high, step + 1)
                    dve.tensor_tensor(hL[n][at], hid[:, u % 2, :], hH[n][at].bitcast(F32), ALU.subtract).then_inc(h_cut, 1)

            def add(e):
                for i in range(TILES):
                    n = TILES * e + i
                    col = comb[:, one(e), i:i + 1].rearrange("p a b -> p (a b)")
                    dve.wait_ge(y_filled, n + 1)
                    need(dve, x_added, n - TILES + 1)
                    dve.scalar_tensor_tensor(s.x[:, i, :], YB[i % 4][:, 0:D], col, s.x[:, i, :],
                                             ALU.mult, ALU.add).then_inc(x_added, 1)

            layer_norm_vector(dve, ln, ql, s.x, xn)
            turn_vector(dve, ql, B[0:4], s.xnTH, s.xnTL)
            at = router_exps(dve, r, q, B[7])
            at = router_softmax(dve, r, q, at)
            at = router_ranks(dve, s, r, q, r.probs[:], at)
            router_keep_two(dve, r, q, at, r.probs[:], comb[:, 0:EXPERTS, :].rearrange("p e t -> p t e"), 1e-20)
            dve.wait_ge(q.kept, 1)
            dve.wait_ge(shared_set, 1)
            cut_hidden(0, 0)
            cut_hidden(1, 1)
            add(0)
            cut_hidden(2, 0)
            add(1)
            with dve.Fori(2, EXPERTS // 2 + 1) as pair:
                cut_hidden(2 * pair - 1, 1)
                add(2 * pair - 2)
                cut_hidden(2 * pair, 0)
                add(2 * pair - 1)
            add(EXPERTS)


def build(nc, dram, out):
    with ExitStack() as ctx:
        s = Names()
        s.x = ctx.enter_context(nc.sbuf_tensor("x_stream", [P, TILES, D], F32))
        s.ident = ctx.enter_context(nc.sbuf_tensor("ident", [P, P], F32))
        s.ones = ctx.enter_context(nc.sbuf_tensor("ones", [P, P], F32))
        s.earlier = ctx.enter_context(nc.sbuf_tensor("earlier", [P, EXPERTS, EXPERTS], F32))
        s.ctxH = ctx.enter_context(nc.sbuf_tensor("ctxH", [P, NK], F32R))
        s.ctxL = ctx.enter_context(nc.sbuf_tensor("ctxL", [P, NK], F32R))
        s.ctxT = ctx.enter_context(nc.sbuf_tensor("ctxT", [P, NK], F32R))
        s.banks = [ctx.enter_context(nc.psum_tensor(f"bank{n}", [P, 512], F32)) for n in range(8)]
        s.stored = ctx.enter_context(nc.semaphore("stored"))
        layer0_attention(nc, s, dram)
        s.xnTH = ctx.enter_context(nc.sbuf_tensor("xnTH", [P, KT, TOK], F32R))
        s.xnTL = ctx.enter_context(nc.sbuf_tensor("xnTL", [P, KT, TOK], F32R))
        with ExitStack() as quantised:
            s.w_quant = quantised.enter_context(nc.sbuf_tensor("w_quant", [P, 3, 2048], BF16))
            s.w_mean = quantised.enter_context(nc.sbuf_tensor("w_mean", [P, 3], F32))
            layer0_ffn(nc, s, dram)
            layer1_attention(nc, s, dram)
            layer1_ffn(nc, s, dram)
        with ExitStack() as combined:
            s.combined = combined.enter_context(nc.sbuf_tensor("combined", [P, EXPERTS, KT * D], F32))
            attention_heads64(nc, s, dram, 2, experts=True)
            layer2_ffn(nc, s, dram)
        attention_heads64(nc, s, dram, 3)
        layer3_ffn(nc, s, dram, out)


def tiled(np, w):
    return w.reshape(-1, P, w.shape[1]).transpose(1, 0, 2)


def attention_weights(np, wq, wk, wv, wo):
    packs = []
    for h in range(HEADS):
        c = slice(h * P, (h + 1) * P)
        parts = [wq[0:P, c], wq[P:D, c]]
        for w in (wk, wv):
            parts += [w[0:P, c], np.concatenate([w[P:DC, c], w[P:DC, c]], axis=0)]
        parts += [wo[c, 0:P], wo[c, P:D]]
        packs.append(np.stack(parts, axis=1))
    return np.stack(packs, axis=0)


def repeated(np, row, rows=P):
    return np.broadcast_to(row, (rows,) + row.shape)


def laid_out(np, i):
    zeros = np.zeros(TAIL, np.float32)

    def column_pair(v):
        return [v[0:P], np.concatenate([v[P:], zeros]) if v.shape[0] == DC else v[P:]]

    a = {"x": i["x"].reshape(TOK, D)}
    rows = i["ctx_768"].reshape(NK, DC)
    a["ctx_rows"], a["ctx_cols"] = rows, rows.T
    a["ident"] = np.eye(P, dtype=np.float32)
    a["ones"] = np.ones((P, P), np.float32)
    a["earlier"] = repeated(np, np.tril(np.ones((EXPERTS, EXPERTS), np.float32), -1))
    a["a0_cols"] = np.stack([c for n in ("ln1_g", "ln1_b", "ln2_g", "ln2_b", "bq", "bk")
                             for c in column_pair(i["L0_xattn_" + n])], axis=1)
    a["a0_rows"] = repeated(np, np.stack([i["L0_xattn_bv"], i["L0_xattn_bo"]]))
    for n in "qkvo":
        a["a0_w" + n] = i["L0_xattn_W" + n]
    a["f0_gate"] = tiled(np, i["L0_ffn_gate_w"])
    a["f0_w"] = tiled(np, np.concatenate([i["L0_ffn_w0"].T, i["L0_ffn_w1"].T], axis=1))
    a["f0_bias"] = repeated(np, np.concatenate([i["L0_ffn_b0"], i["L0_ffn_b1"]]))
    a["f1_w"] = np.stack([tiled(np, i["L1_ffn_" + n].T).reshape(P, 2048) for n in ("w_gate", "w_up", "w_down")], axis=1)
    for l, o, b in ((1, "Wout", "bout"), (2, "Wo", "bo"), (3, "Wo", "bo")):
        p = f"L{l}_xattn_"
        a[f"a{l}_w"] = attention_weights(np, i[p + "Wq"], i[p + "Wk"], i[p + "Wv"], i[p + o])
        a[f"a{l}_bias"] = repeated(np, i[p + b])
    a["f2_gate"] = tiled(np, i["L2_ffn_w_gate"].T)
    a["f2_w"] = np.stack([np.concatenate([tiled(np, i["L2_ffn_w_in"][e]), tiled(np, i["L2_ffn_w_out"][e].T)], axis=1)
                          for e in range(EXPERTS)])
    a["f3_gate"] = tiled(np, i["L3_ffn_gate_w"].T)
    up = [*i["L3_ffn_up_w"], i["L3_ffn_sh_up_w"]]
    down = [*i["L3_ffn_down_w"], i["L3_ffn_sh_down_w"]]
    up_b = [*i["L3_ffn_up_b"], i["L3_ffn_sh_up_b"]]
    a["f3_w"] = np.stack([np.concatenate([tiled(np, u).reshape(P, -1), tiled(np, d).reshape(P, -1), b.reshape(KT, P).T], axis=1)
                          for u, d, b in zip(up, down, up_b)])
    a["f3_down_b"] = np.concatenate([i["L3_ffn_down_b"], i["L3_ffn_sh_down_b"][None]], axis=0)
    return {n: np.ascontiguousarray(v) for n, v in a.items()}


def kernel(**inputs):
    import numpy as np
    import concourse.bacc as bacc
    from concourse.bass_utils import run_bass_kernel_spmd

    nc = bacc.Bacc("TRN2", target_bir_lowering=False, num_devices=1)
    arrays = laid_out(np, {n: np.asarray(v) for n, v in inputs.items()})
    dram = {n: nc.dram_tensor(f"in_{n}", v.shape, mybir.dt.from_np(v.dtype), kind="ExternalInput").ap()
            for n, v in arrays.items()}
    out = nc.dram_tensor("out_x", (TOK, D), F32, kind="ExternalOutput").ap()
    build(nc, dram, out)
    result = run_bass_kernel_spmd(nc, [{f"in_{n}": v for n, v in arrays.items()}], core_ids=[0])
    return result.results[0]["out_x"].reshape(BATCH, SEQ, D)
```

```python
from contextlib import ExitStack, contextmanager

import concourse.bass as bass
from concourse import mybir

F32 = mybir.dt.float32
F32R = mybir.dt.float32r
BF16 = mybir.dt.bfloat16
ALU = mybir.AluOpType
ACT = mybir.ActivationFunctionType
AX = mybir.AxisListType

P = 128
BATCH, SEQ, D = 8, 112, 256
KEYS, DC = 375, 192
TOK = BATCH * SEQ
TILES = TOK // P
KT = D // P
NK = BATCH * KEYS
KB = 125
KTILES = NK // KB
TAIL = DC - P
CHUNK = 500
CHUNKS = NK // CHUNK
GROUPS = (TILES + 1) // 2
HEADS = 8
EPS = 1e-5
EXPERTS = 8
MAGIC = 1.5 * 2.0 ** 23


def need(eng, semaphore, value):
    if not (isinstance(value, int) and value <= 0):
        eng.wait_ge(semaphore, value)


@contextmanager
def phase_semaphores(nc, prefix=""):
    taken = []

    def sem(name):
        taken.append(nc.alloc_semaphore(name=prefix + name))
        return taken[-1]

    yield sem
    nc.clear_and_free_semaphores(taken)
    nc.all_engine_barrier()


class Names:
    pass


def layer_norm_buffers(sb, tag, width=TILES, rows=P):
    b = Names()
    b.stats = sb(f"{tag}_stats", [rows, width, 6])
    b.mean_var = sb(f"{tag}_mean_var", [rows, width, 2])
    b.root = sb(f"{tag}_root", [rows, 6, width])
    return b


def layer_norm_semaphores(sem, tag):
    q = Names()
    q.stats = sem(f"{tag}_stats_done")
    q.aggr = sem(f"{tag}_aggr_done")
    q.var = sem(f"{tag}_var_ready")
    q.std = sem(f"{tag}_std_ready")
    q.newton = sem(f"{tag}_newton_step")
    q.normed = sem(f"{tag}_normed")
    q.turned = sem(f"{tag}_turned")
    q.high = sem(f"{tag}_high_done")
    q.done = sem(f"{tag}_low_done")
    return q


def layer_norm_vector(dve, b, q, src, dst, width=TILES, ready=None):
    for i in range(width):
        if ready is not None:
            dve.wait_ge(*ready(i))
        dve.bn_stats(b.stats[:, i, :], src[:, i, :]).then_inc(q.stats, 1)
    dve.wait_ge(q.stats, width)
    for i in range(width):
        dve.bn_aggr(b.mean_var[:, i, :], b.stats[:, i, :]).then_inc(q.aggr, 1)
    dve.wait_ge(q.aggr, width)
    var, std, y0, t, u, y = (b.root[:, k, :] for k in range(6))
    dve.tensor_scalar(var, b.mean_var[:, :, 1], EPS, None, ALU.add).then_inc(q.var, 1)
    dve.wait_ge(q.std, 1)
    dve.reciprocal(y0, std).then_inc(q.newton, 1)
    dve.wait_ge(q.newton, 1)
    dve.tensor_tensor(t, y0, y0, ALU.mult).then_inc(q.newton, 1)
    dve.wait_ge(q.newton, 2)
    dve.scalar_tensor_tensor(u, t, -0.5, var, ALU.mult, ALU.mult).then_inc(q.newton, 1)
    dve.wait_ge(q.newton, 3)
    dve.scalar_tensor_tensor(y, u, 1.5, y0, ALU.add, ALU.mult).then_inc(q.newton, 1)
    dve.wait_ge(q.newton, 4)
    for i in range(width):
        dve.tensor_scalar(dst[:, i, :], src[:, i, :], b.mean_var[:, i, 0:1], y[:, i:i + 1],
                          ALU.subtract, ALU.mult).then_inc(q.normed, 1)


def layer_norm_scalar(act, b, q):
    act.wait_ge(q.var, 1)
    act.activation(b.root[:, 1, :], b.root[:, 0, :], ACT.Sqrt).then_inc(q.std, 1)


def turn_tensor(pe, q, src, banks, ident):
    for g in range(GROUPS):
        tiles = range(2 * g, min(2 * g + 2, TILES))
        pe.wait_ge(q.normed, tiles[-1] + 1)
        for i in tiles:
            for k in range(KT):
                at = k * 2 * P + (i % 2) * P
                last = pe.transpose(banks[g][:, at:at + P], src[:, i, k * P:(k + 1) * P], ident)
        last.then_inc(q.turned, 1)


def turned_view(bank, g):
    width = min(2 * P, TOK - g * 2 * P)
    return bank[:, :].rearrange("p (k c) -> p k c", k=KT)[:, :, 0:width], slice(g * 2 * P, g * 2 * P + width)


def turn_scalar(act, q, banks, TH):
    for g in range(GROUPS):
        view, cols = turned_view(banks[g], g)
        act.wait_ge(q.turned, g + 1)
        act.activation(TH[:, :, cols], view, ACT.Copy).then_inc(q.high, 1)


def turn_vector(dve, q, banks, TH, TL):
    for g in range(GROUPS):
        view, cols = turned_view(banks[g], g)
        dve.wait_ge(q.high, g + 1)
        dve.tensor_tensor(TL[:, :, cols], view, TH[:, :, cols].bitcast(F32), ALU.subtract).then_inc(q.done, 1)


def split_products(pe, out, terms, start=True, stop=True):
    for n, (a, b) in enumerate(terms):
        last = pe.matmul(out, a, b, start=start and n == 0, stop=stop and n == len(terms) - 1)
    return last


def layer0_attention(nc, s, dram):
    with ExitStack() as ctx:
        def sb(name, shape, dt=F32):
            return ctx.enter_context(nc.sbuf_tensor(name, shape, dt))

        sem = ctx.enter_context(phase_semaphores(nc))

        ctx_rows = sb("a0_ctx_rows", [KB, KTILES, DC])
        raw_main = sb("a0_raw_main", [P, NK])
        raw_tail = sb("a0_raw_tail", [P, NK])
        c_main = sb("a0_c_main", [P, NK])
        c_tail = sb("a0_c_tail", [TAIL, NK])
        kT = sb("a0_kT", [P, KT, NK])
        v = sb("a0_v", [KB, KTILES, D])
        xa = sb("a0_xa", [P, TILES, D])
        xT = sb("a0_xT", [P, KT, TOK])
        qT = sb("a0_qT", [P, KT, TOK])
        w_k = sb("a0_w_k", [P, 2, D])
        w_v = sb("a0_w_v", [P, 2, D])
        w_q = sb("a0_w_q", [P, KT, D])
        w_o = sb("a0_w_o", [P, KT, D])
        cols = sb("a0_cols", [P, 12])
        rows = sb("a0_rows", [P, 2, D])
        prob = sb("a0_prob", [SEQ, 2, KEYS])
        pT = sb("a0_pT", [KB, 2, 3, SEQ])
        nmax = sb("a0_nmax", [SEQ, 2])
        rsum = sb("a0_rsum", [SEQ, 2])
        rinv = sb("a0_rinv", [SEQ, 2])
        tail_high = sb("a0_tail_high", [P, NK // 2], F32R)
        oT = xT
        ln_c = layer_norm_buffers(sb, "a0_ln_c", KTILES, KB)
        ln_x = layer_norm_buffers(sb, "a0_ln_x")
        ln_y = layer_norm_buffers(sb, "a0_ln_y")
        qc = layer_norm_semaphores(sem, "a0_lc")
        qx = layer_norm_semaphores(sem, "a0_lx")
        qy = layer_norm_semaphores(sem, "a0_ly")
        g1, b1 = cols[:, 0:2], cols[:, 2:4]
        g2, b2 = cols[:, 4:6], cols[:, 6:8]
        bq, bk = cols[:, 8:10], cols[:, 10:12]

        LOADS = 4
        PER = KTILES // LOADS
        ctx_loaded = [sem(f"a0_ctx_loaded{n}") for n in range(LOADS)]
        x_loaded = sem("a0_x_loaded")
        small_loaded = sem("a0_small_loaded")
        w_loaded = sem("a0_w_loaded")
        raw_loaded = sem("a0_raw_loaded")
        c_main_done, c_tail_done = sem("a0_c_main_done"), sem("a0_c_tail_done")
        c_turned = sem("a0_c_turned")
        k_filled, k_done = sem("a0_k_filled"), sem("a0_k_done")
        v_filled, v_done = sem("a0_v_filled"), sem("a0_v_done")
        q_filled, q_done = sem("a0_q_filled"), sem("a0_q_done")
        xT_done = sem("a0_xT_done")
        s_filled, max_ready, exp_done, p_normed = (sem("a0_s_filled"), sem("a0_max_ready"),
                                                   sem("a0_exp_done"), sem("a0_p_normed"))
        rinv_ready = sem("a0_rinv_ready")
        t_filled, t_done, o_filled, o_done = (sem("a0_t_filled"), sem("a0_t_done"),
                                              sem("a0_o_filled"), sem("a0_o_done"))
        y_filled, y_added, bias_added = sem("a0_y_filled"), sem("a0_y_added"), sem("a0_bias_added")
        cut_high, cut_done = sem("a0_cut_high"), sem("a0_cut_done")
        B = s.banks
        GRP = 4
        NG = KTILES // GRP

        block = ctx.enter_context(nc.Block())

        @block.sync
        def _(sp):
            c_dram = dram["ctx_rows"].rearrange("(j p) d -> p j d", p=KB)
            for n in range(LOADS):
                sp.dma_start(ctx_rows[:, n * PER:(n + 1) * PER, :],
                             c_dram[:, n * PER:(n + 1) * PER, :]).then_inc(ctx_loaded[n], 16)
            sp.dma_start(s.x[:], dram["x"].rearrange("(t p) d -> p t d", p=P)).then_inc(x_loaded, 16)
            sp.dma_start(s.ident[:], dram["ident"]).then_inc(small_loaded, 16)
            sp.dma_start(s.ones[:], dram["ones"]).then_inc(small_loaded, 16)
            sp.dma_start(s.earlier[:], dram["earlier"]).then_inc(small_loaded, 16)
            sp.dma_start(cols[:], dram["a0_cols"]).then_inc(small_loaded, 16)
            sp.dma_start(rows[:], dram["a0_rows"]).then_inc(small_loaded, 16)
            for w, name in ((w_k, "a0_wk"), (w_v, "a0_wv")):
                sp.dma_start(w[:, 0, :], dram[name][0:P, :]).then_inc(w_loaded, 16)
                sp.dma_start(w[0:TAIL, 1, :], dram[name][P:DC, :]).then_inc(w_loaded, 16)
            for w, name in ((w_q, "a0_wq"), (w_o, "a0_wo")):
                sp.dma_start(w[:], dram[name].rearrange("(k p) n -> p k n", p=P)).then_inc(w_loaded, 16)
            sp.dma_start(raw_main[:], dram["ctx_cols"][0:P, :]).then_inc(raw_loaded, 16)
            sp.dma_start(raw_tail[0:TAIL, :], dram["ctx_cols"][P:DC, :]).then_inc(raw_loaded, 16)
            sp.dma_start(raw_tail[TAIL:P, :], dram["ctx_cols"][P:DC, :]).then_inc(raw_loaded, 16)

        @block.gpsimd
        def _(pool):
            pool.wait_ge(raw_loaded, 48)
            pool.tensor_copy(s.ctxH[:], raw_main[:]).then_inc(cut_high, 1)
            pool.wait_ge(cut_high, 1)
            pool.tensor_tensor(s.ctxL[:], raw_main[:], s.ctxH[:].bitcast(F32), ALU.subtract).then_inc(cut_done, 1)
            pool.wait_ge(cut_done, 1)
            pool.tensor_copy(s.ctxT[0:TAIL, :], raw_tail[0:TAIL, :]).then_inc(cut_done, 1)
            for n in range(2):
                half = slice(n * NK // 2, (n + 1) * NK // 2)
                pool.wait_ge(cut_done, n + 2)
                pool.tensor_copy(tail_high[TAIL:P, :], raw_tail[TAIL:P, half]).then_inc(cut_high, 1)
                pool.wait_ge(cut_high, n + 2)
                pool.tensor_tensor(s.ctxT[TAIL:P, half], raw_tail[TAIL:P, half],
                                   tail_high[TAIL:P, :].bitcast(F32), ALU.subtract).then_inc(cut_done, 1)

        @block.vector
        def _(dve):
            layer_norm_vector(dve, ln_c, qc, ctx_rows, ctx_rows, KTILES,
                              ready=lambda i: (ctx_loaded[i // PER], 16))
            dve.wait_ge(x_loaded, 16)
            layer_norm_vector(dve, ln_x, qx, s.x, xa)
            dve.wait_ge(small_loaded, 80)
            for g in range(NG):
                dve.wait_ge(c_turned, g + 1)
                dve.tensor_scalar(c_tail[:, g * CHUNK:(g + 1) * CHUNK], B[2 + g % 2][0:TAIL, 0:CHUNK],
                                  g2[0:TAIL, 1:2], b2[0:TAIL, 1:2], ALU.mult, ALU.add).then_inc(c_tail_done, 1)
            dve.wait_ge(qx.normed, TILES)
            layer_norm_vector(dve, ln_y, qy, xa, xa)
            dve.tensor_tensor(s.x[:], s.x[:], rows[:, 1:2, :].to_broadcast([P, TILES, D]),
                              ALU.add).then_inc(bias_added, 1)
            for n in range(4):
                dve.wait_ge(q_filled, n + 1)
                e, half = n // 2, slice((n % 2) * 448, (n % 2) * 448 + 448)
                dve.tensor_scalar(qT[:, e, half], B[4 + n][:, 0:448], bq[:, e:e + 1], D ** -0.5,
                                  ALU.add, ALU.mult).then_inc(q_done, 1)
            for n in range(KTILES // 2):
                dve.wait_ge(v_filled, n + 1)
                dve.tensor_tensor(v[:, 2 * n:2 * n + 2, :],
                                  B[2 + n % 2][0:KB, :].rearrange("p (t d) -> p t d", t=2),
                                  rows[0:KB, 0:1, :].to_broadcast([KB, 2, D]), ALU.add).then_inc(v_done, 1)

            def soft_max(b):
                dve.wait_ge(s_filled, b + 1)
                dve.tensor_reduce(nmax[:, b % 2:b % 2 + 1], B[b % 2][0:SEQ, 0:KEYS], AX.X, ALU.max,
                                  negate=True).then_inc(max_ready, 1)

            soft_max(0)
            for b in range(BATCH):
                if b + 1 < BATCH:
                    soft_max(b + 1)
                dve.wait_ge(exp_done, b + 1)
                dve.reciprocal(rinv[:, b % 2:b % 2 + 1], rsum[:, b % 2:b % 2 + 1]).then_inc(rinv_ready, 1)
                dve.wait_ge(rinv_ready, b + 1)
                dve.tensor_scalar(prob[:, b % 2, :], prob[:, b % 2, :], rinv[:, b % 2:b % 2 + 1], None,
                                  ALU.mult).then_inc(p_normed, 1)
                dve.wait_ge(o_filled, b + 1)
                dve.tensor_copy(oT[:, :, b * SEQ:(b + 1) * SEQ],
                                B[4 + b % 2][:, 0:KT * SEQ].rearrange("p (k c) -> p k c", k=KT)).then_inc(o_done, 1)
            dve.wait_ge(bias_added, 1)
            for i in range(TILES):
                dve.wait_ge(y_filled, i + 1)
                dve.tensor_tensor(s.x[:, i, :], s.x[:, i, :], B[6 + i % 2][:, 0:D], ALU.add).then_inc(y_added, 1)

        @block.scalar
        def _(act):
            layer_norm_scalar(act, ln_c, qc)
            layer_norm_scalar(act, ln_x, qx)
            act.wait_ge(small_loaded, 80)
            for g in range(NG):
                act.wait_ge(c_turned, g + 1)
                act.activation(c_main[:, g * CHUNK:(g + 1) * CHUNK], B[g % 2][:, 0:CHUNK], ACT.Identity,
                               scale=g2[:, 0:1], bias=b2[:, 0:1]).then_inc(c_main_done, 1)
            layer_norm_scalar(act, ln_y, qy)
            for g in range(GROUPS):
                view, c = turned_view(B[4 + g], g)
                act.wait_ge(qy.turned, g + 1)
                for k in range(KT):
                    act.activation(xT[:, k, c], view[:, k, :], ACT.Identity,
                                   scale=g1[:, k:k + 1], bias=b1[:, k:k + 1]).then_inc(xT_done, 1)
            for n in range(KT * CHUNKS):
                act.wait_ge(k_filled, n + 1)
                e, c = n // CHUNKS, n % CHUNKS
                act.activation(kT[:, e, c * CHUNK:(c + 1) * CHUNK], B[n % 2][:, 0:CHUNK], ACT.Identity,
                               bias=bk[:, e:e + 1]).then_inc(k_done, 1)
            for b in range(BATCH):
                act.wait_ge(max_ready, b + 1)
                act.activation(prob[:, b % 2, :], B[b % 2][0:SEQ, 0:KEYS], ACT.Exp, bias=nmax[:, b % 2:b % 2 + 1],
                               accum_out=rsum[:, b % 2:b % 2 + 1]).then_inc(exp_done, 1)
                act.wait_ge(t_filled, b + 1)
                act.activation(pT[:, b % 2, :, :], B[2 + b % 2][0:KB, 0:3 * SEQ].rearrange("p (t c) -> p t c", t=3),
                               ACT.Copy).then_inc(t_done, 1)

        @block.tensor
        def _(pe):
            pe.wait_ge(small_loaded, 80)
            pe.wait_ge(qc.normed, KTILES)
            for g in range(NG):
                need(pe, c_main_done, g - 1)
                need(pe, c_tail_done, g - 1)
                for j in range(GRP):
                    t, at = g * GRP + j, j * KB
                    pe.transpose(B[g % 2][:, at:at + KB], ctx_rows[:, t, 0:P], s.ident[0:KB, 0:KB])
                    last = pe.transpose(B[2 + g % 2][0:TAIL, at:at + KB], ctx_rows[:, t, P:DC], s.ident[0:KB, 0:KB])
                last.then_inc(c_turned, 1)
            turn_tensor(pe, qy, xa, B[4:8], s.ident[:])
            pe.wait_ge(w_loaded, 96)
            pe.wait_ge(c_main_done, NG)
            pe.wait_ge(c_tail_done, NG)
            for n in range(KT * CHUNKS):
                e, c = n // CHUNKS, n % CHUNKS
                need(pe, k_done, n - 1)
                split_products(pe, B[n % 2][:, 0:CHUNK], [
                    (w_k[:, 0, e * P:(e + 1) * P], c_main[:, c * CHUNK:(c + 1) * CHUNK]),
                    (w_k[0:TAIL, 1, e * P:(e + 1) * P], c_tail[:, c * CHUNK:(c + 1) * CHUNK])]).then_inc(k_filled, 1)
            pe.wait_ge(xT_done, KT * GROUPS)
            for n in range(4):
                e, half = n // 2, slice((n % 2) * 448, (n % 2) * 448 + 448)
                split_products(pe, B[4 + n][:, 0:448], [
                    (w_q[:, k, e * P:(e + 1) * P], xT[:, k, half]) for k in range(KT)]).then_inc(q_filled, 1)
            for n in range(KTILES // 2):
                need(pe, v_done, n - 1)
                for j in range(2):
                    t = 2 * n + j
                    last = split_products(pe, B[2 + n % 2][0:KB, j * D:(j + 1) * D], [
                        (c_main[:, t * KB:(t + 1) * KB], w_v[:, 0, :]),
                        (c_tail[:, t * KB:(t + 1) * KB], w_v[0:TAIL, 1, :])])
                last.then_inc(v_filled, 1)

            def scores(b):
                if b == 0:
                    pe.wait_ge(k_done, KT * CHUNKS)
                    pe.wait_ge(q_done, 4)
                need(pe, exp_done, b - 1)
                split_products(pe, B[b % 2][0:SEQ, 0:KEYS], [
                    (qT[:, k, b * SEQ:(b + 1) * SEQ], kT[:, k, b * KEYS:(b + 1) * KEYS])
                    for k in range(KT)]).then_inc(s_filled, 1)

            scores(0)
            for b in range(BATCH):
                if b + 1 < BATCH:
                    scores(b + 1)
                if b == 0:
                    pe.wait_ge(v_done, KTILES // 2)
                need(pe, t_done, b - 1)
                pe.wait_ge(p_normed, b + 1)
                for t in range(3):
                    last = pe.transpose(B[2 + b % 2][0:KB, t * SEQ:(t + 1) * SEQ], prob[:, b % 2, t * KB:(t + 1) * KB],
                                        s.ident[0:SEQ, 0:SEQ])
                last.then_inc(t_filled, 1)
                need(pe, o_done, b - 1)
                pe.wait_ge(t_done, b + 1)
                for e in range(KT):
                    last = split_products(pe, B[4 + b % 2][:, e * SEQ:(e + 1) * SEQ], [
                        (v[:, 3 * b + t, e * P:(e + 1) * P], pT[:, b % 2, t, :]) for t in range(3)])
                last.then_inc(o_filled, 1)
            pe.wait_ge(o_done, BATCH)
            for i in range(TILES):
                need(pe, y_added, i - 1)
                split_products(pe, B[6 + i % 2][:, 0:D], [
                    (oT[:, k, i * P:(i + 1) * P], w_o[:, k, :]) for k in range(KT)]).then_inc(y_filled, 1)


def router_buffers(sb, tag):
    r = Names()
    r.raw = sb(f"{tag}_gate_raw", [P, KT, EXPERTS])
    r.gH = sb(f"{tag}_gateH", [P, KT, EXPERTS], F32R)
    r.gL = sb(f"{tag}_gateL", [P, KT, EXPERTS], F32R)
    r.logits = sb(f"{tag}_logits", [P, TILES, EXPERTS])
    r.shifted = sb(f"{tag}_shifted", [P, TILES, EXPERTS])
    r.exps = sb(f"{tag}_exps", [P, TILES, EXPERTS])
    r.probs = sb(f"{tag}_probs", [P, TILES, EXPERTS])
    r.rank = sb(f"{tag}_rank", [P, TILES, EXPERTS])
    r.kept = sb(f"{tag}_kept", [P, TILES, EXPERTS])
    r.above = sb(f"{tag}_above", [P, TILES, EXPERTS, EXPERTS])
    r.ties = sb(f"{tag}_ties", [P, TILES, EXPERTS, EXPERTS])
    r.sums = sb(f"{tag}_sums", [P, 5, TILES])
    return r


def router_semaphores(sem, tag):
    q = Names()
    q.loaded = sem(f"{tag}_gate_loaded")
    q.cut = sem(f"{tag}_gate_cut")
    q.filled = sem(f"{tag}_logits_filled")
    q.step = sem(f"{tag}_route_step")
    q.shifted = sem(f"{tag}_logits_shifted")
    q.exps = sem(f"{tag}_exps_done")
    q.kept = sem(f"{tag}_route_ready")
    return q


def router_cut(pool, r, q):
    pool.wait_ge(q.loaded, 16)
    pool.tensor_copy(r.gH[:], r.raw[:]).then_inc(q.cut, 1)
    pool.wait_ge(q.cut, 1)
    pool.tensor_tensor(r.gL[:], r.raw[:], r.gH[:].bitcast(F32), ALU.subtract).then_inc(q.cut, 1)


def router_tensor(pe, s, r, q, bank):
    pe.wait_ge(q.cut, 2)
    for i in range(TILES):
        tok = slice(i * P, (i + 1) * P)
        last = split_products(pe, bank[:, i * EXPERTS:(i + 1) * EXPERTS], [
            pair for k in range(KT) for pair in (
                (s.xnTH[:, k, tok], r.gH[:, k, :]), (s.xnTH[:, k, tok], r.gL[:, k, :]),
                (s.xnTL[:, k, tok], r.gH[:, k, :]))])
    last.then_inc(q.filled, 1)


def router_scalar(act, r, q):
    act.wait_ge(q.shifted, 1)
    act.activation(r.exps[:], r.shifted[:], ACT.Exp).then_inc(q.exps, 1)


def over_experts(row):
    return row.unsqueeze(2).to_broadcast([P, TILES, EXPERTS])


def router_ranks(dve, s, r, q, key, at):
    every = [P, TILES, EXPERTS, EXPERTS]
    mine, others = key.unsqueeze(3).to_broadcast(every), key.unsqueeze(2).to_broadcast(every)
    dve.tensor_tensor(r.above[:], others, mine, ALU.is_gt).then_inc(q.step, 1)
    dve.tensor_tensor(r.ties[:], others, mine, ALU.is_equal).then_inc(q.step, 1)
    dve.wait_ge(q.step, at + 2)
    dve.tensor_tensor(r.ties[:], r.ties[:], s.earlier[:].unsqueeze(1).to_broadcast(every), ALU.mult).then_inc(q.step, 1)
    dve.wait_ge(q.step, at + 3)
    dve.tensor_tensor(r.above[:], r.above[:], r.ties[:], ALU.add).then_inc(q.step, 1)
    dve.wait_ge(q.step, at + 4)
    dve.tensor_reduce(r.rank[:], r.above[:], AX.X, ALU.add).then_inc(q.step, 1)
    dve.wait_ge(q.step, at + 5)
    return at + 5


def router_exps(dve, r, q, bank):
    dve.wait_ge(q.filled, 1)
    dve.tensor_copy(r.logits[:], bank[:, 0:TILES * EXPERTS].rearrange("p (t e) -> p t e", e=EXPERTS)).then_inc(q.step, 1)
    dve.wait_ge(q.step, 1)
    dve.tensor_reduce(r.sums[:, 0, :], r.logits[:], AX.X, ALU.max).then_inc(q.step, 1)
    dve.wait_ge(q.step, 2)
    dve.tensor_tensor(r.shifted[:], r.logits[:], over_experts(r.sums[:, 0, :]), ALU.subtract).then_inc(q.shifted, 1)
    return 2


def router_softmax(dve, r, q, at):
    dve.wait_ge(q.exps, 1)
    dve.tensor_reduce(r.sums[:, 1, :], r.exps[:], AX.X, ALU.add).then_inc(q.step, 1)
    dve.wait_ge(q.step, at + 1)
    dve.reciprocal(r.sums[:, 2, :], r.sums[:, 1, :]).then_inc(q.step, 1)
    dve.wait_ge(q.step, at + 2)
    dve.tensor_tensor(r.probs[:], r.exps[:], over_experts(r.sums[:, 2, :]), ALU.mult).then_inc(q.step, 1)
    dve.wait_ge(q.step, at + 3)
    return at + 3


def router_keep_two(dve, r, q, at, values, out, tiny):
    dve.scalar_tensor_tensor(r.kept[:], r.rank[:], 1.5, values, ALU.is_lt, ALU.mult).then_inc(q.step, 1)
    dve.wait_ge(q.step, at + 1)
    dve.tensor_reduce(r.sums[:, 3, :], r.kept[:], AX.X, ALU.add).then_inc(q.step, 1)
    dve.wait_ge(q.step, at + 2)
    dve.tensor_scalar(r.sums[:, 4, :], r.sums[:, 3, :], tiny, None, ALU.add).then_inc(q.step, 1)
    dve.wait_ge(q.step, at + 3)
    dve.reciprocal(r.sums[:, 2, :], r.sums[:, 4, :]).then_inc(q.step, 1)
    dve.wait_ge(q.step, at + 4)
    dve.tensor_tensor(out, r.kept[:], over_experts(r.sums[:, 2, :]), ALU.mult).then_inc(q.kept, 1)


def layer0_ffn(nc, s, dram):
    with ExitStack() as ctx:
        def sb(name, shape, dt=F32):
            return ctx.enter_context(nc.sbuf_tensor(name, shape, dt))

        sem = ctx.enter_context(phase_semaphores(nc))

        WIDE = 2 * D
        xn = sb("f0_xn", [P, TILES, D])
        w_raw = sb("f0_w_raw", [P, KT, WIDE])
        wH = sb("f0_wH", [P, KT, WIDE], F32R)
        wL = sb("f0_wL", [P, KT, WIDE], F32R)
        bias = sb("f0_bias", [P, WIDE])
        pre = sb("f0_pre", [P, 2, WIDE])
        post = sb("f0_post", [P, 2, WIDE])
        coef = sb("f0_coef", [P, 2, TILES])
        quant_raw = sb("f0_quant_raw", [P, 3, 2048])
        quant_work = sb("f0_quant_work", [P, 2048])
        ln = layer_norm_buffers(sb, "f0_ln")
        r = router_buffers(sb, "f0")
        ql = layer_norm_semaphores(sem, "f0_ln")
        q = router_semaphores(sem, "f0_r")
        w_loaded, w_cut = sem("f0_w_loaded"), sem("f0_w_cut")
        e_filled, pre_ready, post_ready, x_added = (sem("f0_e_filled"), sem("f0_pre_ready"),
                                                    sem("f0_post_ready"), sem("f0_x_added"))
        first_added = sem("f0_first_added")
        quant_loaded, abs_summed, abs_total = sem("f0_quant_loaded"), sem("f0_abs_summed"), sem("f0_abs_total")
        scale_step, scale_ready = sem("f0_scale_step"), sem("f0_scale_ready")
        quant_step, quant_done = sem("f0_quant_step"), sem("f0_quant_done")
        abs_sum = sb("f0_abs_sum", [P, 3])
        w_scale = sb("f0_w_scale", [P, 3])
        B = s.banks
        block = ctx.enter_context(nc.Block())

        @block.sync
        def _(sp):
            sp.dma_start(r.raw[:], dram["f0_gate"]).then_inc(q.loaded, 16)
            sp.dma_start(w_raw[:], dram["f0_w"]).then_inc(w_loaded, 16)
            sp.dma_start(bias[:], dram["f0_bias"]).then_inc(w_loaded, 16)
            sp.dma_start(quant_raw[:], dram["f1_w"]).then_inc(quant_loaded, 16)

        @block.gpsimd
        def _(pool):
            router_cut(pool, r, q)
            pool.wait_ge(w_loaded, 32)
            pool.tensor_copy(wH[:], w_raw[:]).then_inc(w_cut, 1)
            pool.wait_ge(w_cut, 1)
            pool.tensor_tensor(wL[:], w_raw[:], wH[:].bitcast(F32), ALU.subtract).then_inc(w_cut, 1)
            pool.wait_ge(scale_ready, 1)
            for m in range(3):
                need(pool, quant_done, m)
                pool.tensor_scalar(quant_work[:], quant_raw[:, m, :], w_scale[:, m:m + 1], MAGIC,
                                   ALU.mult, ALU.add).then_inc(quant_step, 1)
                pool.wait_ge(quant_step, 2 * m + 1)
                pool.tensor_scalar(quant_work[:], quant_work[:], MAGIC + 1.0, MAGIC - 1.0,
                                   ALU.min, ALU.max).then_inc(quant_step, 1)
                pool.wait_ge(quant_step, 2 * m + 2)
                pool.tensor_scalar(s.w_quant[:, m, :], quant_work[:], -MAGIC, 1.0,
                                   ALU.add, ALU.mult).then_inc(quant_done, 1)

        @block.vector
        def _(dve):
            layer_norm_vector(dve, ln, ql, s.x, xn)
            turn_vector(dve, ql, B[4:8], s.xnTH, s.xnTL)
            at = router_exps(dve, r, q, B[0])
            at = router_softmax(dve, r, q, at)
            at = router_ranks(dve, s, r, q, r.probs[:], at)
            for e in range(2):
                dve.scalar_tensor_tensor(coef[:, e, :], r.rank[:, :, e], float(e), r.probs[:, :, e],
                                         ALU.is_equal, ALU.mult).then_inc(q.kept, 1)
            dve.wait_ge(w_loaded, 32)

            def bias_add(i):
                dve.wait_ge(e_filled, i + 1)
                dve.tensor_tensor(pre[:, i % 2, :], B[1 + i % 2][:, :], bias[:], ALU.add).then_inc(pre_ready, 1)

            bias_add(0)
            for i in range(TILES):
                if i + 1 < TILES:
                    bias_add(i + 1)
                if i == 0:
                    dve.wait_ge(q.kept, 2)
                dve.wait_ge(post_ready, i + 1)
                dve.scalar_tensor_tensor(s.x[:, i, :], post[:, i % 2, 0:D], coef[:, 0, i:i + 1], s.x[:, i, :],
                                         ALU.mult, ALU.add).then_inc(first_added, 1)
                dve.wait_ge(first_added, i + 1)
                dve.scalar_tensor_tensor(s.x[:, i, :], post[:, i % 2, D:WIDE], coef[:, 1, i:i + 1], s.x[:, i, :],
                                         ALU.mult, ALU.add).then_inc(x_added, 1)
            dve.wait_ge(quant_loaded, 16)
            for m in range(3):
                dve.tensor_reduce(abs_sum[:, m:m + 1], quant_raw[:, m, :], AX.X, ALU.add,
                                  apply_absolute_value=True).then_inc(abs_summed, 1)
            dve.wait_ge(abs_total, 1)
            dve.tensor_scalar(s.w_mean[:], B[3][:, 0:3], 1.0 / (P * 2048), EPS, ALU.mult, ALU.max).then_inc(scale_step, 1)
            dve.wait_ge(scale_step, 1)
            dve.reciprocal(w_scale[:], s.w_mean[:]).then_inc(scale_ready, 1)

        @block.scalar
        def _(act):
            layer_norm_scalar(act, ln, ql)
            turn_scalar(act, ql, B[4:8], s.xnTH)
            router_scalar(act, r, q)
            for i in range(TILES):
                act.wait_ge(pre_ready, i + 1)
                need(act, x_added, i - 1)
                act.activation(post[:, i % 2, :], pre[:, i % 2, :], ACT.Silu).then_inc(post_ready, 1)

        @block.tensor
        def _(pe):
            turn_tensor(pe, ql, xn, B[4:8], s.ident[:])
            pe.wait_ge(ql.done, GROUPS)
            router_tensor(pe, s, r, q, B[0])
            pe.wait_ge(w_cut, 2)
            for i in range(TILES):
                tok = slice(i * P, (i + 1) * P)
                need(pe, pre_ready, i - 1)
                split_products(pe, B[1 + i % 2][:, :], [
                    pair for k in range(KT) for pair in (
                        (s.xnTH[:, k, tok], wH[:, k, :]), (s.xnTH[:, k, tok], wL[:, k, :]),
                        (s.xnTL[:, k, tok], wH[:, k, :]))]).then_inc(e_filled, 1)
            pe.wait_ge(abs_summed, 3)
            pe.matmul(B[3][:, 0:3], s.ones[:], abs_sum[:], start=True, stop=True).then_inc(abs_total, 1)
Q_W, K_W = (0, 1), (2, 3)
HALVES = [slice(0, TOK // 2), slice(TOK // 2, TOK)]
VWIDE = 2
VUSES = KTILES // VWIDE
VGROUP = 4
VGROUPS = KTILES // VGROUP
HIGHS = CHUNKS + 2
QKV = HIGHS + VUSES


class HeadBuffers:

    def __init__(self, sb, tag):
        self.w_raw = sb(f"{tag}_w_raw", [P, 6, P])
        self.wH = sb(f"{tag}_wH", [P, 4, P], F32R)
        self.wL = sb(f"{tag}_wL", [P, 4, P], F32R)
        self.wv = sb(f"{tag}_wvHL", [P, 2, 2, P], F32R)
        self.wo_raw = sb(f"{tag}_wo_raw", [P, D])
        self.woH = sb(f"{tag}_woH", [P, D], F32R)
        self.woL = sb(f"{tag}_woL", [P, D], F32R)
        self.kH = sb(f"{tag}_kH", [P, NK], F32R)
        self.kL = sb(f"{tag}_kL", [P, NK], F32R)
        self.v_sum = sb(f"{tag}_v_sum", [KB, 2, VGROUP, P])
        self.vH = sb(f"{tag}_vH", [KB, KTILES, P], F32R)
        self.vL = sb(f"{tag}_vL", [KB, KTILES, P], F32R)
        self.qH = sb(f"{tag}_qH", [P, TOK], F32R)
        self.qL = sb(f"{tag}_qL", [P, TOK], F32R)
        self.oH = sb(f"{tag}_oH", [P, TOK], F32R)
        self.oL = sb(f"{tag}_oL", [P, TOK], F32R)


class HeadSemaphores:
    def __init__(self, sem, tag):
        self.loaded = sem(f"{tag}_w_loaded")
        self.wo_loaded = sem(f"{tag}_wo_loaded")
        self.qk_high = sem(f"{tag}_qk_high")
        self.qk_cut = sem(f"{tag}_qk_cut")
        self.wv_high = sem(f"{tag}_wv_high")
        self.wv_cut = sem(f"{tag}_wv_cut")
        self.wo_high = sem(f"{tag}_wo_high")
        self.wo_cut = sem(f"{tag}_wo_cut")
        self.filled = sem(f"{tag}_g_filled")
        self.high = sem(f"{tag}_g_high")
        self.done = sem(f"{tag}_g_done")
        self.v_high = sem(f"{tag}_v_high")
        self.v_cut = sem(f"{tag}_v_cut")
        self.bias_loaded = sem(f"{tag}_bias_loaded")
        self.bias_added = sem(f"{tag}_bias_added")
        self.o_written = sem(f"{tag}_o_written")
        self.o_high = sem(f"{tag}_o_high")
        self.o_cut = sem(f"{tag}_o_cut")


def head_loads(sp, w, q, dram_w, dram_wo):
    sp.dma_start(w.w_raw[:], dram_w[0]).then_inc(q.loaded, 16)
    sp.dma_start(w.wo_raw[:], dram_wo[0]).then_inc(q.wo_loaded, 16)
    with sp.Fori(1, HEADS) as h:
        sp.wait_ge(q.wv_cut, h)
        sp.wait_ge(q.qk_cut, h)
        sp.dma_start(w.w_raw[:], dram_w[bass.ds(h, 1)].rearrange("o p t c -> p (o t) c")).then_inc(q.loaded, 16)
        sp.wait_ge(q.wo_cut, h)
        sp.dma_start(w.wo_raw[:], dram_wo[bass.ds(h, 1)].rearrange("o p c -> p (o c)")).then_inc(q.wo_loaded, 16)


def cut_qk(pool, s, w, q, h, used):
    pool.wait_ge(q.loaded, 16 * h + 16)
    need(pool, q.filled, used)
    pool.tensor_tensor(w.wH[:], w.w_raw[:, 0:4, :], s.ones[:].unsqueeze(1).to_broadcast([P, 4, P]), ALU.mult).then_inc(q.qk_high, 1)
    pool.wait_ge(q.qk_high, h + 1)
    pool.tensor_tensor(w.wL[:], w.w_raw[:, 0:4, :], w.wH[:].bitcast(F32), ALU.subtract).then_inc(q.qk_cut, 1)


def cut_wv(pool, s, w, q, h, used):
    need(pool, q.filled, used)
    pool.tensor_tensor(w.wv[:, :, 0, :], w.w_raw[:, 4:6, :], s.ones[:].unsqueeze(1).to_broadcast([P, 2, P]), ALU.mult)\
        .then_inc(q.wv_high, 1)
    pool.wait_ge(q.wv_high, h + 1)
    pool.tensor_tensor(w.wv[:, :, 1, :], w.w_raw[:, 4:6, :], w.wv[:, :, 0, :].bitcast(F32), ALU.subtract).then_inc(q.wv_cut, 1)


def cut_wo(pool, s, w, q, h, used):
    pool.wait_ge(q.wo_loaded, 16 * h + 16)
    need(pool, q.filled, used)
    pool.tensor_tensor(w.woH[:], w.wo_raw[:], s.ones[:, 0:1].to_broadcast([P, D]), ALU.mult).then_inc(q.wo_high, 1)
    pool.wait_ge(q.wo_high, h + 1)
    pool.tensor_tensor(w.woL[:], w.wo_raw[:], w.woH[:].bitcast(F32), ALU.subtract).then_inc(q.wo_cut, 1)


def bank_free(pe, q, banks, use, n, fresh):
    if not (fresh and n < len(banks)):
        pe.wait_ge(q.done, use + n - len(banks) + 1)


def project_keys(pe, s, w, q, banks, h, use):
    pe.wait_ge(q.qk_cut, h + 1)
    main, tail = K_W
    for c in range(CHUNKS):
        cols = slice(c * CHUNK, (c + 1) * CHUNK)
        bank_free(pe, q, banks, use, c, True)
        split_products(pe, banks[c % len(banks)][:, 0:CHUNK], [
            (w.wH[:, main, :], s.ctxH[:, cols]), (w.wH[:, main, :], s.ctxL[:, cols]), (w.wL[:, main, :], s.ctxH[:, cols]),
            (w.wH[:, tail, :], s.ctxT[:, cols]), (w.wL[:, tail, :], s.ctxT[:, cols])]).then_inc(q.filled, 1)


def project_queries(pe, s, w, q, banks, use):
    for n, half in enumerate(HALVES):
        at = CHUNKS + n
        bank_free(pe, q, banks, use, at, False)
        split_products(pe, banks[at % len(banks)][:, 0:TOK // 2], [pair for k in Q_W for pair in (
            (w.wH[:, k, :], s.xnTH[:, k, half]), (w.wH[:, k, :], s.xnTL[:, k, half]),
            (w.wL[:, k, :], s.xnTH[:, k, half]))]).then_inc(q.filled, 1)


def project_values(pe, s, w, q, banks, h, use):
    pe.wait_ge(q.wv_cut, h + 1)
    for n in range(VUSES):
        bank_free(pe, q, banks, use, n, True)
        for j in range(VWIDE):
            t = n * VWIDE + j
            cols = slice(t * KB, (t + 1) * KB)
            out = banks[n % len(banks)][0:KB, j * 2 * P:(j + 1) * 2 * P]
            both = [w.wv[:, k, :, :].rearrange("p a c -> p (a c)") for k in range(2)]
            pe.matmul(out, s.ctxH[:, cols], both[0], start=True, stop=False)
            pe.matmul(out[:, 0:P], s.ctxL[:, cols], w.wv[:, 0, 0, :], start=False, stop=False)
            last = pe.matmul(out, s.ctxT[:, cols], both[1], start=False, stop=True)
        last.then_inc(q.filled, 1)


def project_outputs(pe, w, q, banks, h, use, parts):
    pe.wait_ge(q.o_cut, parts * (h + 1))
    pe.wait_ge(q.wo_cut, h + 1)
    for g in range(GROUPS):
        bank_free(pe, q, banks, use, g, False)
        for i in range(2 * g, min(2 * g + 2, TILES)):
            tok = slice(i * P, (i + 1) * P)
            last = split_products(pe, banks[g % len(banks)][:, (i % 2) * D:(i % 2 + 1) * D], [
                (w.oH[:, tok], w.woH[:]), (w.oH[:, tok], w.woL[:]), (w.oL[:, tok], w.woH[:])])
        last.then_inc(q.filled, 1)


def high_keys(act, w, q, banks, use):
    for c in range(CHUNKS):
        act.wait_ge(q.filled, use + c + 1)
        act.activation(w.kH[:, c * CHUNK:(c + 1) * CHUNK], banks[c % len(banks)][:, 0:CHUNK], ACT.Copy).then_inc(q.high, 1)


def high_queries(act, w, q, banks, use, scale):
    for n, half in enumerate(HALVES):
        at = CHUNKS + n
        act.wait_ge(q.filled, use + at + 1)
        act.activation(w.qH[:, half], banks[at % len(banks)][:, 0:TOK // 2], ACT.Copy, scale=scale).then_inc(q.high, 1)


def high_values(act, w, q, use):
    for g in range(VGROUPS):
        act.wait_ge(q.done, use + 2 * g + 2)
        act.activation(w.vH[:, g * VGROUP:(g + 1) * VGROUP, :], w.v_sum[:, g % 2, :, :], ACT.Copy).then_inc(q.v_high, 1)


def low_keys(dve, w, q, banks, h):
    for c in range(CHUNKS):
        cols = slice(c * CHUNK, (c + 1) * CHUNK)
        dve.wait_ge(q.high, HIGHS * h + c + 1)
        dve.tensor_tensor(w.kL[:, cols], banks[c % len(banks)][:, 0:CHUNK], w.kH[:, cols].bitcast(F32),
                          ALU.subtract).then_inc(q.done, 1)


def low_queries(dve, w, q, banks, h, scale):
    for n, half in enumerate(HALVES):
        at = CHUNKS + n
        dve.wait_ge(q.high, HIGHS * h + at + 1)
        dve.scalar_tensor_tensor(w.qL[:, half], banks[at % len(banks)][:, 0:TOK // 2], scale, w.qH[:, half].bitcast(F32),
                                 ALU.mult, ALU.subtract).then_inc(q.done, 1)


def sum_values(dve, w, q, banks, h, use):
    def low(g):
        dve.wait_ge(q.v_high, VGROUPS * h + g + 1)
        dve.tensor_tensor(w.vL[:, g * VGROUP:(g + 1) * VGROUP, :], w.v_sum[:, g % 2, :, :],
                          w.vH[:, g * VGROUP:(g + 1) * VGROUP, :].bitcast(F32), ALU.subtract).then_inc(q.v_cut, 1)

    for n in range(VUSES):
        g = n // 2
        parts = banks[n % len(banks)][0:KB, :].rearrange("p (t a c) -> p t c a", t=VWIDE, a=2)
        dve.wait_ge(q.filled, use + n + 1)
        if n % 2 == 0 and g >= 2:
            dve.wait_ge(q.v_cut, VGROUPS * h + g - 1)
        dve.tensor_reduce(w.v_sum[:, g % 2, (n % 2) * VWIDE:(n % 2 + 1) * VWIDE, :], parts, AX.X, ALU.add).then_inc(q.done, 1)
        if n % 2 == 1 and g >= 1:
            low(g - 1)
    low(VGROUPS - 1)


def add_outputs(dve, s, q, banks, use):
    for g in range(GROUPS):
        tiles = slice(2 * g, min(2 * g + 2, TILES))
        wide = (tiles.stop - tiles.start) * D
        dve.wait_ge(q.filled, use + g + 1)
        dve.tensor_tensor(s.x[:, tiles, :], s.x[:, tiles, :],
                          banks[g % len(banks)][:, 0:wide].rearrange("p (t d) -> p t d", d=D), ALU.add).then_inc(q.done, 1)


def layer1_attention(nc, s, dram):
    SCALE = 1.5 * P ** -0.5
    RING = 3
    AHEAD = 3

    class Group:
        def __init__(self, tiles, at):
            self.tiles, self.wide, self.at = tiles, len(tiles) * P, at
            self.kts = 512 // self.wide
            self.chunks = KTILES // self.kts
            self.tok = slice(tiles[0] * P, (tiles[-1] + 1) * P)

    groups = [Group((0, 1), 0)]
    for tiles in ((2, 3), (4, 5, 6)):
        groups.append(Group(tiles, groups[-1].at + groups[-1].chunks))
    TCHUNKS = groups[-1].at + groups[-1].chunks
    NG = len(groups)
    EARLY = 4
    with ExitStack() as ctx:
        def sb(name, shape, dt=F32):
            return ctx.enter_context(nc.sbuf_tensor(f"a1_{name}", shape, dt))

        sem = ctx.enter_context(phase_semaphores(nc, "a1_"))
        w = HeadBuffers(sb, "head")
        prob = sb("prob", [P, RING, NK])
        xn = prob[:, 0, 0:TILES * D].rearrange("p (t d) -> p t d", d=D)
        pH = sb("pH", [KB, RING, 512], F32R)
        pL = sb("pL", [KB, RING, 512], F32R)
        o = sb("o", [P, groups[-1].wide])
        bias = sb("bias", [P, D])
        chunk_max = sb("chunk_max", [P, RING, CHUNKS])
        nmax = sb("nmax", [P, RING])
        rsum = sb("rsum", [P, RING])
        rinv = sb("rinv", [P, RING])
        spread = sb("spread", [P, groups[-1].wide])
        over_sums = sb("over_sums", [P, groups[-1].wide])
        ln = layer_norm_buffers(sb, "ln")
        ql = layer_norm_semaphores(sem, "ln")
        q = HeadSemaphores(sem, "head")
        s_filled, s_out, max_ready, exp_done = sem("s_filled"), sem("s_out"), sem("max_ready"), sem("exp_done")
        rinv_ready, spread_ready = sem("rinv_ready"), sem("spread_ready")
        t_filled, t_high, t_done, pv_done = sem("t_filled"), sem("t_high"), sem("t_done"), sem("pv_done")
        sums_filled, sums_out = sem("sums_filled"), sem("sums_out")
        B = s.banks
        SB, OB = B[0:3], B[5]
        TB = [B[6], B[7], B[3], B[4]]
        LNB = [*SB, OB]
        EACH = QKV + GROUPS

        def base(h):
            return 0 if isinstance(h, int) and h == 0 else EACH * h - GROUPS

        block = ctx.enter_context(nc.Block())

        @block.sync
        def _(sp):
            sp.dma_start(bias[:], dram["a1_bias"]).then_inc(q.bias_loaded, 16)
            head_loads(sp, w, q, dram["a1_w"], dram["a1_wo"])

        @block.gpsimd
        def _(pool):
            def cut_outputs(h, g):
                tok, n = groups[g].tok, NG * h + g
                pool.wait_ge(q.o_written, n + 1)
                mine = o[:, 0:groups[g].wide]
                pool.tensor_tensor(w.oH[:, tok], mine, s.ones[:, 0:1].to_broadcast([P, groups[g].wide]), ALU.mult)\
                    .then_inc(q.o_high, 1)
                pool.wait_ge(q.o_high, n + 1)
                pool.tensor_tensor(w.oL[:, tok], mine, w.oH[:, tok].bitcast(F32), ALU.subtract).then_inc(q.o_cut, 1)

            def head(h, last):
                if not last:
                    cut_qk(pool, s, w, q, h + 1, base(h) + HIGHS)
                    cut_wv(pool, s, w, q, h + 1, base(h) + QKV)
                for g in range(NG):
                    cut_outputs(h, g)
                if not last:
                    cut_wo(pool, s, w, q, h + 1, base(h + 1) + EACH)

            cut_qk(pool, s, w, q, 0, 0)
            cut_wv(pool, s, w, q, 0, 0)
            cut_wo(pool, s, w, q, 0, 0)
            head(0, False)
            with pool.Fori(1, HEADS - 1) as h:
                head(h, False)
            head(HEADS - 1, True)

        @block.tensor
        def _(pe):
            def scores(h, t):
                for c in range(CHUNKS):
                    n = CHUNKS * (TILES * h + t) + c
                    need(pe, s_out, n - 2)
                    cols, tok = slice(c * CHUNK, (c + 1) * CHUNK), slice(t * P, (t + 1) * P)
                    split_products(pe, SB[c % 3][:, 0:CHUNK], [
                        (w.qH[:, tok], w.kH[:, cols]), (w.qH[:, tok], w.kL[:, cols]),
                        (w.qL[:, tok], w.kH[:, cols])]).then_inc(s_filled, 1)

            def turn(g, c):
                for j in range(g.kts):
                    key = (c * g.kts + j) * KB
                    for i, t in enumerate(g.tiles):
                        at = j * g.wide + i * P
                        last = pe.transpose(TB[c % 4][0:KB, at:at + P], prob[:, t % RING, key:key + KB], s.ident[:])
                last.then_inc(t_filled, 1)

            def mix(h, g, c):
                n = TCHUNKS * h + g.at + c
                pe.wait_ge(t_done, n + 1)
                terms = []
                for j in range(g.kts):
                    k, cols = c * g.kts + j, slice(j * g.wide, (j + 1) * g.wide)
                    high, low = pH[:, c % RING, cols], pL[:, c % RING, cols]
                    terms += [(w.vH[:, k, :], high), (w.vL[:, k, :], high), (w.vH[:, k, :], low)]
                split_products(pe, OB[:, 0:g.wide], terms, c == 0, c == g.chunks - 1).then_inc(pv_done, 1)

            def turn_and_mix(h, g, between):
                group = groups[g]
                pe.wait_ge(exp_done, TILES * h + group.tiles[-1] + 1)
                need(pe, q.o_written, NG * h + g)
                for c in range(AHEAD):
                    turn(group, c)
                for c in range(group.chunks):
                    if c + AHEAD < group.chunks:
                        turn(group, c + AHEAD)
                        if c + AHEAD == group.chunks - 1 and between is not None:
                            scores(*between)
                    if c == group.chunks - 2:
                        pe.wait_ge(spread_ready, TILES * h + group.tiles[-1] + 1)
                        pe.matmul(TB[0][:, 0:group.wide], s.ones[:], spread[:, 0:group.wide], start=True, stop=True)\
                          .then_inc(sums_filled, 1)
                    mix(h, group, c)

            def head(h, last):
                following = h + 1
                scores(h, 2)
                turn_and_mix(h, 0, (h, 3))
                scores(h, 4)
                turn_and_mix(h, 1, (h, 5))
                scores(h, 6)
                if last:
                    turn_and_mix(h, 2, None)
                    return
                use = base(following)
                pe.wait_ge(q.o_written, NG * h + 2)
                project_keys(pe, s, w, q, TB, following, use)
                project_queries(pe, s, w, q, TB, use)
                pe.wait_ge(q.done, use + HIGHS)
                turn_and_mix(h, 2, (following, 0))
                scores(following, 1)
                pe.wait_ge(q.o_written, NG * following)
                project_values(pe, s, w, q, TB, following, use + HIGHS)
                project_outputs(pe, w, q, TB, h, use + QKV, NG)
                pe.wait_ge(q.done, use + EACH)
                pe.wait_ge(q.v_cut, VGROUPS * (following + 1))

            turn_tensor(pe, ql, xn, LNB, s.ident[:])
            pe.wait_ge(ql.done, GROUPS)
            project_keys(pe, s, w, q, TB, 0, 0)
            project_queries(pe, s, w, q, TB, 0)
            pe.wait_ge(q.done, HIGHS)
            scores(0, 0)
            scores(0, 1)
            project_values(pe, s, w, q, TB, 0, HIGHS)
            pe.wait_ge(q.done, QKV)
            pe.wait_ge(q.v_cut, VGROUPS)
            head(0, False)
            with pe.Fori(1, HEADS - 1) as h:
                head(h, False)
            head(HEADS - 1, True)
            pe.wait_ge(q.o_written, NG * HEADS)
            project_outputs(pe, w, q, TB, HEADS - 1, base(HEADS), NG)

        @block.scalar
        def _(act):
            def exps(h, t):
                act.wait_ge(max_ready, TILES * h + t + 1)
                act.activation(prob[:, t % RING, :], prob[:, t % RING, :], ACT.Exp, bias=nmax[:, t % RING:t % RING + 1],
                               accum_out=rsum[:, t % RING:t % RING + 1]).then_inc(exp_done, 1)

            def highs(h, n, between):
                g, group = groups[n], NG * h + n
                wide = g.kts * g.wide
                for c in range(g.chunks):
                    n = TCHUNKS * h + g.at + c
                    act.wait_ge(t_filled, n + 1)
                    need(act, pv_done, n + 1 - RING)
                    act.activation(pH[:, c % RING, 0:wide], TB[c % 4][0:KB, 0:wide], ACT.Copy).then_inc(t_high, 1)
                    if c == EARLY and between is not None:
                        exps(*between)
                act.wait_ge(sums_filled, group + 1)
                need(act, q.o_written, group)
                act.activation(over_sums[:, 0:g.wide], TB[0][:, 0:g.wide], ACT.Copy).then_inc(sums_out, 1)

            def head(h, last):
                following = h + 1
                highs(h, 0, (h, 2))
                exps(h, 3)
                highs(h, 1, (h, 4))
                exps(h, 5)
                exps(h, 6)
                if last:
                    highs(h, 2, None)
                    return
                use = base(following)
                high_keys(act, w, q, TB, use)
                high_queries(act, w, q, TB, use, 1.0)
                highs(h, 2, None)
                exps(following, 0)
                exps(following, 1)
                high_values(act, w, q, use + HIGHS)

            layer_norm_scalar(act, ln, ql)
            turn_scalar(act, ql, LNB, s.xnTH)
            high_keys(act, w, q, TB, 0)
            high_queries(act, w, q, TB, 0, 1.0)
            exps(0, 0)
            exps(0, 1)
            high_values(act, w, q, HIGHS)
            head(0, False)
            with act.Fori(1, HEADS - 1) as h:
                head(h, False)
            head(HEADS - 1, True)

        @block.vector
        def _(dve):
            def scores_out(h, t):
                at = t % RING
                for c in range(CHUNKS):
                    dve.wait_ge(s_filled, CHUNKS * (TILES * h + t) + c + 1)
                    dve.tensor_scalar(prob[:, at, c * CHUNK:(c + 1) * CHUNK], SB[c % 3][:, 0:CHUNK], SCALE, None,
                                      ALU.mult, ALU.max, accum_out=chunk_max[:, at, c:c + 1]).then_inc(s_out, 1)
                dve.wait_ge(s_out, CHUNKS * (TILES * h + t + 1))
                dve.tensor_reduce(nmax[:, at:at + 1], chunk_max[:, at, :], AX.X, ALU.max, negate=True).then_inc(max_ready, 1)

            def one_over_sums(h, g):
                for i, t in enumerate(g.tiles):
                    at, tile = t % RING, TILES * h + t
                    dve.wait_ge(exp_done, tile + 1)
                    dve.reciprocal(rinv[:, at:at + 1], rsum[:, at:at + 1]).then_inc(rinv_ready, 1)
                    dve.wait_ge(rinv_ready, tile + 1)
                    dve.tensor_scalar(spread[:, i * P:(i + 1) * P], s.ident[:], rinv[:, at:at + 1], None,
                                      ALU.mult).then_inc(spread_ready, 1)

            def lows(h, g, between):
                wide = g.kts * g.wide
                for c in range(g.chunks):
                    if c == g.chunks - 1 and between is not None:
                        scores_out(*between)
                    dve.wait_ge(t_high, TCHUNKS * h + g.at + c + 1)
                    dve.tensor_tensor(pL[:, c % RING, 0:wide], TB[c % 4][0:KB, 0:wide], pH[:, c % RING, 0:wide].bitcast(F32),
                                      ALU.subtract).then_inc(t_done, 1)

            def outputs(h, g):
                group, n = groups[g], NG * h + g
                part = slice(0, group.wide)
                dve.wait_ge(pv_done, TCHUNKS * h + group.at + group.chunks)
                dve.wait_ge(sums_out, n + 1)
                need(dve, q.o_cut, n)
                dve.tensor_tensor(o[:, part], OB[:, part], over_sums[:, part], ALU.mult).then_inc(q.o_written, 1)

            def mixed(h, g, between):
                one_over_sums(h, groups[g])
                lows(h, groups[g], between)
                outputs(h, g)

            def head(h, last):
                following = h + 1
                scores_out(h, 2)
                mixed(h, 0, (h, 3))
                scores_out(h, 4)
                mixed(h, 1, (h, 5))
                scores_out(h, 6)
                if last:
                    mixed(h, 2, None)
                    return
                use = base(following)
                low_keys(dve, w, q, TB, following)
                low_queries(dve, w, q, TB, following, 1.0)
                mixed(h, 2, (following, 0))
                scores_out(following, 1)
                sum_values(dve, w, q, TB, following, use + HIGHS)
                add_outputs(dve, s, q, TB, use + QKV)

            layer_norm_vector(dve, ln, ql, s.x, xn)
            turn_vector(dve, ql, LNB, s.xnTH, s.xnTL)
            dve.wait_ge(q.bias_loaded, 16)
            dve.tensor_tensor(s.x[:], s.x[:], bias[:].unsqueeze(1).to_broadcast([P, TILES, D]), ALU.add)\
               .then_inc(q.bias_added, 1)
            dve.wait_ge(q.bias_added, 1)
            low_keys(dve, w, q, TB, 0)
            low_queries(dve, w, q, TB, 0, 1.0)
            scores_out(0, 0)
            scores_out(0, 1)
            sum_values(dve, w, q, TB, 0, HIGHS)
            head(0, False)
            with dve.Fori(1, HEADS - 1) as h:
                head(h, False)
            head(HEADS - 1, True)
            add_outputs(dve, s, q, TB, base(HEADS))


def layer1_ffn(nc, s, dram):
    INNER = 1024
    IT = INNER // P
    with ExitStack() as ctx:
        def sb(name, shape, dt=F32):
            return ctx.enter_context(nc.sbuf_tensor(name, shape, dt))

        sem = ctx.enter_context(phase_semaphores(nc))

        xn = sb("f1_xn", [P, TILES, D])
        big = sb("f1_big", [P, TILES, D])
        xq = sb("f1_xq", [P, TILES, D], BF16)
        xqT = sb("f1_xqT", [P, KT, TOK], BF16)
        ident = sb("f1_ident", [P, P], BF16)
        xa = sb("f1_xa", [P, 6, TILES])
        gate = sb("f1_gate", [P, 2, INNER])
        hid = sb("f1_hid", [P, 2, INNER])
        hbig = sb("f1_hbig", [P, 2, INNER])
        hq = sb("f1_hq", [P, 2, INNER], BF16)
        hqT = sb("f1_hqT", [P, 2, IT, P], BF16)
        ha = sb("f1_ha", [P, 4, TILES])
        ln = layer_norm_buffers(sb, "f1_ln")
        ql = layer_norm_semaphores(sem, "f1_ln")
        const_ready, x_step, x_scaled, x_rounded = (sem("f1_const_ready"), sem("f1_x_step"), sem("f1_x_scaled"),
                                                    sem("f1_x_rounded"))
        scales_ready = sem("f1_scales_ready")
        xt_filled, xt_done = sem("f1_xt_filled"), sem("f1_xt_done")
        g_filled, g_done, u_filled, h_done = sem("f1_g_filled"), sem("f1_g_done"), sem("f1_u_filled"), sem("f1_h_done")
        h_step, h_scaled, h_big, h_rounded = sem("f1_h_step"), sem("f1_h_scaled"), sem("f1_h_big"), sem("f1_h_rounded")
        ht_filled, ht_done, y_filled, y_added = (sem("f1_ht_filled"), sem("f1_ht_done"), sem("f1_y_filled"),
                                                 sem("f1_y_added"))
        B = s.banks
        w_gate = s.w_quant[:, 0, :].rearrange("p (k n) -> p k n", k=KT)
        w_up = s.w_quant[:, 1, :].rearrange("p (k n) -> p k n", k=KT)
        w_down = s.w_quant[:, 2, :].rearrange("p (k n) -> p k n", k=IT)
        turned = [B[n][:, :].bitcast(BF16) for n in (4, 5)]
        top, room, scale, inv, inv_gate, inv_up = (xa[:, n, :] for n in range(6))
        block = ctx.enter_context(nc.Block())

        @block.vector
        def _(dve):
            dve.tensor_copy(ident[:], s.ident[:]).then_inc(const_ready, 1)
            layer_norm_vector(dve, ln, ql, s.x, xn)
            dve.wait_ge(ql.normed, TILES)
            dve.tensor_reduce(top, xn[:], AX.X, ALU.max, apply_absolute_value=True).then_inc(x_step, 1)
            dve.wait_ge(x_step, 1)
            dve.tensor_scalar(room, top, EPS, None, ALU.max).then_inc(x_step, 1)
            dve.wait_ge(x_step, 2)
            dve.reciprocal(top, room).then_inc(x_step, 1)
            dve.tensor_scalar(inv, room, 1.0 / 127.0, None, ALU.mult).then_inc(x_step, 1)
            dve.wait_ge(x_step, 4)
            dve.tensor_scalar(scale, top, 127.0, None, ALU.mult).then_inc(x_step, 1)
            dve.wait_ge(x_step, 5)
            for i in range(TILES):
                dve.tensor_scalar(big[:, i, :], xn[:, i, :], scale[:, i:i + 1], MAGIC, ALU.mult, ALU.add)\
                   .then_inc(x_scaled, 1)
                dve.wait_ge(x_scaled, i + 1)
                dve.tensor_scalar(xq[:, i, :], big[:, i, :], MAGIC, 127.0, ALU.subtract, ALU.min)\
                   .then_inc(x_rounded, 1)
            dve.tensor_scalar(inv_gate, inv, s.w_mean[:, 0:1], None, ALU.mult).then_inc(scales_ready, 1)
            dve.tensor_scalar(inv_up, inv, s.w_mean[:, 1:2], None, ALU.mult).then_inc(scales_ready, 1)
            dve.wait_ge(scales_ready, 2)

            def hidden(i):
                for n in range(2):
                    part = slice(n * 512, n * 512 + 512)
                    dve.wait_ge(g_done, 2 * i + n + 1)
                    dve.wait_ge(u_filled, 2 * i + n + 1)
                    dve.scalar_tensor_tensor(hid[:, i % 2, part], B[2 + n][:, :], inv_up[:, i:i + 1],
                                             gate[:, i % 2, part], ALU.mult, ALU.mult).then_inc(h_done, 1)
                dve.wait_ge(h_done, 2 * i + 2)
                dve.tensor_reduce(ha[:, 0, i:i + 1], hid[:, i % 2, :], AX.X, ALU.max,
                                  apply_absolute_value=True).then_inc(h_step, 1)
                dve.wait_ge(h_step, 4 * i + 1)
                dve.tensor_scalar(ha[:, 1, i:i + 1], ha[:, 0, i:i + 1], EPS, None, ALU.max).then_inc(h_step, 1)
                dve.wait_ge(h_step, 4 * i + 2)
                dve.reciprocal(ha[:, 0, i:i + 1], ha[:, 1, i:i + 1]).then_inc(h_step, 1)
                dve.wait_ge(h_step, 4 * i + 3)
                dve.tensor_scalar(ha[:, 2, i:i + 1], ha[:, 0, i:i + 1], 127.0, None, ALU.mult).then_inc(h_scaled, 1)
                dve.tensor_scalar(ha[:, 3, i:i + 1], ha[:, 1, i:i + 1], 1.0 / 127.0, s.w_mean[:, 2:3],
                                  ALU.mult, ALU.mult).then_inc(h_step, 1)

            def rounded(i):
                dve.wait_ge(h_big, i + 1)
                dve.tensor_scalar(hq[:, i % 2, :], hbig[:, i % 2, :], MAGIC, 127.0, ALU.subtract, ALU.min)\
                   .then_inc(h_rounded, 1)

            def into_x(i):
                dve.wait_ge(y_filled, i + 1)
                dve.scalar_tensor_tensor(s.x[:, i, :], B[6 + i % 2][:, 0:D], ha[:, 3, i:i + 1], s.x[:, i, :],
                                         ALU.mult, ALU.add).then_inc(y_added, 1)

            hidden(0)
            for i in range(TILES):
                if i + 1 < TILES:
                    hidden(i + 1)
                rounded(i)
                if i >= 1:
                    into_x(i - 1)
            into_x(TILES - 1)

        @block.scalar
        def _(act):
            layer_norm_scalar(act, ln, ql)
            for i in range(TILES):
                act.wait_ge(xt_filled, i + 1)
                act.activation(xqT[:, :, i * P:(i + 1) * P], turned[i % 2][:, 0:D].rearrange("p (k c) -> p k c", k=KT),
                               ACT.Copy).then_inc(xt_done, 1)
            act.wait_ge(scales_ready, 2)

            def gates(i):
                for n in range(2):
                    act.wait_ge(g_filled, 2 * i + n + 1)
                    act.activation(gate[:, i % 2, n * 512:n * 512 + 512], B[n][:, :], ACT.Silu,
                                   scale=inv_gate[:, i:i + 1]).then_inc(g_done, 1)

            def scaled(i):
                act.wait_ge(h_scaled, i + 1)
                act.activation(hbig[:, i % 2, :], hid[:, i % 2, :], ACT.Copy, scale=ha[:, 2, i:i + 1],
                               bias=MAGIC).then_inc(h_big, 1)

            def turned_out(i):
                act.wait_ge(ht_filled, i + 1)
                act.activation(hqT[:, i % 2, :, :], turned[i % 2].rearrange("p (k c) -> p k c", k=IT),
                               ACT.Copy).then_inc(ht_done, 1)

            gates(0)
            for i in range(TILES):
                if i + 1 < TILES:
                    gates(i + 1)
                scaled(i)
                if i >= 1:
                    turned_out(i - 1)
            turned_out(TILES - 1)

        @block.tensor
        def _(pe):
            pe.wait_ge(const_ready, 1)
            for i in range(TILES):
                pe.wait_ge(x_rounded, i + 1)
                need(pe, xt_done, i - 1)
                for k in range(KT):
                    last = pe.transpose(turned[i % 2][:, k * P:(k + 1) * P], xq[:, i, k * P:(k + 1) * P], ident[:])
                last.then_inc(xt_filled, 1)
            pe.wait_ge(xt_done, TILES)

            def up(i):
                tok = slice(i * P, (i + 1) * P)
                for bank, weights, filled, read in ((0, w_gate, g_filled, g_done), (2, w_up, u_filled, h_done)):
                    for n in range(2):
                        need(pe, read, 2 * (i - 1) + n + 1)
                        split_products(pe, B[bank + n][:, :], [
                            (xqT[:, k, tok], weights[:, k, n * 512:n * 512 + 512]) for k in range(KT)]).then_inc(filled, 1)

            def down(i):
                pe.wait_ge(h_rounded, i + 1)
                need(pe, ht_done, i - 1)
                for k in range(IT):
                    last = pe.transpose(turned[i % 2][:, k * P:(k + 1) * P], hq[:, i % 2, k * P:(k + 1) * P], ident[:])
                last.then_inc(ht_filled, 1)
                pe.wait_ge(ht_done, i + 1)
                need(pe, y_added, i - 1)
                split_products(pe, B[6 + i % 2][:, 0:D], [
                    (hqT[:, i % 2, k, :], w_down[:, k, :]) for k in range(IT)]).then_inc(y_filled, 1)

            up(0)
            for i in range(TILES):
                if i + 1 < TILES:
                    up(i + 1)
                if i >= 1:
                    down(i - 1)
            down(TILES - 1)
def attention_heads64(nc, s, dram, layer, experts=False):
    RING = 4
    AHEAD = 3
    HD = 64
    SCALE = HD ** -0.5
    BKT = KEYS // KB
    PAIR = 2 * SEQ
    EVEN = KEYS + 1

    def first_key(b):
        return min(b * KEYS, NK - EVEN)

    def own_keys(b):
        skip = b * KEYS - first_key(b)
        return slice(skip, skip + KEYS)

    with ExitStack() as ctx:
        def sb(name, shape, dt=F32):
            return ctx.enter_context(nc.sbuf_tensor(f"a{layer}_{name}", shape, dt))

        sem = ctx.enter_context(phase_semaphores(nc, f"a{layer}_"))

        w = HeadBuffers(sb, "head")
        prob = sb("prob", [P, RING, 2 * KEYS])
        xn = prob[:].rearrange("p r k -> p (r k)")[:, 0:TILES * D].rearrange("p (t d) -> p t d", d=D)
        o = sb("o", [P, TOK])
        pH = sb("pH", [KB, 2, BKT, PAIR], F32R)
        pL = sb("pL", [KB, 2, BKT, PAIR], F32R)
        bias = sb("bias", [P, D])
        nmax = sb("nmax", [SEQ, RING, 2])
        rsum = sb("rsum", [SEQ, RING, 2])
        rinv = sb("rinv", [SEQ, RING, 2])
        ln = layer_norm_buffers(sb, "ln")
        ql = layer_norm_semaphores(sem, "ln")
        q = HeadSemaphores(sem, "head")
        s_filled, max_ready, exp_done = sem("s_filled"), sem("max_ready"), sem("exp_done")
        rinv_ready, p_normed = sem("rinv_ready"), sem("p_normed")
        t_filled, t_high, t_done, pv_done = sem("t_filled"), sem("t_high"), sem("t_done"), sem("pv_done")
        expert_loaded = sem("expert_loaded")
        if experts:
            expert = sb("expert", [P, 2 * EXPERTS, D])
        B = s.banks
        SB = [B[0:2], B[2:4]]
        TB = [B[4:6], B[6:8]]
        GB = TB[1]
        KB4 = SB[0] + GB
        OUT = slice(PAIR, 2 * PAIR)
        EXPERT = 1 if experts else 0
        EACH = QKV + GROUPS + EXPERT

        def base(h):
            return 0 if isinstance(h, int) and h == 0 else EACH * h - GROUPS

        def probs(b, i):
            return prob[0:SEQ, b % RING, i * KEYS:(i + 1) * KEYS]

        block = ctx.enter_context(nc.Block())

        @block.sync
        def _(sp):
            sp.dma_start(bias[:], dram[f"a{layer}_bias"]).then_inc(q.bias_loaded, 16)
            head_loads(sp, w, q, dram[f"a{layer}_w"], dram[f"a{layer}_wo"])

        @block.gpsimd
        def _(pool):
            def norm(h, b):
                both = prob[0:SEQ, b % RING, :].rearrange("p (i k) -> p i k", i=2)
                pool.wait_ge(rinv_ready, BATCH * h + b + 1)
                pool.tensor_tensor(both, both, rinv[:, b % RING, :].unsqueeze(2).to_broadcast([SEQ, 2, KEYS]),
                                   ALU.mult).then_inc(p_normed, 1)

            def cut_outputs(h, b):
                tok = slice(b * SEQ, (b + 1) * SEQ)
                n = BATCH * h + b
                pool.wait_ge(q.o_written, n + 1)
                pool.tensor_tensor(w.oH[:, tok], o[:, tok], s.ones[:, 0:SEQ], ALU.mult).then_inc(q.o_high, 1)
                pool.wait_ge(q.o_high, n + 1)
                pool.tensor_tensor(w.oL[:, tok], o[:, tok], w.oH[:, tok].bitcast(F32), ALU.subtract).then_inc(q.o_cut, 1)

            def pair(h, first, last):
                norm(h, 0)
                norm(h, 1)
                if not last:
                    cut_qk(pool, s, w, q, h + 1, base(h) + HIGHS)
                    cut_wv(pool, s, w, q, h + 1, base(h) + QKV)
                norm(h, 2)
                if not first:
                    cut_wo(pool, s, w, q, h, base(h) + QKV + GROUPS)
                for b in range(AHEAD, BATCH):
                    norm(h, b)
                    cut_outputs(h, b - AHEAD)
                for b in range(BATCH - AHEAD, BATCH):
                    cut_outputs(h, b)

            cut_qk(pool, s, w, q, 0, 0)
            cut_wv(pool, s, w, q, 0, 0)
            cut_wo(pool, s, w, q, 0, 0)
            pair(0, True, False)
            with pool.Fori(1, HEADS - 1) as h:
                pair(h, False, False)
            pair(HEADS - 1, False, True)

        @block.tensor
        def _(pe):
            def scores(h, b):
                n = BATCH * h + b
                need(pe, exp_done, n - 1)
                tok, keys = slice(b * SEQ, (b + 1) * SEQ), slice(first_key(b), first_key(b) + EVEN)
                for i in range(2):
                    rows = slice(i * HD, (i + 1) * HD)
                    last = split_products(pe, SB[b % 2][i][0:SEQ, 0:EVEN], [
                        (w.qH[rows, tok], w.kH[rows, keys]), (w.qH[rows, tok], w.kL[rows, keys]),
                        (w.qL[rows, tok], w.kH[rows, keys])])
                last.then_inc(s_filled, 1)

            def turn(h, b):
                n = BATCH * h + b
                pe.wait_ge(p_normed, n + 1)
                need(pe, q.o_written, n - 1)
                for k in range(BKT):
                    for i in range(2):
                        at = (k % 2) * PAIR + i * SEQ
                        last = pe.transpose(TB[b % 2][k // 2][0:KB, at:at + SEQ],
                                            probs(b, i)[:, k * KB:(k + 1) * KB], s.ident[0:SEQ, 0:SEQ])
                last.then_inc(t_filled, 1)

            def mix(h, b):
                pe.wait_ge(t_done, BATCH * h + b + 1)
                terms = []
                for k in range(BKT):
                    t = BKT * b + k
                    terms += [(w.vH[:, t, :], pH[:, b % 2, k, :]), (w.vL[:, t, :], pH[:, b % 2, k, :]),
                              (w.vH[:, t, :], pL[:, b % 2, k, :])]
                split_products(pe, TB[b % 2][1][:, OUT], terms).then_inc(pv_done, 1)

            def combine(h, use):
                pe.wait_ge(expert_loaded, 16 * h + 16)
                pe.wait_ge(q.done, use)
                for j in range(KT):
                    last = split_products(pe, GB[0][:, j * D:(j + 1) * D], [
                        (expert[:, k, j * P:(j + 1) * P], expert[:, EXPERTS + k, :]) for k in range(EXPERTS)])
                last.then_inc(q.filled, 1)

            def pair(h, first):
                use = base(h)
                if not first:
                    turn(h - 1, BATCH - 2)
                    mix(h - 1, BATCH - 3)
                    pe.wait_ge(exp_done, BATCH * h - 1)
                    pe.wait_ge(q.o_written, BATCH * h - 2)
                project_keys(pe, s, w, q, KB4, h, use)
                project_queries(pe, s, w, q, KB4, use)
                if not first:
                    mix(h - 1, BATCH - 2)
                pe.wait_ge(q.done, use + HIGHS)
                scores(h, 0)
                if not first:
                    turn(h - 1, BATCH - 1)
                scores(h, 1)
                if not first:
                    mix(h - 1, BATCH - 1)
                    pe.wait_ge(q.o_written, BATCH * h)
                project_values(pe, s, w, q, GB, h, use + HIGHS)
                use = use + QKV
                if not first:
                    project_outputs(pe, w, q, GB, h - 1, use, BATCH)
                    use = use + GROUPS
                scores(h, 2)
                if experts:
                    combine(h, use)
                    use = use + 1
                turn(h, 0)
                pe.wait_ge(q.done, use)
                pe.wait_ge(q.v_cut, VGROUPS * (h + 1))
                for b in range(BATCH - AHEAD):
                    scores(h, b + AHEAD)
                    turn(h, b + 1)
                    mix(h, b)

            turn_tensor(pe, ql, xn, B[0:4], s.ident[:])
            pe.wait_ge(ql.done, GROUPS)
            pair(0, True)
            with pe.Fori(1, HEADS) as h:
                pair(h, False)
            turn(HEADS - 1, BATCH - 2)
            mix(HEADS - 1, BATCH - 3)
            turn(HEADS - 1, BATCH - 1)
            mix(HEADS - 1, BATCH - 2)
            mix(HEADS - 1, BATCH - 1)
            pe.wait_ge(q.o_written, BATCH * HEADS)
            project_outputs(pe, w, q, GB, HEADS - 1, base(HEADS), BATCH)

        @block.scalar
        def _(act):
            def exps(h, b):
                act.wait_ge(max_ready, BATCH * h + b + 1)
                for i in range(2):
                    last = act.activation(probs(b, i), SB[b % 2][i][0:SEQ, own_keys(b)], ACT.Exp,
                                          bias=nmax[:, b % RING, i:i + 1], accum_out=rsum[:, b % RING, i:i + 1])
                last.then_inc(exp_done, 1)

            def highs(h, b):
                act.wait_ge(t_filled, BATCH * h + b + 1)
                act.activation(pH[:, b % 2, 0:2, :], TB[b % 2][0][0:KB, 0:2 * PAIR].rearrange("p (k c) -> p k c", k=2),
                               ACT.Copy).then_inc(t_high, 1)
                act.activation(pH[:, b % 2, 2, :], TB[b % 2][1][0:KB, 0:PAIR], ACT.Copy).then_inc(t_high, 1)

            def pair(h, first):
                use = base(h)
                if not first:
                    highs(h - 1, BATCH - 2)
                high_keys(act, w, q, KB4, use)
                high_queries(act, w, q, KB4, use, SCALE)
                if not first:
                    highs(h - 1, BATCH - 1)
                exps(h, 0)
                exps(h, 1)
                high_values(act, w, q, use + HIGHS)
                exps(h, 2)
                highs(h, 0)
                for b in range(BATCH - AHEAD):
                    highs(h, b + 1)
                    exps(h, b + AHEAD)

            if experts:
                act.dma_start(expert[:], dram["f2_w"][0]).then_inc(expert_loaded, 16)
            layer_norm_scalar(act, ln, ql)
            turn_scalar(act, ql, B[0:4], s.xnTH)
            pair(0, True)
            with act.Fori(1, HEADS) as h:
                if experts:
                    act.wait_ge(q.filled, base(h))
                    act.dma_start(expert[:], dram["f2_w"][bass.ds(h, 1)].rearrange("o p t c -> p (o t) c"))\
                       .then_inc(expert_loaded, 16)
                pair(h, False)
            highs(HEADS - 1, BATCH - 2)
            highs(HEADS - 1, BATCH - 1)

        @block.vector
        def _(dve):
            def maxima(h, b):
                dve.wait_ge(s_filled, BATCH * h + b + 1)
                for i in range(2):
                    last = dve.tensor_reduce(nmax[:, b % RING, i:i + 1], SB[b % 2][i][0:SEQ, own_keys(b)], AX.X, ALU.max, negate=True)
                last.then_inc(max_ready, 1)

            def one_over_sums(h, b):
                dve.wait_ge(exp_done, BATCH * h + b + 1)
                dve.reciprocal(rinv[:, b % RING, :], rsum[:, b % RING, :]).then_inc(rinv_ready, 1)

            def lows(h, b):
                n = 2 * (BATCH * h + b)
                dve.wait_ge(t_high, n + 1)
                dve.tensor_tensor(pL[:, b % 2, 0:2, :], TB[b % 2][0][0:KB, 0:2 * PAIR].rearrange("p (k c) -> p k c", k=2),
                                  pH[:, b % 2, 0:2, :].bitcast(F32), ALU.subtract)
                dve.wait_ge(t_high, n + 2)
                dve.tensor_tensor(pL[:, b % 2, 2, :], TB[b % 2][1][0:KB, 0:PAIR], pH[:, b % 2, 2, :].bitcast(F32),
                                  ALU.subtract).then_inc(t_done, 1)

            def outputs(h, b):
                tok = slice(b * SEQ, (b + 1) * SEQ)
                dve.wait_ge(pv_done, BATCH * h + b + 1)
                for i in range(2):
                    rows = slice(i * HD, (i + 1) * HD)
                    last = dve.tensor_copy(o[rows, tok], TB[b % 2][1][rows, PAIR + i * SEQ:PAIR + (i + 1) * SEQ])
                last.then_inc(q.o_written, 1)

            def pair(h, first):
                use = base(h)
                if not first:
                    lows(h - 1, BATCH - 2)
                    outputs(h - 1, BATCH - 3)
                low_keys(dve, w, q, KB4, h)
                low_queries(dve, w, q, KB4, h, SCALE)
                if not first:
                    outputs(h - 1, BATCH - 2)
                maxima(h, 0)
                if not first:
                    lows(h - 1, BATCH - 1)
                maxima(h, 1)
                one_over_sums(h, 0)
                if not first:
                    outputs(h - 1, BATCH - 1)
                one_over_sums(h, 1)
                sum_values(dve, w, q, GB, h, use + HIGHS)
                use = use + QKV
                if not first:
                    add_outputs(dve, s, q, GB, use)
                    use = use + GROUPS
                maxima(h, 2)
                if experts:
                    dve.wait_ge(q.filled, use + 1)
                    dve.tensor_copy(s.combined[:, h:h + 1, :] if first else s.combined[:, bass.ds(h, 1), :],
                                    GB[0][:, :].unsqueeze(1)).then_inc(q.done, 1)
                lows(h, 0)
                one_over_sums(h, 2)
                for b in range(BATCH - AHEAD):
                    maxima(h, b + AHEAD)
                    lows(h, b + 1)
                    outputs(h, b)
                    one_over_sums(h, b + AHEAD)

            layer_norm_vector(dve, ln, ql, s.x, xn)
            turn_vector(dve, ql, B[0:4], s.xnTH, s.xnTL)
            dve.wait_ge(q.bias_loaded, 16)
            dve.tensor_tensor(s.x[:], s.x[:], bias[:].unsqueeze(1).to_broadcast([P, TILES, D]), ALU.add)\
               .then_inc(q.bias_added, 1)
            dve.wait_ge(q.bias_added, 1)
            pair(0, True)
            with dve.Fori(1, HEADS) as h:
                pair(h, False)
            lows(HEADS - 1, BATCH - 2)
            outputs(HEADS - 1, BATCH - 3)
            lows(HEADS - 1, BATCH - 1)
            outputs(HEADS - 1, BATCH - 2)
            outputs(HEADS - 1, BATCH - 1)
            add_outputs(dve, s, q, GB, base(HEADS))


def layer2_ffn(nc, s, dram):
    PAIRS = EXPERTS // 2
    with ExitStack() as ctx:
        def sb(name, shape, dt=F32):
            return ctx.enter_context(nc.sbuf_tensor(f"f2_{name}", shape, dt))

        sem = ctx.enter_context(phase_semaphores(nc, "f2_"))
        xn = sb("xn", [P, TILES, D])
        cH = sb("cH", [P, KT, PAIRS, 2 * D], F32R)
        cL = sb("cL", [P, KT, PAIRS, 2 * D], F32R)
        gates = sb("gates", [P, PAIRS, 2, TILES])
        ln = layer_norm_buffers(sb, "ln")
        r = router_buffers(sb, "r")
        ql = layer_norm_semaphores(sem, "ln")
        q = router_semaphores(sem, "r")
        c_high, c_cut = sem("c_high"), sem("c_cut")
        y_filled, first_added, x_added = sem("y_filled"), sem("first_added"), sem("x_added")
        B = s.banks
        block = ctx.enter_context(nc.Block())

        @block.sync
        def _(sp):
            sp.dma_start(r.raw[:], dram["f2_gate"]).then_inc(q.loaded, 16)

        @block.gpsimd
        def _(pool):
            router_cut(pool, r, q)
            for e in range(EXPERTS):
                whole = s.combined[:, e, :].rearrange("p (k d) -> p k d", k=KT)
                mine = slice((e % 2) * D, (e % 2) * D + D)
                pool.tensor_copy(cH[:, :, e // 2, mine], whole).then_inc(c_high, 1)
                pool.wait_ge(c_high, e + 1)
                pool.tensor_tensor(cL[:, :, e // 2, mine], whole, cH[:, :, e // 2, mine].bitcast(F32),
                                   ALU.subtract).then_inc(c_cut, 1)

        @block.vector
        def _(dve):
            def add_pair(p):
                for i in range(TILES):
                    n = TILES * p + i
                    dve.wait_ge(y_filled, n + 1)
                    for j in range(2):
                        gate = gates[:, p:p + 1, j, i:i + 1] if isinstance(p, int) else gates[:, bass.ds(p, 1), j, i:i + 1]
                        if j == 1:
                            dve.wait_ge(first_added, n + 1)
                        dve.scalar_tensor_tensor(s.x[:, i, :], B[i][:, j * D:(j + 1) * D], gate.rearrange("p a b -> p (a b)"),
                                                 s.x[:, i, :], ALU.mult, ALU.add).then_inc(x_added if j else first_added, 1)

            layer_norm_vector(dve, ln, ql, s.x, xn)
            turn_vector(dve, ql, B[3:7], s.xnTH, s.xnTL)
            at = router_exps(dve, r, q, B[7])
            at = router_ranks(dve, s, r, q, r.logits[:], at)
            dve.wait_ge(q.exps, 1)
            router_keep_two(dve, r, q, at, r.exps[:], gates[:].rearrange("p a b t -> p t (a b)"), 0.0)
            dve.wait_ge(q.kept, 1)
            add_pair(0)
            with dve.Fori(1, PAIRS) as p:
                add_pair(p)

        @block.scalar
        def _(act):
            layer_norm_scalar(act, ln, ql)
            turn_scalar(act, ql, B[3:7], s.xnTH)
            router_scalar(act, r, q)

        @block.tensor
        def _(pe):
            def two_experts(p):
                pe.wait_ge(c_cut, 2 * p + 2)
                here = slice(p, p + 1) if isinstance(p, int) else bass.ds(p, 1)
                for i in range(TILES):
                    tok = slice(i * P, (i + 1) * P)
                    need(pe, x_added, TILES * (p - 1) + i + 1)
                    split_products(pe, B[i][:, :], [
                        pair for k in range(KT) for pair in (
                            (s.xnTH[:, k, tok], cH[:, k, here, :].rearrange("p a d -> p (a d)")),
                            (s.xnTH[:, k, tok], cL[:, k, here, :].rearrange("p a d -> p (a d)")),
                            (s.xnTL[:, k, tok], cH[:, k, here, :].rearrange("p a d -> p (a d)")))]).then_inc(y_filled, 1)

            turn_tensor(pe, ql, xn, B[3:7], s.ident[:])
            pe.wait_ge(ql.done, GROUPS)
            router_tensor(pe, s, r, q, B[7])
            two_experts(0)
            with pe.Fori(1, PAIRS) as p:
                two_experts(p)


def layer3_ffn(nc, s, dram, out):
    ALL = EXPERTS + 1
    WIDE = KT * D
    HALF = TOK // 2
    with ExitStack() as ctx:
        def sb(name, shape, dt=F32):
            return ctx.enter_context(nc.sbuf_tensor(f"f3_{name}", shape, dt))

        sem = ctx.enter_context(phase_semaphores(nc, "f3_"))
        xn = sb("xn", [P, TILES, D])
        raw = [sb(f"raw{n}", [P, 2 * WIDE + KT]) for n in range(2)]
        uH = [sb(f"u{n}H", [P, KT, D], F32R) for n in range(2)]
        uL = [sb(f"u{n}L", [P, KT, D], F32R) for n in range(2)]
        dH = [sb(f"d{n}H", [P, KT, D], F32R) for n in range(2)]
        dL = [sb(f"d{n}L", [P, KT, D], F32R) for n in range(2)]
        hid = sb("hid", [P, 2, HALF])
        hH = [sb(f"h{n}H", [P, KT, TOK], F32R) for n in range(2)]
        hL = [sb(f"h{n}L", [P, KT, TOK], F32R) for n in range(2)]
        comb = sb("comb", [P, ALL, TILES])
        combT = sb("combT", [ALL, TOK])
        down_b = sb("down_b", [ALL, D])
        ln = layer_norm_buffers(sb, "ln")
        r = router_buffers(sb, "r")
        ql = layer_norm_semaphores(sem, "ln")
        q = router_semaphores(sem, "r")
        w_loaded = [sem(f"w_loaded{n}") for n in range(2)]
        down_b_loaded, shared_set = sem("down_b_loaded"), sem("shared_set")
        w_high, w_cut = sem("w_high"), sem("w_cut")
        up_filled, silu_done, h_high, h_cut = sem("up_filled"), sem("silu_done"), sem("h_high"), sem("h_cut")
        y_filled, x_added = sem("y_filled"), sem("x_added")
        c_turned, c_out, b_filled, b_added = sem("c_turned"), sem("c_out"), sem("b_filled"), sem("b_added")
        B = s.banks
        UB, YB = B[0:4], B[4:8]
        UPS = KT * 2
        block = ctx.enter_context(nc.Block())

        def one(e):
            return slice(e, e + 1) if isinstance(e, int) else bass.ds(e, 1)

        @block.sync
        def _(sp):
            sp.dma_start(r.raw[:], dram["f3_gate"]).then_inc(q.loaded, 16)
            for e in range(2):
                sp.dma_start(raw[e][:], dram["f3_w"][e]).then_inc(w_loaded[e], 16)
            sp.dma_start(down_b[:], dram["f3_down_b"]).then_inc(down_b_loaded, 16)

            def load(e, n):
                sp.wait_ge(w_cut, 2 * e - 2)
                sp.wait_ge(silu_done, UPS * e - UPS)
                source = dram["f3_w"][e] if isinstance(e, int) else dram["f3_w"][bass.ds(e, 1)].rearrange("a p c -> p (a c)")
                sp.dma_start(raw[n][:], source).then_inc(w_loaded[n], 16)

            load(2, 0)
            with sp.Fori(2, EXPERTS // 2 + 1) as pair:
                load(2 * pair - 1, 1)
                load(2 * pair, 0)
            for i in range(TILES):
                sp.wait_ge(x_added, TILES * (ALL - 1) + i + 1)
                sp.dma_start(out[i * P:(i + 1) * P, :], s.x[:, i, :]).then_inc(s.stored, 16)
            sp.wait_ge(s.stored, 16 * TILES)

        @block.gpsimd
        def _(pool):
            def cut(e, n):
                pool.wait_ge(w_loaded[n], 8 * (e - n) + 16)
                need(pool, y_filled, TILES * (e - 1))
                for at, (high, low) in enumerate(((uH[n], uL[n]), (dH[n], dL[n]))):
                    whole = raw[n][:, at * WIDE:(at + 1) * WIDE].rearrange("p (k d) -> p k d", k=KT)
                    step = 2 * e + at + 1
                    pool.tensor_tensor(high[:], whole, s.ones[:, 0:1].unsqueeze(2).to_broadcast([P, KT, D]),
                                       ALU.mult).then_inc(w_high, 1)
                    pool.wait_ge(w_high, step)
                    pool.tensor_tensor(low[:], whole, high[:].bitcast(F32), ALU.subtract).then_inc(w_cut, 1)

            router_cut(pool, r, q)
            pool.tensor_copy(comb[:, EXPERTS, :], s.ones[:, 0:TILES]).then_inc(shared_set, 1)
            cut(0, 0)
            cut(1, 1)
            cut(2, 0)
            with pool.Fori(2, EXPERTS // 2 + 1) as pair:
                cut(2 * pair - 1, 1)
                cut(2 * pair, 0)

        @block.tensor
        def _(pe):
            def up(e, n):
                pe.wait_ge(w_cut, 2 * e + 1)
                for u in range(UPS):
                    j, half = u // 2, HALVES[u % 2]
                    cols = slice(j * P, (j + 1) * P)
                    need(pe, silu_done, UPS * (e - 1) + u + 1)
                    split_products(pe, UB[u][:, 0:HALF], [
                        pair for k in range(KT) for pair in (
                            (uH[n][:, k, cols], s.xnTH[:, k, half]), (uH[n][:, k, cols], s.xnTL[:, k, half]),
                            (uL[n][:, k, cols], s.xnTH[:, k, half]))]).then_inc(up_filled, 1)

            def down(e, n, last=False):
                pe.wait_ge(h_cut, UPS * (e + 1))
                pe.wait_ge(w_cut, 2 * e + 2)
                for i in range(TILES):
                    tok = slice(i * P, (i + 1) * P)
                    before = i - 4 if i >= 4 else (i + 4 if i + 4 < TILES else i) - TILES
                    need(pe, x_added, TILES * e + before + 1)
                    if isinstance(e, int) and e == 0 and i in (2, 3):
                        pe.wait_ge(c_out, i - 1)
                    terms = [pair for k in range(KT) for pair in (
                        (hH[n][:, k, tok], dH[n][:, k, :]), (hH[n][:, k, tok], dL[n][:, k, :]),
                        (hL[n][:, k, tok], dH[n][:, k, :]))]
                    if last:
                        terms += [(combT[:, tok], down_b[:])]
                    split_products(pe, YB[i % 4][:, 0:D], terms).then_inc(y_filled, 1)

            turn_tensor(pe, ql, xn, B[0:4], s.ident[:])
            pe.wait_ge(ql.done, GROUPS)
            router_tensor(pe, s, r, q, B[7])
            up(0, 0)
            pe.wait_ge(q.kept, 1)
            pe.wait_ge(shared_set, 1)
            for i in range(TILES):
                last = pe.transpose(YB[2 + i // 4][0:ALL, (i % 4) * P:(i % 4 + 1) * P], comb[:, :, i], s.ident[:])
                if i in (3, TILES - 1):
                    last.then_inc(c_turned, 1)
            up(1, 1)
            down(0, 0)
            up(2, 0)
            down(1, 1)
            with pe.Fori(2, EXPERTS // 2 + 1) as pair:
                up(2 * pair - 1, 1)
                down(2 * pair - 2, 0)
                up(2 * pair, 0)
                down(2 * pair - 1, 1)
            pe.wait_ge(down_b_loaded, 16)
            down(EXPERTS, 0, True)

        @block.scalar
        def _(act):
            def hidden(e, n):
                act.wait_ge(w_loaded[n], 8 * (e - n) + 16)
                for u in range(UPS):
                    step = UPS * e + u
                    act.wait_ge(up_filled, step + 1)
                    need(act, h_cut, step - 1)
                    col = raw[n][:, 2 * WIDE + u // 2:2 * WIDE + u // 2 + 1]
                    act.activation(hid[:, u % 2, :], UB[u][:, 0:HALF], ACT.Silu, bias=col).then_inc(silu_done, 1)

            layer_norm_scalar(act, ln, ql)
            turn_scalar(act, ql, B[0:4], s.xnTH)
            router_scalar(act, r, q)
            hidden(0, 0)
            for n in range(2):
                cols = slice(4 * P * n, min(4 * P * (n + 1), TOK))
                act.wait_ge(c_turned, n + 1)
                act.activation(combT[:, cols], YB[2 + n][0:ALL, 0:cols.stop - cols.start], ACT.Copy).then_inc(c_out, 1)
            hidden(1, 1)
            hidden(2, 0)
            with act.Fori(2, EXPERTS // 2 + 1) as pair:
                hidden(2 * pair - 1, 1)
                hidden(2 * pair, 0)

        @block.vector
        def _(dve):
            def cut_hidden(e, n):
                for u in range(UPS):
                    step = UPS * e + u
                    at = (slice(None), u // 2, HALVES[u % 2])
                    dve.wait_ge(silu_done, step + 1)
                    dve.tensor_copy(hH[n][at], hid[:, u % 2, :]).then_inc(h_high, 1)
                    dve.wait_ge(h_high, step + 1)
                    dve.tensor_tensor(hL[n][at], hid[:, u % 2, :], hH[n][at].bitcast(F32), ALU.subtract).then_inc(h_cut, 1)

            def add(e):
                for i in range(TILES):
                    n = TILES * e + i
                    col = comb[:, one(e), i:i + 1].rearrange("p a b -> p (a b)")
                    dve.wait_ge(y_filled, n + 1)
                    need(dve, x_added, n - TILES + 1)
                    dve.scalar_tensor_tensor(s.x[:, i, :], YB[i % 4][:, 0:D], col, s.x[:, i, :],
                                             ALU.mult, ALU.add).then_inc(x_added, 1)

            layer_norm_vector(dve, ln, ql, s.x, xn)
            turn_vector(dve, ql, B[0:4], s.xnTH, s.xnTL)
            at = router_exps(dve, r, q, B[7])
            at = router_softmax(dve, r, q, at)
            at = router_ranks(dve, s, r, q, r.probs[:], at)
            router_keep_two(dve, r, q, at, r.probs[:], comb[:, 0:EXPERTS, :].rearrange("p e t -> p t e"), 1e-20)
            dve.wait_ge(q.kept, 1)
            dve.wait_ge(shared_set, 1)
            cut_hidden(0, 0)
            cut_hidden(1, 1)
            add(0)
            cut_hidden(2, 0)
            add(1)
            with dve.Fori(2, EXPERTS // 2 + 1) as pair:
                cut_hidden(2 * pair - 1, 1)
                add(2 * pair - 2)
                cut_hidden(2 * pair, 0)
                add(2 * pair - 1)
            add(EXPERTS)


def build(nc, dram, out):
    with ExitStack() as ctx:
        s = Names()
        s.x = ctx.enter_context(nc.sbuf_tensor("x_stream", [P, TILES, D], F32))
        s.ident = ctx.enter_context(nc.sbuf_tensor("ident", [P, P], F32))
        s.ones = ctx.enter_context(nc.sbuf_tensor("ones", [P, P], F32))
        s.earlier = ctx.enter_context(nc.sbuf_tensor("earlier", [P, EXPERTS, EXPERTS], F32))
        s.ctxH = ctx.enter_context(nc.sbuf_tensor("ctxH", [P, NK], F32R))
        s.ctxL = ctx.enter_context(nc.sbuf_tensor("ctxL", [P, NK], F32R))
        s.ctxT = ctx.enter_context(nc.sbuf_tensor("ctxT", [P, NK], F32R))
        s.banks = [ctx.enter_context(nc.psum_tensor(f"bank{n}", [P, 512], F32)) for n in range(8)]
        s.stored = ctx.enter_context(nc.semaphore("stored"))
        layer0_attention(nc, s, dram)
        s.xnTH = ctx.enter_context(nc.sbuf_tensor("xnTH", [P, KT, TOK], F32R))
        s.xnTL = ctx.enter_context(nc.sbuf_tensor("xnTL", [P, KT, TOK], F32R))
        with ExitStack() as quantised:
            s.w_quant = quantised.enter_context(nc.sbuf_tensor("w_quant", [P, 3, 2048], BF16))
            s.w_mean = quantised.enter_context(nc.sbuf_tensor("w_mean", [P, 3], F32))
            layer0_ffn(nc, s, dram)
            layer1_attention(nc, s, dram)
            layer1_ffn(nc, s, dram)
        with ExitStack() as combined:
            s.combined = combined.enter_context(nc.sbuf_tensor("combined", [P, EXPERTS, KT * D], F32))
            attention_heads64(nc, s, dram, 2, experts=True)
            layer2_ffn(nc, s, dram)
        attention_heads64(nc, s, dram, 3)
        layer3_ffn(nc, s, dram, out)


def tiled(np, w):
    return w.reshape(-1, P, w.shape[1]).transpose(1, 0, 2)


def attention_weights(np, wq, wk, wv):
    packs = []
    for h in range(HEADS):
        c = slice(h * P, (h + 1) * P)
        parts = [wq[0:P, c], wq[P:D, c]]
        for w in (wk, wv):
            parts += [w[0:P, c], np.concatenate([w[P:DC, c], w[P:DC, c]], axis=0)]
        packs.append(np.stack(parts, axis=1))
    return np.stack(packs, axis=0)


def repeated(np, row, rows=P):
    return np.broadcast_to(row, (rows,) + row.shape)


def laid_out(np, i):
    zeros = np.zeros(TAIL, np.float32)

    def column_pair(v):
        return [v[0:P], np.concatenate([v[P:], zeros]) if v.shape[0] == DC else v[P:]]

    a = {"x": i["x"].reshape(TOK, D)}
    rows = i["ctx_768"].reshape(NK, DC)
    a["ctx_rows"], a["ctx_cols"] = rows, rows.T
    a["ident"] = np.eye(P, dtype=np.float32)
    a["ones"] = np.ones((P, P), np.float32)
    a["earlier"] = repeated(np, np.tril(np.ones((EXPERTS, EXPERTS), np.float32), -1))
    a["a0_cols"] = np.stack([c for n in ("ln1_g", "ln1_b", "ln2_g", "ln2_b", "bq", "bk")
                             for c in column_pair(i["L0_xattn_" + n])], axis=1)
    a["a0_rows"] = repeated(np, np.stack([i["L0_xattn_bv"], i["L0_xattn_bo"]]))
    for n in "qkvo":
        a["a0_w" + n] = i["L0_xattn_W" + n]
    a["f0_gate"] = tiled(np, i["L0_ffn_gate_w"])
    a["f0_w"] = tiled(np, np.concatenate([i["L0_ffn_w0"].T, i["L0_ffn_w1"].T], axis=1))
    a["f0_bias"] = repeated(np, np.concatenate([i["L0_ffn_b0"], i["L0_ffn_b1"]]))
    a["f1_w"] = np.stack([tiled(np, i["L1_ffn_" + n].T).reshape(P, 2048) for n in ("w_gate", "w_up", "w_down")], axis=1)
    for l, o, b in ((1, "Wout", "bout"), (2, "Wo", "bo"), (3, "Wo", "bo")):
        p = f"L{l}_xattn_"
        a[f"a{l}_w"] = attention_weights(np, i[p + "Wq"], i[p + "Wk"], i[p + "Wv"])
        a[f"a{l}_wo"] = i[p + o].reshape(HEADS, P, D)
        a[f"a{l}_bias"] = repeated(np, i[p + b])
    a["f2_gate"] = tiled(np, i["L2_ffn_w_gate"].T)
    a["f2_w"] = np.stack([np.concatenate([tiled(np, i["L2_ffn_w_in"][e]), tiled(np, i["L2_ffn_w_out"][e].T)], axis=1)
                          for e in range(EXPERTS)])
    a["f3_gate"] = tiled(np, i["L3_ffn_gate_w"].T)
    up = [*i["L3_ffn_up_w"], i["L3_ffn_sh_up_w"]]
    down = [*i["L3_ffn_down_w"], i["L3_ffn_sh_down_w"]]
    up_b = [*i["L3_ffn_up_b"], i["L3_ffn_sh_up_b"]]
    a["f3_w"] = np.stack([np.concatenate([tiled(np, u).reshape(P, -1), tiled(np, d).reshape(P, -1), b.reshape(KT, P).T], axis=1)
                          for u, d, b in zip(up, down, up_b)])
    a["f3_down_b"] = np.concatenate([i["L3_ffn_down_b"], i["L3_ffn_sh_down_b"][None]], axis=0)
    return {n: np.ascontiguousarray(v) for n, v in a.items()}


def kernel(**inputs):
    import numpy as np
    import concourse.bacc as bacc
    from concourse.bass_utils import run_bass_kernel_spmd

    nc = bacc.Bacc("TRN2", target_bir_lowering=False, num_devices=1)
    arrays = laid_out(np, {n: np.asarray(v) for n, v in inputs.items()})
    dram = {n: nc.dram_tensor(f"in_{n}", v.shape, mybir.dt.from_np(v.dtype), kind="ExternalInput").ap()
            for n, v in arrays.items()}
    out = nc.dram_tensor("out_x", (TOK, D), F32, kind="ExternalOutput").ap()
    build(nc, dram, out)
    result = run_bass_kernel_spmd(nc, [{f"in_{n}": v for n, v in arrays.items()}], core_ids=[0])
    return result.results[0]["out_x"].reshape(BATCH, SEQ, D)
```

```python
from contextlib import ExitStack, contextmanager

import concourse.bass as bass
from concourse import mybir

F32 = mybir.dt.float32
F32R = mybir.dt.float32r
BF16 = mybir.dt.bfloat16
ALU = mybir.AluOpType
ACT = mybir.ActivationFunctionType
AX = mybir.AxisListType

P = 128
BATCH, SEQ, D = 8, 112, 256
KEYS, DC = 375, 192
TOK = BATCH * SEQ
TILES = TOK // P
KT = D // P
NK = BATCH * KEYS
KB = 125
KTILES = NK // KB
TAIL = DC - P
CHUNK = 500
CHUNKS = NK // CHUNK
GROUPS = (TILES + 1) // 2
HEADS = 8
EPS = 1e-5
EXPERTS = 8
MAGIC = 1.5 * 2.0 ** 23


def need(eng, semaphore, value):
    if not (isinstance(value, int) and value <= 0):
        eng.wait_ge(semaphore, value)


@contextmanager
def phase_semaphores(nc, prefix=""):
    taken = []

    def sem(name):
        taken.append(nc.alloc_semaphore(name=prefix + name))
        return taken[-1]

    yield sem
    nc.clear_and_free_semaphores(taken)
    nc.all_engine_barrier()


class Names:
    pass


def layer_norm_buffers(sb, tag, width=TILES, rows=P):
    b = Names()
    b.stats = sb(f"{tag}_stats", [rows, width, 6])
    b.mean_var = sb(f"{tag}_mean_var", [rows, width, 2])
    b.root = sb(f"{tag}_root", [rows, 6, width])
    return b


def layer_norm_semaphores(sem, tag):
    q = Names()
    q.stats = sem(f"{tag}_stats_done")
    q.aggr = sem(f"{tag}_aggr_done")
    q.var = sem(f"{tag}_var_ready")
    q.std = sem(f"{tag}_std_ready")
    q.newton = sem(f"{tag}_newton_step")
    q.normed = sem(f"{tag}_normed")
    q.turned = sem(f"{tag}_turned")
    q.high = sem(f"{tag}_high_done")
    q.done = sem(f"{tag}_low_done")
    return q


def layer_norm_roots(dve, b, q, src, width=TILES, ready=None):
    for i in range(width):
        if ready is not None:
            dve.wait_ge(*ready(i))
        dve.bn_stats(b.stats[:, i, :], src[:, i, :]).then_inc(q.stats, 1)
    dve.wait_ge(q.stats, width)
    for i in range(width):
        dve.bn_aggr(b.mean_var[:, i, :], b.stats[:, i, :]).then_inc(q.aggr, 1)
    dve.wait_ge(q.aggr, width)
    var, std, y0, t, u, y = (b.root[:, k, :] for k in range(6))
    dve.tensor_scalar(var, b.mean_var[:, :, 1], EPS, None, ALU.add).then_inc(q.var, 1)
    dve.wait_ge(q.std, 1)
    dve.reciprocal(y0, std).then_inc(q.newton, 1)
    dve.wait_ge(q.newton, 1)
    dve.tensor_tensor(t, y0, y0, ALU.mult).then_inc(q.newton, 1)
    dve.wait_ge(q.newton, 2)
    dve.scalar_tensor_tensor(u, t, -0.5, var, ALU.mult, ALU.mult).then_inc(q.newton, 1)
    dve.wait_ge(q.newton, 3)
    dve.scalar_tensor_tensor(y, u, 1.5, y0, ALU.add, ALU.mult).then_inc(q.newton, 1)


def layer_norm_apply(eng, b, q, src, dst, tiles=range(TILES)):
    eng.wait_ge(q.newton, 4)
    for i in tiles:
        eng.tensor_scalar(dst[:, i, :], src[:, i, :], b.mean_var[:, i, 0:1], b.root[:, 5, i:i + 1],
                          ALU.subtract, ALU.mult).then_inc(q.normed, 1)


def layer_norm_vector(dve, b, q, src, dst):
    layer_norm_roots(dve, b, q, src)
    layer_norm_apply(dve, b, q, src, dst)


def layer_norm_scalar(act, b, q):
    act.wait_ge(q.var, 1)
    act.activation(b.root[:, 1, :], b.root[:, 0, :], ACT.Sqrt).then_inc(q.std, 1)


def turn_tensor(pe, q, src, banks, ident):
    for g in range(GROUPS):
        tiles = range(2 * g, min(2 * g + 2, TILES))
        pe.wait_ge(q.normed, tiles[-1] + 1)
        for i in tiles:
            for k in range(KT):
                at = k * 2 * P + (i % 2) * P
                last = pe.transpose(banks[g][:, at:at + P], src[:, i, k * P:(k + 1) * P], ident)
        last.then_inc(q.turned, 1)


def turned_view(bank, g):
    width = min(2 * P, TOK - g * 2 * P)
    return bank[:, :].rearrange("p (k c) -> p k c", k=KT)[:, :, 0:width], slice(g * 2 * P, g * 2 * P + width)


def turn_scalar(act, q, banks, TH):
    for g in range(GROUPS):
        view, cols = turned_view(banks[g], g)
        act.wait_ge(q.turned, g + 1)
        act.activation(TH[:, :, cols], view, ACT.Copy).then_inc(q.high, 1)


def turn_vector(dve, q, banks, TH, TL):
    for g in range(GROUPS):
        view, cols = turned_view(banks[g], g)
        dve.wait_ge(q.high, g + 1)
        dve.tensor_tensor(TL[:, :, cols], view, TH[:, :, cols].bitcast(F32), ALU.subtract).then_inc(q.done, 1)


def load_table(act, s, function):
    act.activation(s.primed[:], s.ones[:, 0:1], function)


def split_products(pe, out, terms, start=True, stop=True):
    for n, (a, b) in enumerate(terms):
        last = pe.matmul(out, a, b, start=start and n == 0, stop=stop and n == len(terms) - 1)
    return last


def layer0_attention(nc, s, dram):
    AHEAD = 2
    with ExitStack() as ctx:
        def sb(name, shape, dt=F32):
            return ctx.enter_context(nc.sbuf_tensor(name, shape, dt))

        sem = ctx.enter_context(phase_semaphores(nc))

        v = sb("a0_v", [KB, KTILES, D])
        ctx_rows = v[:, :, 0:DC]
        raw_main = sb("a0_raw_main", [P, NK])
        raw_tail = sb("a0_raw_tail", [P, NK])
        cH = sb("a0_cH", [P, NK], F32R)
        cL = sb("a0_cL", [P, NK], F32R)
        cT = sb("a0_cT", [P, NK], F32R)
        kT = sb("a0_kT", [P, KT, NK])
        xa = sb("a0_xa", [P, TILES, D])
        xT = sb("a0_xT", [P, KT, TOK])
        qT = sb("a0_qT", [P, KT, TOK])
        wkv = sb("a0_wkv", [P, 2, 2, D])
        wkvH = sb("a0_wkvH", [P, 2, 2, D], F32R)
        wkvL = sb("a0_wkvL", [P, 2, 2, D], F32R)
        kv_bias = sb("a0_kv_bias", [P, 2 * KT])
        w_q = sb("a0_w_q", [P, KT, D])
        w_o = sb("a0_w_o", [P, KT, D])
        cols = sb("a0_cols", [P, 14])
        rows = sb("a0_rows", [P, D])
        prob = sb("a0_prob", [SEQ, AHEAD + 1, KEYS])
        pT = sb("a0_pT", [KB, 2, 3, SEQ])
        nmax = sb("a0_nmax", [SEQ, AHEAD + 1])
        rsum = sb("a0_rsum", [SEQ, AHEAD + 1])
        rinv = sb("a0_rinv", [SEQ, AHEAD + 1])
        tail_high = sb("a0_tail_high", [P, NK // 2], F32R)
        oT = xT
        ln_c = layer_norm_buffers(sb, "a0_ln_c", KTILES, KB)
        ln_x = layer_norm_buffers(sb, "a0_ln_x")
        ln_y = layer_norm_buffers(sb, "a0_ln_y")
        qc = layer_norm_semaphores(sem, "a0_lc")
        qx = layer_norm_semaphores(sem, "a0_lx")
        qy = layer_norm_semaphores(sem, "a0_ly")
        g1, b1 = cols[:, 0:2], cols[:, 2:4]
        g2, b2 = cols[:, 4:6], cols[:, 6:8]
        bq, bkv = cols[:, 8:10], cols[:, 10:14]
        bk, bv = kv_bias[:, 0:KT], kv_bias[:, KT:]

        LOADS = 4
        PER = KTILES // LOADS
        ctx_loaded = [sem(f"a0_ctx_loaded{n}") for n in range(LOADS)]
        x_loaded = sem("a0_x_loaded")
        small_loaded = sem("a0_small_loaded")
        w_loaded = sem("a0_w_loaded")
        raw_loaded = sem("a0_raw_loaded")
        wkv_loaded, kv_bias_filled, kv_bias_ready = sem("a0_wkv_loaded"), sem("a0_kv_bias_filled"), sem("a0_kv_bias_ready")
        w_scaled, w_high, w_cut = sem("a0_w_scaled"), sem("a0_w_high"), sem("a0_w_cut")
        c_turned, c_high, c_cut = sem("a0_c_turned"), sem("a0_c_high"), sem("a0_c_cut")
        k_filled, k_done = sem("a0_k_filled"), sem("a0_k_done")
        v_filled, v_done = sem("a0_v_filled"), sem("a0_v_done")
        q_filled, q_done = sem("a0_q_filled"), sem("a0_q_done")
        xT_first, xT_done = sem("a0_xT_first"), sem("a0_xT_done")
        s_filled, max_ready, exp_done, p_normed = (sem("a0_s_filled"), sem("a0_max_ready"),
                                                   sem("a0_exp_done"), sem("a0_p_normed"))
        rinv_ready = sem("a0_rinv_ready")
        t_filled, t_done, o_filled, o_done = (sem("a0_t_filled"), sem("a0_t_done"),
                                              sem("a0_o_filled"), sem("a0_o_done"))
        y_filled, y_added, bias_added = sem("a0_y_filled"), sem("a0_y_added"), sem("a0_bias_added")
        cut_high, cut_done = sem("a0_cut_high"), sem("a0_cut_done")
        B = s.banks
        SB = [B[0], B[1], B[6]]
        GRP = 4
        NG = KTILES // GRP

        block = ctx.enter_context(nc.Block())

        @block.sync
        def _(sp):
            c_dram = dram["ctx_rows"].rearrange("(j p) d -> p j d", p=KB)
            for n in range(LOADS):
                sp.dma_start(ctx_rows[:, n * PER:(n + 1) * PER, :],
                             c_dram[:, n * PER:(n + 1) * PER, :]).then_inc(ctx_loaded[n], 16)
            sp.dma_start(s.x[:], dram["x"].rearrange("(t p) d -> p t d", p=P)).then_inc(x_loaded, 16)
            sp.dma_start(s.ident[:], dram["ident"]).then_inc(small_loaded, 16)
            sp.dma_start(s.ones[:], dram["ones"]).then_inc(small_loaded, 16)
            sp.dma_start(s.earlier[:], dram["earlier"]).then_inc(small_loaded, 16)
            sp.dma_start(rows[:], dram["a0_rows"]).then_inc(small_loaded, 16)
            for w, name in ((w_q, "a0_wq"), (w_o, "a0_wo")):
                sp.dma_start(w[:], dram[name].rearrange("(k p) n -> p k n", p=P)).then_inc(w_loaded, 16)
            sp.dma_start(raw_main[:], dram["ctx_cols"][0:P, :]).then_inc(raw_loaded, 16)
            sp.dma_start(raw_tail[0:TAIL, :], dram["ctx_cols"][P:DC, :]).then_inc(raw_loaded, 16)
            sp.dma_start(raw_tail[TAIL:P, :], dram["ctx_cols"][P:DC, :]).then_inc(raw_loaded, 16)

        @block.gpsimd
        def _(pool):
            pool.wait_ge(raw_loaded, 48)
            pool.tensor_copy(s.ctxH[:], raw_main[:]).then_inc(cut_high, 1)
            pool.wait_ge(cut_high, 1)
            pool.tensor_tensor(s.ctxL[:], raw_main[:], s.ctxH[:].bitcast(F32), ALU.subtract).then_inc(cut_done, 1)
            pool.wait_ge(cut_done, 1)
            pool.tensor_copy(s.ctxT[0:TAIL, :], raw_tail[0:TAIL, :]).then_inc(cut_done, 1)
            for n in range(2):
                half = slice(n * NK // 2, (n + 1) * NK // 2)
                pool.wait_ge(cut_done, n + 2)
                pool.tensor_copy(tail_high[TAIL:P, :], raw_tail[TAIL:P, half]).then_inc(cut_high, 1)
                pool.wait_ge(cut_high, n + 2)
                pool.tensor_tensor(s.ctxT[TAIL:P, half], raw_tail[TAIL:P, half],
                                   tail_high[TAIL:P, :].bitcast(F32), ALU.subtract).then_inc(cut_done, 1)

        @block.vector
        def _(dve):
            def normed(g):
                layer_norm_apply(dve, ln_c, qc, ctx_rows, ctx_rows, range(g * GRP, (g + 1) * GRP))

            def lows(g):
                cols = slice(g * CHUNK, (g + 1) * CHUNK)
                dve.wait_ge(c_high, 2 * g + 1)
                dve.tensor_tensor(cL[:, cols], B[g % 2][:, 0:CHUNK], cH[:, cols].bitcast(F32), ALU.subtract).then_inc(c_cut, 1)
                dve.wait_ge(c_high, 2 * g + 2)
                dve.tensor_tensor(cT[TAIL:P, cols], B[2 + g % 2][TAIL:P, 0:CHUNK], cT[TAIL:P, cols].bitcast(F32),
                                  ALU.subtract).then_inc(c_cut, 1)

            layer_norm_roots(dve, ln_c, qc, ctx_rows, KTILES, ready=lambda i: (ctx_loaded[i // PER], 16))
            normed(0)
            normed(1)
            dve.wait_ge(kv_bias_filled, 1)
            dve.tensor_tensor(kv_bias[:], B[7][:, 0:2 * KT], bkv, ALU.add).then_inc(kv_bias_ready, 1)
            for j in range(2):
                dve.tensor_scalar(wkv[:, :, j, :], wkv[:, :, j, :], g2[:, j:j + 1], None, ALU.mult).then_inc(w_scaled, 1)
            normed(2)
            lows(0)
            dve.wait_ge(w_high, 1)
            dve.tensor_tensor(wkvL[:], wkv[:], wkvH[:].bitcast(F32), ALU.subtract).then_inc(w_cut, 1)
            for g in range(1, NG):
                if g + 2 < NG:
                    normed(g + 2)
                lows(g)
            dve.wait_ge(x_loaded, 16)
            layer_norm_vector(dve, ln_x, qx, s.x, xa)
            dve.wait_ge(qx.normed, TILES)
            layer_norm_vector(dve, ln_y, qy, xa, xa)
            for g in range(GROUPS):
                view, c = turned_view(B[g], g)
                dve.wait_ge(xT_first, g + 1)
                dve.tensor_scalar(xT[:, 1, c], view[:, 1, :], g1[:, 1:2], b1[:, 1:2], ALU.mult, ALU.add).then_inc(xT_done, 1)
            for n in range(4):
                dve.wait_ge(q_filled, n + 1)
                e, half = n // 2, slice((n % 2) * 448, (n % 2) * 448 + 448)
                dve.tensor_scalar(qT[:, e, half], B[4 + n % 2][:, 0:448], bq[:, e:e + 1], D ** -0.5,
                                  ALU.add, ALU.mult).then_inc(q_done, 1)
            def soft_max(b):
                dve.wait_ge(s_filled, b + 1)
                dve.tensor_reduce(nmax[:, b % 3:b % 3 + 1], SB[b % 3][0:SEQ, 0:KEYS], AX.X, ALU.max,
                                  negate=True).then_inc(max_ready, 1)

            def outputs(b):
                dve.wait_ge(o_filled, b + 1)
                dve.tensor_tensor(oT[:, :, b * SEQ:(b + 1) * SEQ],
                                  B[4 + b % 2][:, 0:KT * SEQ].rearrange("p (k c) -> p k c", k=KT),
                                  bv.unsqueeze(2).to_broadcast([P, KT, SEQ]), ALU.add).then_inc(o_done, 1)

            for b in range(AHEAD):
                soft_max(b)
            dve.wait_ge(small_loaded, 64)
            dve.tensor_tensor(s.x[:], s.x[:], rows[:].unsqueeze(1).to_broadcast([P, TILES, D]),
                              ALU.add).then_inc(bias_added, 1)
            for b in range(BATCH):
                dve.wait_ge(exp_done, b + 1)
                dve.reciprocal(rinv[:, b % 3:b % 3 + 1], rsum[:, b % 3:b % 3 + 1]).then_inc(rinv_ready, 1)
                dve.wait_ge(rinv_ready, b + 1)
                dve.tensor_scalar(prob[:, b % 3, :], prob[:, b % 3, :], rinv[:, b % 3:b % 3 + 1], None,
                                  ALU.mult).then_inc(p_normed, 1)
                if b + AHEAD < BATCH:
                    soft_max(b + AHEAD)
                if b >= 1:
                    outputs(b - 1)
            outputs(BATCH - 1)
            dve.wait_ge(bias_added, 1)
            for i in range(TILES):
                dve.wait_ge(y_filled, i + 1)
                dve.tensor_tensor(s.x[:, i, :], s.x[:, i, :], B[6 + i % 2][:, 0:D], ALU.add).then_inc(y_added, 1)

        @block.scalar
        def _(act):
            act.dma_start(cols[:], dram["a0_cols"]).then_inc(wkv_loaded, 16)
            act.dma_start(wkv[:], dram["a0_wkv"]).then_inc(wkv_loaded, 16)

            def highs(g):
                cols = slice(g * CHUNK, (g + 1) * CHUNK)
                act.wait_ge(c_turned, g + 1)
                act.activation(cH[:, cols], B[g % 2][:, 0:CHUNK], ACT.Copy).then_inc(c_high, 1)
                act.activation(cT[:, cols], B[2 + g % 2][:, 0:CHUNK], ACT.Copy).then_inc(c_high, 1)

            def keys(c):
                for e in range(KT):
                    n = KT * c + e
                    act.wait_ge(k_filled, n + 1)
                    act.activation(kT[:, e, c * CHUNK:(c + 1) * CHUNK], B[4 + n % 2][:, 0:CHUNK], ACT.Identity,
                                   bias=bk[:, e:e + 1]).then_inc(k_done, 1)

            layer_norm_scalar(act, ln_c, qc)
            highs(0)
            act.wait_ge(w_scaled, 2)
            act.activation(wkvH[:], wkv[:], ACT.Copy).then_inc(w_high, 1)
            act.wait_ge(kv_bias_ready, 1)
            for g in range(1, NG):
                highs(g)
                keys(g - 1)
            keys(NG - 1)
            for n in range(KTILES // 2):
                if n in (1, 6):
                    layer_norm_scalar(act, *((ln_x, qx) if n == 1 else (ln_y, qy)))
                act.wait_ge(v_filled, n + 1)
                act.activation(v[:, 2 * n:2 * n + 2, :], B[6 + n % 2][0:KB, :].rearrange("p (t d) -> p t d", t=2),
                               ACT.Copy).then_inc(v_done, 1)
            for g in range(GROUPS):
                view, c = turned_view(B[g], g)
                act.wait_ge(qy.turned, g + 1)
                act.activation(xT[:, 0, c], view[:, 0, :], ACT.Identity,
                               scale=g1[:, 0:1], bias=b1[:, 0:1]).then_inc(xT_first, 1)

            def exps(b):
                act.wait_ge(max_ready, b + 1)
                act.activation(prob[:, b % 3, :], SB[b % 3][0:SEQ, 0:KEYS], ACT.Exp, bias=nmax[:, b % 3:b % 3 + 1],
                               accum_out=rsum[:, b % 3:b % 3 + 1]).then_inc(exp_done, 1)

            for b in range(AHEAD):
                exps(b)
            for b in range(BATCH):
                act.wait_ge(t_filled, b + 1)
                act.activation(pT[:, b % 2, :, :], B[2 + b % 2][0:KB, 0:3 * SEQ].rearrange("p (t c) -> p t c", t=3),
                               ACT.Copy).then_inc(t_done, 1)
                if b + AHEAD < BATCH:
                    exps(b + AHEAD)

        @block.tensor
        def _(pe):
            def turn_context(g):
                pe.wait_ge(qc.normed, (g + 1) * GRP)
                need(pe, c_cut, 2 * (g - 1))
                for j in range(GRP):
                    t, at = g * GRP + j, j * KB
                    pe.transpose(B[g % 2][:, at:at + KB], ctx_rows[:, t, 0:P], s.ident[0:KB, 0:KB])
                    pe.transpose(B[2 + g % 2][:, at:at + KB], ctx_rows[:, t, DC - P:DC], s.ident[0:KB, 0:KB])
                    last = pe.transpose(B[2 + g % 2][0:TAIL, at:at + KB], ctx_rows[:, t, P:DC], s.ident[0:KB, 0:KB])
                last.then_inc(c_turned, 1)

            pe.wait_ge(wkv_loaded, 32)
            for n in range(2 * KT):
                at = slice((n % KT) * P, (n % KT + 1) * P)
                last = split_products(pe, B[7][:, n:n + 1], [(wkv[:, n // KT, 0, at], b2[:, 0:1]),
                                                             (wkv[0:TAIL, n // KT, 1, at], b2[0:TAIL, 1:2])])
            last.then_inc(kv_bias_filled, 1)
            pe.wait_ge(small_loaded, 64)
            turn_context(0)
            turn_context(1)
            pe.wait_ge(w_cut, 1)
            for c in range(CHUNKS):
                cols = slice(c * CHUNK, (c + 1) * CHUNK)
                pe.wait_ge(c_cut, 2 * c + 2)
                for e in range(KT):
                    n, at = KT * c + e, slice(e * P, (e + 1) * P)
                    need(pe, k_done, n - 1)
                    split_products(pe, B[4 + n % 2][:, 0:CHUNK], [
                        (wkvH[:, 0, 0, at], cH[:, cols]), (wkvH[:, 0, 0, at], cL[:, cols]), (wkvL[:, 0, 0, at], cH[:, cols]),
                        (wkvH[:, 0, 1, at], cT[:, cols]), (wkvL[:, 0, 1, at], cT[:, cols])]).then_inc(k_filled, 1)
                if c + 2 < NG:
                    turn_context(c + 2)
            pe.wait_ge(kv_bias_ready, 1)
            for n in range(KTILES // 2):
                need(pe, v_done, n - 1)
                for j in range(2):
                    rows_of = slice((2 * n + j) * KB, (2 * n + j + 1) * KB)
                    last = split_products(pe, B[6 + n % 2][0:KB, j * D:(j + 1) * D], [
                        (cH[:, rows_of], wkvH[:, 1, 0, :]), (cH[:, rows_of], wkvL[:, 1, 0, :]), (cL[:, rows_of], wkvH[:, 1, 0, :]),
                        (cT[:, rows_of], wkvH[:, 1, 1, :]), (cT[:, rows_of], wkvL[:, 1, 1, :])])
                last.then_inc(v_filled, 1)
            turn_tensor(pe, qy, xa, B[0:4], s.ident[:])
            pe.wait_ge(xT_done, GROUPS)
            pe.wait_ge(w_loaded, 32)
            pe.wait_ge(k_done, KT * CHUNKS)
            for n in range(4):
                e, half = n // 2, slice((n % 2) * 448, (n % 2) * 448 + 448)
                need(pe, q_done, n - 1)
                split_products(pe, B[4 + n % 2][:, 0:448], [
                    (w_q[:, k, e * P:(e + 1) * P], xT[:, k, half]) for k in range(KT)]).then_inc(q_filled, 1)

            def scores(b):
                if b == 0:
                    pe.wait_ge(q_done, 4)
                need(pe, exp_done, b - AHEAD)
                split_products(pe, SB[b % 3][0:SEQ, 0:KEYS], [
                    (qT[:, k, b * SEQ:(b + 1) * SEQ], kT[:, k, b * KEYS:(b + 1) * KEYS])
                    for k in range(KT)]).then_inc(s_filled, 1)

            def turn(b):
                need(pe, t_done, b - 1)
                pe.wait_ge(p_normed, b + 1)
                for t in range(3):
                    last = pe.transpose(B[2 + b % 2][0:KB, t * SEQ:(t + 1) * SEQ], prob[:, b % 3, t * KB:(t + 1) * KB],
                                        s.ident[0:SEQ, 0:SEQ])
                last.then_inc(t_filled, 1)

            def mix(b):
                need(pe, o_done, b - 1)
                pe.wait_ge(t_done, b + 1)
                for e in range(KT):
                    last = split_products(pe, B[4 + b % 2][:, e * SEQ:(e + 1) * SEQ], [
                        (v[:, 3 * b + t, e * P:(e + 1) * P], pT[:, b % 2, t, :]) for t in range(3)])
                last.then_inc(o_filled, 1)

            for b in range(AHEAD):
                scores(b)
            pe.wait_ge(v_done, KTILES // 2)
            for b in range(BATCH):
                if b + AHEAD < BATCH:
                    scores(b + AHEAD)
                turn(b)
                if b >= 1:
                    mix(b - 1)
            mix(BATCH - 1)
            pe.wait_ge(o_done, BATCH)
            for i in range(TILES):
                need(pe, y_added, i - 1)
                split_products(pe, B[6 + i % 2][:, 0:D], [
                    (oT[:, k, i * P:(i + 1) * P], w_o[:, k, :]) for k in range(KT)]).then_inc(y_filled, 1)


def router_buffers(sb, tag):
    r = Names()
    r.raw = sb(f"{tag}_gate_raw", [P, KT, EXPERTS])
    r.gate = sb(f"{tag}_gateHL", [P, KT, 2 * EXPERTS], F32R)
    r.rows = sb(f"{tag}_logit_rows", [2 * EXPERTS, TOK])
    r.logits = sb(f"{tag}_logits", [P, TILES, EXPERTS])
    r.shifted = sb(f"{tag}_shifted", [P, TILES, EXPERTS])
    r.exps = sb(f"{tag}_exps", [P, TILES, EXPERTS])
    r.probs = sb(f"{tag}_probs", [P, TILES, EXPERTS])
    r.rank = sb(f"{tag}_rank", [P, TILES, EXPERTS])
    r.kept = sb(f"{tag}_kept", [P, TILES, EXPERTS])
    r.above = sb(f"{tag}_above", [P, TILES, EXPERTS, EXPERTS])
    r.ties = sb(f"{tag}_ties", [P, TILES, EXPERTS, EXPERTS])
    r.sums = sb(f"{tag}_sums", [P, 5, TILES])
    return r


def router_semaphores(sem, tag):
    q = Names()
    q.loaded = sem(f"{tag}_gate_loaded")
    q.cut = sem(f"{tag}_gate_cut")
    q.rows_filled = sem(f"{tag}_rows_filled")
    q.rows_out = sem(f"{tag}_rows_out")
    q.filled = sem(f"{tag}_logits_filled")
    q.step = sem(f"{tag}_route_step")
    q.shifted = sem(f"{tag}_logits_shifted")
    q.exps = sem(f"{tag}_exps_done")
    q.kept = sem(f"{tag}_route_ready")
    return q


def router_cut(pool, r, q):
    pool.wait_ge(q.loaded, 16)
    pool.tensor_copy(r.gate[:, :, 0:EXPERTS], r.raw[:]).then_inc(q.cut, 1)
    pool.wait_ge(q.cut, 1)
    pool.tensor_tensor(r.gate[:, :, EXPERTS:], r.raw[:], r.gate[:, :, 0:EXPERTS].bitcast(F32), ALU.subtract).then_inc(q.cut, 1)


def turn_and_route(pe, s, ql, src, banks, r, q, bank):
    turn_tensor(pe, ql, src, banks, s.ident[:])
    pe.wait_ge(q.cut, 2)
    both, high = slice(0, 2 * EXPERTS), slice(0, EXPERTS)
    for n, half in enumerate(HALVES):
        pe.wait_ge(ql.done, GROUPS // 2 * (n + 1))
        for k, x, rows in ((0, s.xnTH, both), (0, s.xnTL, high), (1, s.xnTL, high), (1, s.xnTH, both)):
            last = pe.matmul(banks[n][rows, 0:TOK // 2], r.gate[:, k, rows], x[:, k, half],
                             start=k == 0 and rows is both, stop=k == 1 and rows is both)
        last.then_inc(q.rows_filled, 1)
    for i in range(TILES):
        pe.wait_ge(q.rows_out, 1 if (i + 1) * P <= TOK // 2 else 2)
        last = pe.transpose(bank[:, i * 2 * EXPERTS:(i + 1) * 2 * EXPERTS], r.rows[:, i * P:(i + 1) * P],
                            s.ident[0:2 * EXPERTS, 0:2 * EXPERTS])
    last.then_inc(q.filled, 1)


def router_scalar(act, r, q, banks):
    for n, half in enumerate(HALVES):
        act.wait_ge(q.rows_filled, n + 1)
        act.activation(r.rows[:, half], banks[n][0:2 * EXPERTS, 0:TOK // 2], ACT.Copy).then_inc(q.rows_out, 1)
    act.wait_ge(q.shifted, 1)
    act.activation(r.exps[:], r.shifted[:], ACT.Exp).then_inc(q.exps, 1)


def over_experts(row):
    return row.unsqueeze(2).to_broadcast([P, TILES, EXPERTS])


def router_ranks(dve, s, r, q, key, at):
    every = [P, TILES, EXPERTS, EXPERTS]
    mine, others = key.unsqueeze(3).to_broadcast(every), key.unsqueeze(2).to_broadcast(every)
    dve.tensor_tensor(r.above[:], others, mine, ALU.is_gt).then_inc(q.step, 1)
    dve.tensor_tensor(r.ties[:], others, mine, ALU.is_equal).then_inc(q.step, 1)
    dve.wait_ge(q.step, at + 2)
    dve.tensor_tensor(r.ties[:], r.ties[:], s.earlier[:].unsqueeze(1).to_broadcast(every), ALU.mult).then_inc(q.step, 1)
    dve.wait_ge(q.step, at + 3)
    dve.tensor_tensor(r.above[:], r.above[:], r.ties[:], ALU.add).then_inc(q.step, 1)
    dve.wait_ge(q.step, at + 4)
    dve.tensor_reduce(r.rank[:], r.above[:], AX.X, ALU.add).then_inc(q.step, 1)
    dve.wait_ge(q.step, at + 5)
    return at + 5


def router_exps(dve, r, q, bank):
    dve.wait_ge(q.filled, 1)
    parts = bank[:, 0:TILES * 2 * EXPERTS].rearrange("p (t a e) -> p t e a", a=2, e=EXPERTS)
    dve.tensor_reduce(r.logits[:], parts, AX.X, ALU.add).then_inc(q.step, 1)
    dve.wait_ge(q.step, 1)
    dve.tensor_reduce(r.sums[:, 0, :], r.logits[:], AX.X, ALU.max).then_inc(q.step, 1)
    dve.wait_ge(q.step, 2)
    dve.tensor_tensor(r.shifted[:], r.logits[:], over_experts(r.sums[:, 0, :]), ALU.subtract).then_inc(q.shifted, 1)
    return 2


def router_softmax(dve, r, q, at):
    dve.wait_ge(q.exps, 1)
    dve.tensor_reduce(r.sums[:, 1, :], r.exps[:], AX.X, ALU.add).then_inc(q.step, 1)
    dve.wait_ge(q.step, at + 1)
    dve.reciprocal(r.sums[:, 2, :], r.sums[:, 1, :]).then_inc(q.step, 1)
    dve.wait_ge(q.step, at + 2)
    dve.tensor_tensor(r.probs[:], r.exps[:], over_experts(r.sums[:, 2, :]), ALU.mult).then_inc(q.step, 1)
    dve.wait_ge(q.step, at + 3)
    return at + 3


def router_keep_two(dve, r, q, at, values, out, tiny):
    dve.scalar_tensor_tensor(r.kept[:], r.rank[:], 1.5, values, ALU.is_lt, ALU.mult).then_inc(q.step, 1)
    dve.wait_ge(q.step, at + 1)
    dve.tensor_reduce(r.sums[:, 3, :], r.kept[:], AX.X, ALU.add).then_inc(q.step, 1)
    dve.wait_ge(q.step, at + 2)
    dve.tensor_scalar(r.sums[:, 4, :], r.sums[:, 3, :], tiny, None, ALU.add).then_inc(q.step, 1)
    dve.wait_ge(q.step, at + 3)
    dve.reciprocal(r.sums[:, 2, :], r.sums[:, 4, :]).then_inc(q.step, 1)
    dve.wait_ge(q.step, at + 4)
    dve.tensor_tensor(out, r.kept[:], over_experts(r.sums[:, 2, :]), ALU.mult).then_inc(q.kept, 1)


def layer0_ffn(nc, s, dram):
    with ExitStack() as ctx:
        def sb(name, shape, dt=F32):
            return ctx.enter_context(nc.sbuf_tensor(name, shape, dt))

        sem = ctx.enter_context(phase_semaphores(nc))

        WIDE = 2 * D
        POST = 4
        QUANT_AT = 2
        xn = sb("f0_xn", [P, TILES, D])
        w_raw = sb("f0_w_raw", [P, KT, WIDE])
        wH = sb("f0_wH", [P, KT, WIDE], F32R)
        wL = sb("f0_wL", [P, KT, WIDE], F32R)
        bias = sb("f0_bias", [1, WIDE])
        biasH = sb("f0_biasH", [1, WIDE], F32R)
        biasL = sb("f0_biasL", [1, WIDE], F32R)
        one = sb("f0_one", [1, P], F32R)
        post = sb("f0_post", [P, POST, WIDE])
        coef = sb("f0_coef", [P, 2, TILES])
        quant_raw = sb("f0_quant_raw", [P, 3, 2048])
        abs_out = sb("f0_abs_out", [P, 2048])
        ln = layer_norm_buffers(sb, "f0_ln")
        r = router_buffers(sb, "f0")
        ql = layer_norm_semaphores(sem, "f0_ln")
        q = router_semaphores(sem, "f0_r")
        w_loaded, w_cut, bias_high = sem("f0_w_loaded"), sem("f0_w_cut"), sem("f0_bias_high")
        e_filled, post_ready, x_added = sem("f0_e_filled"), sem("f0_post_ready"), sem("f0_x_added")
        first_added = sem("f0_first_added")
        quant_loaded = [sem(f"f0_quant_loaded{m}") for m in range(3)]
        abs_summed, abs_total = sem("f0_abs_summed"), sem("f0_abs_total")
        scale_step, scale_ready = sem("f0_scale_step"), sem("f0_scale_ready")
        quant_scaled, quant_clipped, quant_done = sem("f0_quant_scaled"), sem("f0_quant_clipped"), sem("f0_quant_done")
        abs_sum = sb("f0_abs_sum", [P, 3])
        w_scale = sb("f0_w_scale", [P, 3])
        B = s.banks
        EB = B[4:8]

        def quant_scale(dve, m):
            dve.wait_ge(scale_ready, 1)
            dve.tensor_scalar(quant_raw[:, m, :], quant_raw[:, m, :], w_scale[:, m:m + 1], 1.0,
                              ALU.mult, ALU.min).then_inc(quant_scaled, 1)

        def quant_round(dve, m):
            dve.wait_ge(quant_scaled, m + 1)
            dve.tensor_scalar(quant_raw[:, m, :], quant_raw[:, m, :], -1.0, MAGIC, ALU.max, ALU.add).then_inc(quant_clipped, 1)

        block = ctx.enter_context(nc.Block())

        @block.sync
        def _(sp):
            sp.dma_start(r.raw[:], dram["f0_gate"]).then_inc(q.loaded, 16)
            sp.dma_start(w_raw[:], dram["f0_w"]).then_inc(w_loaded, 16)
            sp.dma_start(bias[:], dram["f0_bias"]).then_inc(w_loaded, 16)
            for m in range(3):
                sp.dma_start(quant_raw[:, m, :], dram["f1_w"][:, m, :]).then_inc(quant_loaded[m], 16)

        @block.gpsimd
        def _(pool):
            router_cut(pool, r, q)
            pool.tensor_copy(one[:], s.ones[0:1, :])
            pool.wait_ge(w_loaded, 32)
            pool.tensor_copy(biasH[:], bias[:]).then_inc(bias_high, 1)
            pool.tensor_copy(wH[:], w_raw[:]).then_inc(w_cut, 1)
            pool.wait_ge(bias_high, 1)
            pool.tensor_tensor(biasL[:], bias[:], biasH[:].bitcast(F32), ALU.subtract)
            pool.wait_ge(w_cut, 1)
            pool.tensor_tensor(wL[:], w_raw[:], wH[:].bitcast(F32), ALU.subtract).then_inc(w_cut, 1)

        @block.vector
        def _(dve):
            layer_norm_vector(dve, ln, ql, s.x, xn)
            turn_vector(dve, ql, B[4:8], s.xnTH, s.xnTL)
            at = router_exps(dve, r, q, B[0])
            at = router_softmax(dve, r, q, at)
            at = router_ranks(dve, s, r, q, r.probs[:], at)
            for e in range(2):
                dve.scalar_tensor_tensor(coef[:, e, :], r.rank[:, :, e], float(e), r.probs[:, :, e],
                                         ALU.is_equal, ALU.mult).then_inc(q.kept, 1)
            dve.wait_ge(q.kept, 2)
            for i in range(TILES):
                dve.wait_ge(post_ready, i + 1)
                dve.scalar_tensor_tensor(s.x[:, i, :], post[:, i % POST, 0:D], coef[:, 0, i:i + 1], s.x[:, i, :],
                                         ALU.mult, ALU.add).then_inc(first_added, 1)
                dve.wait_ge(first_added, i + 1)
                dve.scalar_tensor_tensor(s.x[:, i, :], post[:, i % POST, D:WIDE], coef[:, 1, i:i + 1], s.x[:, i, :],
                                         ALU.mult, ALU.add).then_inc(x_added, 1)
                if i == QUANT_AT:
                    dve.wait_ge(abs_total, 1)
                    dve.tensor_scalar(s.w_mean[:], B[3][:, 0:3], 1.0 / (P * 2048), EPS, ALU.mult, ALU.max)\
                       .then_inc(scale_step, 1)
                    dve.wait_ge(scale_step, 1)
                    dve.reciprocal(w_scale[:], s.w_mean[:]).then_inc(scale_ready, 1)
                if QUANT_AT < i <= QUANT_AT + 3:
                    quant_scale(dve, i - QUANT_AT - 1)
                if QUANT_AT + 1 < i <= QUANT_AT + 4:
                    quant_round(dve, i - QUANT_AT - 2)

        @block.scalar
        def _(act):
            def brought_back(m):
                act.wait_ge(quant_clipped, m + 1)
                act.activation(s.w_quant[:, m, :], quant_raw[:, m, :], ACT.Copy, bias=-MAGIC).then_inc(quant_done, 1)

            layer_norm_scalar(act, ln, ql)
            turn_scalar(act, ql, B[4:8], s.xnTH)
            router_scalar(act, r, q, B[4:8])
            for i in range(TILES):
                if i < 3:
                    act.wait_ge(quant_loaded[i], 16)
                    need(act, abs_summed, i)
                    act.activation(abs_out[:], quant_raw[:, i, :], ACT.Abs, accum_out=abs_sum[:, i:i + 1]).then_inc(abs_summed, 1)
                act.wait_ge(e_filled, i + 1)
                need(act, x_added, i - POST + 1)
                act.activation(post[:, i % POST, :], EB[i % 4][:, :], ACT.Silu).then_inc(post_ready, 1)
                if i >= QUANT_AT + 3:
                    brought_back(i - QUANT_AT - 3)
            for m in range(TILES - QUANT_AT - 3, 3):
                brought_back(m)

        @block.tensor
        def _(pe):
            turn_and_route(pe, s, ql, xn, B[4:8], r, q, B[0])
            pe.wait_ge(w_cut, 2)
            for i in range(TILES):
                if i == QUANT_AT + 2:
                    pe.wait_ge(abs_summed, 3)
                    pe.matmul(B[3][:, 0:3], s.ones[:], abs_sum[:], start=True, stop=True).then_inc(abs_total, 1)
                tok = slice(i * P, (i + 1) * P)
                need(pe, post_ready, i - 3)
                split_products(pe, EB[i % 4][:, :], [
                    pair for k in range(KT) for pair in (
                        (s.xnTH[:, k, tok], wH[:, k, :]), (s.xnTH[:, k, tok], wL[:, k, :]),
                        (s.xnTL[:, k, tok], wH[:, k, :]))]
                    + [(one[:], biasH[:]), (one[:], biasL[:])]).then_inc(e_filled, 1)
Q_W, K_W = (0, 1), (2, 3)
HALVES = [slice(0, TOK // 2), slice(TOK // 2, TOK)]
VWIDE = 2
VUSES = KTILES // VWIDE
VRING = 4
HIGHS = CHUNKS + 2
QKV = HIGHS + VUSES


class HeadBuffers:

    def __init__(self, sb, tag, ring=VRING):
        self.ring = ring
        self.w_raw = sb(f"{tag}_w_raw", [P, 6, P])
        self.wH = sb(f"{tag}_wH", [P, 4, P], F32R)
        self.wL = sb(f"{tag}_wL", [P, 4, P], F32R)
        self.wv = sb(f"{tag}_wvHL", [P, 2, 2, P], F32R)
        self.wo_raw = sb(f"{tag}_wo_raw", [P, D])
        self.woH = sb(f"{tag}_woH", [P, D], F32R)
        self.woL = sb(f"{tag}_woL", [P, D], F32R)
        self.kH = sb(f"{tag}_kH", [P, NK], F32R)
        self.kL = sb(f"{tag}_kL", [P, NK], F32R)
        self.v_sum = sb(f"{tag}_v_sum", [KB, ring, VWIDE, P])
        self.vH = sb(f"{tag}_vH", [KB, KTILES, P], F32R)
        self.vL = sb(f"{tag}_vL", [KB, KTILES, P], F32R)
        self.qH = sb(f"{tag}_qH", [P, TOK], F32R)
        self.qL = sb(f"{tag}_qL", [P, TOK], F32R)
        self.oH = sb(f"{tag}_oH", [P, TOK], F32R)
        self.oL = sb(f"{tag}_oL", [P, TOK], F32R)


class HeadSemaphores:
    def __init__(self, sem, tag):
        self.loaded = sem(f"{tag}_w_loaded")
        self.wo_loaded = sem(f"{tag}_wo_loaded")
        self.qk_high = sem(f"{tag}_qk_high")
        self.qk_cut = sem(f"{tag}_qk_cut")
        self.wv_high = sem(f"{tag}_wv_high")
        self.wv_cut = sem(f"{tag}_wv_cut")
        self.wo_high = sem(f"{tag}_wo_high")
        self.wo_cut = sem(f"{tag}_wo_cut")
        self.filled = sem(f"{tag}_g_filled")
        self.high = sem(f"{tag}_g_high")
        self.done = sem(f"{tag}_g_done")
        self.v_high = sem(f"{tag}_v_high")
        self.v_cut = sem(f"{tag}_v_cut")
        self.bias_loaded = sem(f"{tag}_bias_loaded")
        self.bias_added = sem(f"{tag}_bias_added")
        self.o_written = sem(f"{tag}_o_written")
        self.o_high = sem(f"{tag}_o_high")
        self.o_cut = sem(f"{tag}_o_cut")


def head_loads(sp, w, q, dram_w, dram_wo):
    sp.dma_start(w.w_raw[:], dram_w[0]).then_inc(q.loaded, 16)
    sp.dma_start(w.wo_raw[:], dram_wo[0]).then_inc(q.wo_loaded, 16)
    with sp.Fori(1, HEADS) as h:
        sp.wait_ge(q.wv_cut, h)
        sp.wait_ge(q.qk_cut, h)
        sp.dma_start(w.w_raw[:], dram_w[bass.ds(h, 1)].rearrange("o p t c -> p (o t) c")).then_inc(q.loaded, 16)
        sp.wait_ge(q.wo_cut, h)
        sp.dma_start(w.wo_raw[:], dram_wo[bass.ds(h, 1)].rearrange("o p c -> p (o c)")).then_inc(q.wo_loaded, 16)


def cut_qk(pool, s, w, q, h, used):
    pool.wait_ge(q.loaded, 16 * h + 16)
    need(pool, q.filled, used)
    pool.tensor_tensor(w.wH[:], w.w_raw[:, 0:4, :], s.ones[:].unsqueeze(1).to_broadcast([P, 4, P]), ALU.mult).then_inc(q.qk_high, 1)
    pool.wait_ge(q.qk_high, h + 1)
    pool.tensor_tensor(w.wL[:], w.w_raw[:, 0:4, :], w.wH[:].bitcast(F32), ALU.subtract).then_inc(q.qk_cut, 1)


def cut_wv(pool, s, w, q, h, used):
    need(pool, q.filled, used)
    pool.tensor_tensor(w.wv[:, :, 0, :], w.w_raw[:, 4:6, :], s.ones[:].unsqueeze(1).to_broadcast([P, 2, P]), ALU.mult)\
        .then_inc(q.wv_high, 1)
    pool.wait_ge(q.wv_high, h + 1)
    pool.tensor_tensor(w.wv[:, :, 1, :], w.w_raw[:, 4:6, :], w.wv[:, :, 0, :].bitcast(F32), ALU.subtract).then_inc(q.wv_cut, 1)


def cut_wo(pool, s, w, q, h, used):
    pool.wait_ge(q.wo_loaded, 16 * h + 16)
    need(pool, q.filled, used)
    pool.tensor_tensor(w.woH[:], w.wo_raw[:], s.ones[:, 0:1].to_broadcast([P, D]), ALU.mult).then_inc(q.wo_high, 1)
    pool.wait_ge(q.wo_high, h + 1)
    pool.tensor_tensor(w.woL[:], w.wo_raw[:], w.woH[:].bitcast(F32), ALU.subtract).then_inc(q.wo_cut, 1)


def bank_free(pe, q, banks, use, n):
    for m in range(n - 1, -1, -1):
        if banks[m] is banks[n]:
            pe.wait_ge(q.done, use + m + 1)
            return


def project_keys(pe, s, w, q, banks, h, use, chunks=range(CHUNKS), waits={}):
    pe.wait_ge(q.qk_cut, h + 1)
    main, tail = K_W
    for c in chunks:
        cols = slice(c * CHUNK, (c + 1) * CHUNK)
        bank_free(pe, q, banks, use, c)
        if c in waits:
            pe.wait_ge(*waits[c])
        split_products(pe, banks[c][:, 0:CHUNK], [
            (w.wH[:, main, :], s.ctxH[:, cols]), (w.wH[:, main, :], s.ctxL[:, cols]), (w.wL[:, main, :], s.ctxH[:, cols]),
            (w.wH[:, tail, :], s.ctxT[:, cols]), (w.wL[:, tail, :], s.ctxT[:, cols])]).then_inc(q.filled, 1)


def project_queries(pe, s, w, q, banks, use):
    for n, half in enumerate(HALVES):
        bank_free(pe, q, banks, use, CHUNKS + n)
        split_products(pe, banks[CHUNKS + n][:, 0:TOK // 2], [pair for k in Q_W for pair in (
            (w.wH[:, k, :], s.xnTH[:, k, half]), (w.wH[:, k, :], s.xnTL[:, k, half]),
            (w.wL[:, k, :], s.xnTH[:, k, half]))]).then_inc(q.filled, 1)


def project_values(pe, s, w, q, banks, h, use, between={}):
    pe.wait_ge(q.wv_cut, h + 1)
    for n in range(VUSES):
        if n in between:
            between[n]()
        bank_free(pe, q, banks, use, HIGHS + n)
        for j in range(VWIDE):
            t = n * VWIDE + j
            cols = slice(t * KB, (t + 1) * KB)
            out = banks[HIGHS + n][0:KB, j * 2 * P:(j + 1) * 2 * P]
            both = [w.wv[:, k, :, :].rearrange("p a c -> p (a c)") for k in range(2)]
            pe.matmul(out, s.ctxH[:, cols], both[0], start=True, stop=False)
            pe.matmul(out[:, 0:P], s.ctxL[:, cols], w.wv[:, 0, 0, :], start=False, stop=False)
            last = pe.matmul(out, s.ctxT[:, cols], both[1], start=False, stop=True)
        last.then_inc(q.filled, 1)


def project_outputs(pe, w, q, banks, h, use, parts):
    pe.wait_ge(q.o_cut, parts * (h + 1))
    pe.wait_ge(q.wo_cut, h + 1)
    for g in range(GROUPS):
        bank_free(pe, q, banks, use, QKV + g)
        for i in range(2 * g, min(2 * g + 2, TILES)):
            tok = slice(i * P, (i + 1) * P)
            last = split_products(pe, banks[QKV + g][:, (i % 2) * D:(i % 2 + 1) * D], [
                (w.oH[:, tok], w.woH[:]), (w.oH[:, tok], w.woL[:]), (w.oL[:, tok], w.woH[:])])
        last.then_inc(q.filled, 1)


def last_outputs(pe, w, q, banks, parts, use):
    pe.wait_ge(q.o_cut, parts * HEADS)
    pe.wait_ge(q.wo_cut, HEADS)
    for g in range(GROUPS):
        for i in range(2 * g, min(2 * g + 2, TILES)):
            tok = slice(i * P, (i + 1) * P)
            last = split_products(pe, banks[g][:, (i % 2) * D:(i % 2 + 1) * D], [
                (w.oH[:, tok], w.woH[:]), (w.oH[:, tok], w.woL[:]), (w.oL[:, tok], w.woH[:])])
        last.then_inc(q.filled, 1)


def high_keys(act, w, q, banks, use, between={}):
    for c in range(CHUNKS):
        if c in between:
            between[c]()
        act.wait_ge(q.filled, use + c + 1)
        act.activation(w.kH[:, c * CHUNK:(c + 1) * CHUNK], banks[c][:, 0:CHUNK], ACT.Copy).then_inc(q.high, 1)


def high_queries(act, w, q, banks, use, scale):
    for n, half in enumerate(HALVES):
        act.wait_ge(q.filled, use + CHUNKS + n + 1)
        act.activation(w.qH[:, half], banks[CHUNKS + n][:, 0:TOK // 2], ACT.Copy, scale=scale).then_inc(q.high, 1)


def high_values(act, w, q, h, use, between={}):
    for n in range(VUSES):
        if n in between:
            between[n]()
        act.wait_ge(q.done, use + HIGHS + n + 1)
        act.activation(w.vH[:, n * VWIDE:(n + 1) * VWIDE, :], w.v_sum[:, n % w.ring, :, :], ACT.Copy).then_inc(q.v_high, 1)


def add_bias(pool, s, q, ql, bias, steps=1):
    pool.wait_ge(q.bias_loaded, 16)
    pool.wait_ge(ql.normed, TILES)
    pool.tensor_tensor(s.x[:], s.x[:], bias[:].unsqueeze(1).to_broadcast([P, TILES, D]), ALU.add).then_inc(q.bias_added, steps)


def low_values(pool, w, q, h):
    for n in range(VUSES):
        tiles = slice(n * VWIDE, (n + 1) * VWIDE)
        pool.wait_ge(q.v_high, VUSES * h + n + 1)
        pool.tensor_tensor(w.vL[:, tiles, :], w.v_sum[:, n % w.ring, :, :], w.vH[:, tiles, :].bitcast(F32),
                           ALU.subtract).then_inc(q.v_cut, 1)


def low_keys(dve, w, q, banks, h, between={}):
    for c in range(CHUNKS):
        if c in between:
            between[c]()
        cols = slice(c * CHUNK, (c + 1) * CHUNK)
        dve.wait_ge(q.high, HIGHS * h + c + 1)
        dve.tensor_tensor(w.kL[:, cols], banks[c][:, 0:CHUNK], w.kH[:, cols].bitcast(F32),
                          ALU.subtract).then_inc(q.done, 1)


def low_queries(dve, w, q, banks, h, scale):
    for n, half in enumerate(HALVES):
        dve.wait_ge(q.high, HIGHS * h + CHUNKS + n + 1)
        dve.scalar_tensor_tensor(w.qL[:, half], banks[CHUNKS + n][:, 0:TOK // 2], scale, w.qH[:, half].bitcast(F32),
                                 ALU.mult, ALU.subtract).then_inc(q.done, 1)


def sum_values(dve, w, q, banks, h, use, between={}):
    for n in range(VUSES):
        if n in between:
            between[n]()
        parts = banks[HIGHS + n][0:KB, :].rearrange("p (t a c) -> p t c a", t=VWIDE, a=2)
        dve.wait_ge(q.filled, use + HIGHS + n + 1)
        if n >= w.ring:
            dve.wait_ge(q.v_cut, VUSES * h + n - w.ring + 1)
        dve.tensor_reduce(w.v_sum[:, n % w.ring, :, :], parts, AX.X, ALU.add).then_inc(q.done, 1)


def add_outputs(dve, s, q, banks, use):
    for g in range(GROUPS):
        tiles = slice(2 * g, min(2 * g + 2, TILES))
        wide = (tiles.stop - tiles.start) * D
        dve.wait_ge(q.filled, use + g + 1)
        dve.tensor_tensor(s.x[:, tiles, :], s.x[:, tiles, :],
                          banks[g][:, 0:wide].rearrange("p (t d) -> p t d", d=D), ALU.add).then_inc(q.done, 1)


def layer1_attention(nc, s, dram):
    SCALE = 1.5 * P ** -0.5
    RING = 3
    AHEAD = 3

    class Group:
        def __init__(self, tiles, at):
            self.tiles, self.wide, self.at = tiles, len(tiles) * P, at
            self.kts = 512 // self.wide
            self.chunks = KTILES // self.kts
            self.tok = slice(tiles[0] * P, (tiles[-1] + 1) * P)

    groups = [Group((0, 1), 0)]
    for tiles in ((2, 3), (4, 5, 6)):
        groups.append(Group(tiles, groups[-1].at + groups[-1].chunks))
    TCHUNKS = groups[-1].at + groups[-1].chunks
    NG = len(groups)
    EXPS = 3
    EXP_AT = (3, 5, 7)
    SUMS_AT = (6, 8, 10)
    with ExitStack() as ctx:
        def sb(name, shape, dt=F32):
            return ctx.enter_context(nc.sbuf_tensor(f"a1_{name}", shape, dt))

        sem = ctx.enter_context(phase_semaphores(nc, "a1_"))
        w = HeadBuffers(sb, "head")
        prob = sb("prob", [P, RING, NK])
        xn = prob[:, 0, 0:TILES * D].rearrange("p (t d) -> p t d", d=D)
        pH = sb("pH", [KB, RING, 512], F32R)
        pL = sb("pL", [KB, RING, 512], F32R)
        o = sb("o", [P, groups[-1].wide])
        bias = sb("bias", [P, D])
        chunk_max = sb("chunk_max", [P, RING, CHUNKS])
        nmax = sb("nmax", [P, RING])
        rsum = sb("rsum", [P, RING, EXPS])
        total = sb("total", [P, RING])
        rinv = sb("rinv", [P, RING])
        spread = sb("spread", [P, groups[-1].wide])
        over_sums = sb("over_sums", [P, groups[-1].wide])
        ln = layer_norm_buffers(sb, "ln")
        ql = layer_norm_semaphores(sem, "ln")
        q = HeadSemaphores(sem, "head")
        s_filled, s_out, max_ready, exp_done = sem("s_filled"), sem("s_out"), sem("max_ready"), sem("exp_done")
        rinv_ready, spread_ready = sem("rinv_ready"), sem("spread_ready")
        t_filled, t_high, t_done, pv_done = sem("t_filled"), sem("t_high"), sem("t_done"), sem("pv_done")
        sums_filled, sums_out = sem("sums_filled"), sem("sums_out")
        B = s.banks
        SB, OB = B[0:3], B[5]
        TB = [B[6], B[7], B[3], B[4]]
        LNB = [*SB, OB]
        EACH = QKV + GROUPS
        GB = TB * (EACH // len(TB))

        def base(h):
            return 0 if isinstance(h, int) and h == 0 else EACH * h - GROUPS

        block = ctx.enter_context(nc.Block())

        @block.sync
        def _(sp):
            sp.dma_start(bias[:], dram["a1_bias"]).then_inc(q.bias_loaded, 16)
            head_loads(sp, w, q, dram["a1_w"], dram["a1_wo"])

        @block.gpsimd
        def _(pool):
            def cut_outputs(h, g):
                tok, n = groups[g].tok, NG * h + g
                pool.wait_ge(q.o_written, n + 1)
                mine = o[:, 0:groups[g].wide]
                pool.tensor_tensor(w.oH[:, tok], mine, s.ones[:, 0:1].to_broadcast([P, groups[g].wide]), ALU.mult)\
                    .then_inc(q.o_high, 1)
                pool.wait_ge(q.o_high, n + 1)
                pool.tensor_tensor(w.oL[:, tok], mine, w.oH[:, tok].bitcast(F32), ALU.subtract).then_inc(q.o_cut, 1)

            def head(h, last):
                if not last:
                    cut_qk(pool, s, w, q, h + 1, base(h) + HIGHS)
                    cut_wv(pool, s, w, q, h + 1, base(h) + QKV)
                for g in range(NG):
                    cut_outputs(h, g)
                if not last:
                    low_values(pool, w, q, h + 1)
                if not last:
                    cut_wo(pool, s, w, q, h + 1, base(h + 1) + EACH)

            cut_qk(pool, s, w, q, 0, 0)
            cut_wv(pool, s, w, q, 0, 0)
            cut_wo(pool, s, w, q, 0, 0)
            add_bias(pool, s, q, ql, bias)
            low_values(pool, w, q, 0)
            head(0, False)
            with pool.Fori(1, HEADS - 1) as h:
                head(h, False)
            head(HEADS - 1, True)

        @block.tensor
        def _(pe):
            def scores(h, t):
                for c in range(CHUNKS):
                    n = CHUNKS * (TILES * h + t) + c
                    need(pe, s_out, n - 2)
                    cols, tok = slice(c * CHUNK, (c + 1) * CHUNK), slice(t * P, (t + 1) * P)
                    split_products(pe, SB[c % 3][:, 0:CHUNK], [
                        (w.qH[:, tok], w.kH[:, cols]), (w.qH[:, tok], w.kL[:, cols]),
                        (w.qL[:, tok], w.kH[:, cols])]).then_inc(s_filled, 1)

            def turn(g, c):
                for j in range(g.kts):
                    key = (c * g.kts + j) * KB
                    for i, t in enumerate(g.tiles):
                        at = j * g.wide + i * P
                        last = pe.transpose(TB[c % 4][0:KB, at:at + P], prob[:, t % RING, key:key + KB], s.ident[:])
                last.then_inc(t_filled, 1)

            def mix(h, g, c):
                n = TCHUNKS * h + g.at + c
                pe.wait_ge(t_done, n + 1)
                terms = []
                for j in range(g.kts):
                    k, cols = c * g.kts + j, slice(j * g.wide, (j + 1) * g.wide)
                    high, low = pH[:, c % RING, cols], pL[:, c % RING, cols]
                    terms += [(w.vH[:, k, :], high), (w.vL[:, k, :], high), (w.vH[:, k, :], low)]
                split_products(pe, OB[:, 0:g.wide], terms, c == 0, c == g.chunks - 1).then_inc(pv_done, 1)

            def turn_and_mix(h, g, between, waits={}):
                group = groups[g]
                pe.wait_ge(exp_done, EXPS * (TILES * h + group.tiles[-1] + 1))
                need(pe, q.o_written, NG * h + g)
                for c in range(AHEAD):
                    if c in waits:
                        pe.wait_ge(q.done, waits[c])
                    turn(group, c)
                for c in range(group.chunks):
                    if c + AHEAD < group.chunks:
                        if c + AHEAD in waits:
                            pe.wait_ge(q.done, waits[c + AHEAD])
                        turn(group, c + AHEAD)
                        if c + AHEAD == group.chunks - 1 and between is not None:
                            scores(*between)
                    if c == group.chunks - 2:
                        pe.wait_ge(spread_ready, TILES * h + group.tiles[-1] + 1)
                        pe.matmul(TB[0][:, 0:group.wide], s.ones[:], spread[:, 0:group.wide], start=True, stop=True)\
                          .then_inc(sums_filled, 1)
                    mix(h, group, c)

            def head(h, last, first=False):
                following = h + 1
                scores(h, 2)
                pe.wait_ge(q.v_cut, VUSES * following)
                done = base(h) + QKV
                turn_and_mix(h, 0, (h, 3), {0: done} if first else {c: done + c + 1 for c in range(4)})
                scores(h, 4)
                turn_and_mix(h, 1, (h, 5))
                scores(h, 6)
                if last:
                    turn_and_mix(h, 2, None)
                    return
                use = base(following)
                pe.wait_ge(q.o_written, NG * h + 2)
                project_keys(pe, s, w, q, GB, following, use)
                project_queries(pe, s, w, q, GB, use)
                turn_and_mix(h, 2, (following, 0), {0: use + HIGHS - 3, 1: use + HIGHS - 2, 2: use + HIGHS - 1, 3: use + HIGHS})
                scores(following, 1)
                pe.wait_ge(q.o_written, NG * following)
                project_values(pe, s, w, q, GB, following, use)
                project_outputs(pe, w, q, GB, h, use, NG)

            project_keys(pe, s, w, q, GB, 0, 0, range(2))
            turn_tensor(pe, ql, xn, LNB, s.ident[:])
            project_keys(pe, s, w, q, GB, 0, 0, range(2, CHUNKS))
            pe.wait_ge(ql.done, GROUPS)
            project_queries(pe, s, w, q, GB, 0)
            pe.wait_ge(q.done, HIGHS)
            scores(0, 0)
            scores(0, 1)
            project_values(pe, s, w, q, GB, 0, 0)
            head(0, False, True)
            with pe.Fori(1, HEADS - 1) as h:
                head(h, False)
            head(HEADS - 1, True)
            pe.wait_ge(q.o_written, NG * HEADS)
            last_outputs(pe, w, q, TB, NG, base(HEADS))

        @block.scalar
        def _(act):
            def part_exps(h, t, n):
                row = prob[:, t % RING, n * NK // EXPS:(n + 1) * NK // EXPS]
                act.wait_ge(max_ready, TILES * h + t + 1)
                act.activation(row, row, ACT.Exp, bias=nmax[:, t % RING:t % RING + 1],
                               accum_out=rsum[:, t % RING, n:n + 1]).then_inc(exp_done, 1)

            def exps(h, t):
                for n in range(EXPS):
                    part_exps(h, t, n)

            def highs(h, n, between):
                g, group = groups[n], NG * h + n
                wide = g.kts * g.wide
                for c in range(g.chunks):
                    n = TCHUNKS * h + g.at + c
                    act.wait_ge(t_filled, n + 1)
                    need(act, pv_done, n + 1 - RING)
                    act.activation(pH[:, c % RING, 0:wide], TB[c % 4][0:KB, 0:wide], ACT.Copy).then_inc(t_high, 1)
                    if c in EXP_AT and between is not None:
                        part_exps(*between, EXP_AT.index(c))
                act.wait_ge(sums_filled, group + 1)
                need(act, q.o_written, group)
                act.activation(over_sums[:, 0:g.wide], TB[0][:, 0:g.wide], ACT.Copy).then_inc(sums_out, 1)

            def head(h, last):
                following = h + 1
                highs(h, 0, (h, 2))
                exps(h, 3)
                highs(h, 1, (h, 4))
                exps(h, 5)
                if last:
                    exps(h, 6)
                    highs(h, 2, None)
                    return
                use = base(following)
                high_keys(act, w, q, GB, use, {n: lambda n=n: part_exps(h, 6, n) for n in range(EXPS)})
                high_queries(act, w, q, GB, use, 1.0)
                highs(h, 2, None)
                exps(following, 0)
                high_values(act, w, q, following, use, {
                    3 * n + 3: lambda n=n: part_exps(following, 1, n) for n in range(EXPS)})

            layer_norm_scalar(act, ln, ql)
            def turned():
                turn_scalar(act, ql, LNB, s.xnTH)
                load_table(act, s, ACT.Exp)

            high_keys(act, w, q, GB, 0, {2: turned})
            high_queries(act, w, q, GB, 0, 1.0)
            exps(0, 0)
            exps(0, 1)
            high_values(act, w, q, 0, 0)
            head(0, False)
            with act.Fori(1, HEADS - 1) as h:
                head(h, False)
            head(HEADS - 1, True)

        @block.vector
        def _(dve):
            def scores_out(h, t):
                at = t % RING
                for c in range(CHUNKS):
                    dve.wait_ge(s_filled, CHUNKS * (TILES * h + t) + c + 1)
                    dve.tensor_scalar(prob[:, at, c * CHUNK:(c + 1) * CHUNK], SB[c % 3][:, 0:CHUNK], SCALE, None,
                                      ALU.mult, ALU.max, accum_out=chunk_max[:, at, c:c + 1]).then_inc(s_out, 1)
                dve.wait_ge(s_out, CHUNKS * (TILES * h + t + 1))
                dve.tensor_reduce(nmax[:, at:at + 1], chunk_max[:, at, :], AX.X, ALU.max, negate=True).then_inc(max_ready, 1)

            def one_over_sums(h, t, i):
                at, tile = t % RING, TILES * h + t
                dve.tensor_reduce(total[:, at:at + 1], rsum[:, at, :], AX.X, ALU.add).then_inc(rinv_ready, 1)
                dve.wait_ge(rinv_ready, 2 * tile + 1)
                dve.reciprocal(rinv[:, at:at + 1], total[:, at:at + 1]).then_inc(rinv_ready, 1)
                dve.wait_ge(rinv_ready, 2 * tile + 2)
                dve.tensor_scalar(spread[:, i * P:(i + 1) * P], s.ident[:], rinv[:, at:at + 1], None,
                                  ALU.mult).then_inc(spread_ready, 1)

            def lows(h, g, between):
                wide = g.kts * g.wide
                for c in range(g.chunks):
                    if c in SUMS_AT[:len(g.tiles)]:
                        i = SUMS_AT.index(c)
                        one_over_sums(h, g.tiles[i], i)
                    if c == g.chunks - 1 and between is not None:
                        scores_out(*between)
                    dve.wait_ge(t_high, TCHUNKS * h + g.at + c + 1)
                    dve.tensor_tensor(pL[:, c % RING, 0:wide], TB[c % 4][0:KB, 0:wide], pH[:, c % RING, 0:wide].bitcast(F32),
                                      ALU.subtract).then_inc(t_done, 1)

            def outputs(h, g):
                group, n = groups[g], NG * h + g
                part = slice(0, group.wide)
                dve.wait_ge(pv_done, TCHUNKS * h + group.at + group.chunks)
                dve.wait_ge(sums_out, n + 1)
                need(dve, q.o_cut, n)
                dve.tensor_tensor(o[:, part], OB[:, part], over_sums[:, part], ALU.mult).then_inc(q.o_written, 1)

            def mixed(h, g, between):
                lows(h, groups[g], between)
                outputs(h, g)

            def head(h, last):
                following = h + 1
                scores_out(h, 2)
                mixed(h, 0, (h, 3))
                scores_out(h, 4)
                mixed(h, 1, (h, 5))
                scores_out(h, 6)
                if last:
                    mixed(h, 2, None)
                    return
                use = base(following)
                low_keys(dve, w, q, GB, following)
                low_queries(dve, w, q, GB, following, 1.0)
                mixed(h, 2, (following, 0))
                scores_out(following, 1)
                sum_values(dve, w, q, GB, following, use)
                add_outputs(dve, s, q, GB[QKV:], use + QKV)

            layer_norm_vector(dve, ln, ql, s.x, xn)
            low_keys(dve, w, q, GB, 0, {2: lambda: turn_vector(dve, ql, LNB, s.xnTH, s.xnTL)})
            low_queries(dve, w, q, GB, 0, 1.0)
            scores_out(0, 0)
            scores_out(0, 1)
            sum_values(dve, w, q, GB, 0, 0)
            dve.wait_ge(q.bias_added, 1)
            head(0, False)
            with dve.Fori(1, HEADS - 1) as h:
                head(h, False)
            head(HEADS - 1, True)
            add_outputs(dve, s, q, TB, base(HEADS))


def layer1_ffn(nc, s, dram):
    INNER = 1024
    IT = INNER // P
    with ExitStack() as ctx:
        def sb(name, shape, dt=F32):
            return ctx.enter_context(nc.sbuf_tensor(name, shape, dt))

        sem = ctx.enter_context(phase_semaphores(nc))

        xn = sb("f1_xn", [P, TILES, D])
        big = sb("f1_big", [P, TILES, D])
        xq = sb("f1_xq", [P, TILES, D], BF16)
        xqT = sb("f1_xqT", [P, KT, TOK], BF16)
        ident = sb("f1_ident", [P, P], BF16)
        xa = sb("f1_xa", [P, 6, TILES])
        gate = sb("f1_gate", [P, 2, INNER])
        hid = sb("f1_hid", [P, 2, INNER])
        hbig = sb("f1_hbig", [P, 2, INNER])
        hq = sb("f1_hq", [P, 2, INNER], BF16)
        hqT = sb("f1_hqT", [P, 2, IT, P], BF16)
        ha = sb("f1_ha", [P, 4, TILES])
        ln = layer_norm_buffers(sb, "f1_ln")
        ql = layer_norm_semaphores(sem, "f1_ln")
        const_ready, x_step, x_scaled, x_rounded = (sem("f1_const_ready"), sem("f1_x_step"), sem("f1_x_scaled"),
                                                    sem("f1_x_rounded"))
        scales_ready = sem("f1_scales_ready")
        xt_filled, xt_done = sem("f1_xt_filled"), sem("f1_xt_done")
        g_filled, g_done, u_filled, h_done = sem("f1_g_filled"), sem("f1_g_done"), sem("f1_u_filled"), sem("f1_h_done")
        h_step, h_scaled, h_big, h_rounded = sem("f1_h_step"), sem("f1_h_scaled"), sem("f1_h_big"), sem("f1_h_rounded")
        ht_filled, ht_done, y_filled, y_added = (sem("f1_ht_filled"), sem("f1_ht_done"), sem("f1_y_filled"),
                                                 sem("f1_y_added"))
        B = s.banks
        w_gate = s.w_quant[:, 0, :].rearrange("p (k n) -> p k n", k=KT)
        w_up = s.w_quant[:, 1, :].rearrange("p (k n) -> p k n", k=KT)
        w_down = s.w_quant[:, 2, :].rearrange("p (k n) -> p k n", k=IT)
        turned = [B[n][:, :].bitcast(BF16) for n in (4, 5)]
        top, room, scale, inv, inv_gate, inv_up = (xa[:, n, :] for n in range(6))
        block = ctx.enter_context(nc.Block())

        @block.vector
        def _(dve):
            dve.tensor_copy(ident[:], s.ident[:]).then_inc(const_ready, 1)
            layer_norm_vector(dve, ln, ql, s.x, xn)
            dve.wait_ge(ql.normed, TILES)
            dve.tensor_reduce(top, xn[:], AX.X, ALU.max, apply_absolute_value=True).then_inc(x_step, 1)
            dve.wait_ge(x_step, 1)
            dve.tensor_scalar(room, top, EPS, None, ALU.max).then_inc(x_step, 1)
            dve.wait_ge(x_step, 2)
            dve.reciprocal(top, room).then_inc(x_step, 1)
            dve.tensor_scalar(inv, room, 1.0 / 127.0, None, ALU.mult).then_inc(x_step, 1)
            dve.wait_ge(x_step, 4)
            dve.tensor_scalar(scale, top, 127.0, None, ALU.mult).then_inc(x_step, 1)
            dve.wait_ge(x_step, 5)
            for i in range(TILES):
                dve.tensor_scalar(big[:, i, :], xn[:, i, :], scale[:, i:i + 1], MAGIC, ALU.mult, ALU.add)\
                   .then_inc(x_scaled, 1)
            for i in range(TILES):
                dve.wait_ge(x_scaled, i + 1)
                dve.tensor_scalar(xq[:, i, :], big[:, i, :], MAGIC, 127.0, ALU.subtract, ALU.min)\
                   .then_inc(x_rounded, 1)
            dve.tensor_scalar(inv_gate, inv, s.w_mean[:, 0:1], None, ALU.mult).then_inc(scales_ready, 1)
            dve.tensor_scalar(inv_up, inv, s.w_mean[:, 1:2], None, ALU.mult).then_inc(scales_ready, 1)
            dve.wait_ge(scales_ready, 2)

            def hidden(i):
                for n in range(2):
                    part = slice(n * 512, n * 512 + 512)
                    dve.wait_ge(g_done, 2 * i + n + 1)
                    dve.wait_ge(u_filled, 2 * i + n + 1)
                    dve.scalar_tensor_tensor(hid[:, i % 2, part], B[2 + n][:, :], inv_up[:, i:i + 1],
                                             gate[:, i % 2, part], ALU.mult, ALU.mult).then_inc(h_done, 1)
                dve.wait_ge(h_done, 2 * i + 2)
                dve.tensor_reduce(ha[:, 0, i:i + 1], hid[:, i % 2, :], AX.X, ALU.max,
                                  apply_absolute_value=True).then_inc(h_step, 1)
                dve.wait_ge(h_step, 4 * i + 1)
                dve.tensor_scalar(ha[:, 1, i:i + 1], ha[:, 0, i:i + 1], EPS, None, ALU.max).then_inc(h_step, 1)
                dve.wait_ge(h_step, 4 * i + 2)
                dve.reciprocal(ha[:, 0, i:i + 1], ha[:, 1, i:i + 1]).then_inc(h_step, 1)
                dve.wait_ge(h_step, 4 * i + 3)
                dve.tensor_scalar(ha[:, 2, i:i + 1], ha[:, 0, i:i + 1], 127.0, None, ALU.mult).then_inc(h_scaled, 1)
                dve.tensor_scalar(ha[:, 3, i:i + 1], ha[:, 1, i:i + 1], 1.0 / 127.0, s.w_mean[:, 2:3],
                                  ALU.mult, ALU.mult).then_inc(h_step, 1)

            def rounded(i):
                dve.wait_ge(h_big, i + 1)
                dve.tensor_scalar(hq[:, i % 2, :], hbig[:, i % 2, :], MAGIC, 127.0, ALU.subtract, ALU.min)\
                   .then_inc(h_rounded, 1)

            def into_x(i):
                dve.wait_ge(y_filled, i + 1)
                dve.scalar_tensor_tensor(s.x[:, i, :], B[6 + i % 2][:, 0:D], ha[:, 3, i:i + 1], s.x[:, i, :],
                                         ALU.mult, ALU.add).then_inc(y_added, 1)

            hidden(0)
            for i in range(TILES):
                if i + 1 < TILES:
                    hidden(i + 1)
                rounded(i)
                if i >= 1:
                    into_x(i - 1)
            into_x(TILES - 1)

        @block.scalar
        def _(act):
            layer_norm_scalar(act, ln, ql)
            load_table(act, s, ACT.Silu)
            for i in range(TILES):
                act.wait_ge(xt_filled, i + 1)
                act.activation(xqT[:, :, i * P:(i + 1) * P], turned[i % 2][:, 0:D].rearrange("p (k c) -> p k c", k=KT),
                               ACT.Copy).then_inc(xt_done, 1)
            act.wait_ge(scales_ready, 2)

            def gates(i):
                for n in range(2):
                    act.wait_ge(g_filled, 2 * i + n + 1)
                    act.activation(gate[:, i % 2, n * 512:n * 512 + 512], B[n][:, :], ACT.Silu,
                                   scale=inv_gate[:, i:i + 1]).then_inc(g_done, 1)

            def scaled(i):
                act.wait_ge(h_scaled, i + 1)
                act.activation(hbig[:, i % 2, :], hid[:, i % 2, :], ACT.Copy, scale=ha[:, 2, i:i + 1],
                               bias=MAGIC).then_inc(h_big, 1)

            def turned_out(i):
                act.wait_ge(ht_filled, i + 1)
                act.activation(hqT[:, i % 2, :, :], turned[i % 2].rearrange("p (k c) -> p k c", k=IT),
                               ACT.Copy).then_inc(ht_done, 1)

            gates(0)
            for i in range(TILES):
                if i + 1 < TILES:
                    gates(i + 1)
                scaled(i)
                if i >= 1:
                    turned_out(i - 1)
            turned_out(TILES - 1)

        @block.tensor
        def _(pe):
            pe.wait_ge(const_ready, 1)
            for i in range(TILES):
                pe.wait_ge(x_rounded, i + 1)
                need(pe, xt_done, i - 1)
                for k in range(KT):
                    last = pe.transpose(turned[i % 2][:, k * P:(k + 1) * P], xq[:, i, k * P:(k + 1) * P], ident[:])
                last.then_inc(xt_filled, 1)
            pe.wait_ge(xt_done, TILES)

            def up(i):
                tok = slice(i * P, (i + 1) * P)
                for bank, weights, filled, read in ((0, w_gate, g_filled, g_done), (2, w_up, u_filled, h_done)):
                    for n in range(2):
                        need(pe, read, 2 * (i - 1) + n + 1)
                        split_products(pe, B[bank + n][:, :], [
                            (xqT[:, k, tok], weights[:, k, n * 512:n * 512 + 512]) for k in range(KT)]).then_inc(filled, 1)

            def down(i):
                pe.wait_ge(h_rounded, i + 1)
                need(pe, ht_done, i - 1)
                for k in range(IT):
                    last = pe.transpose(turned[i % 2][:, k * P:(k + 1) * P], hq[:, i % 2, k * P:(k + 1) * P], ident[:])
                last.then_inc(ht_filled, 1)
                pe.wait_ge(ht_done, i + 1)
                need(pe, y_added, i - 1)
                split_products(pe, B[6 + i % 2][:, 0:D], [
                    (hqT[:, i % 2, k, :], w_down[:, k, :]) for k in range(IT)]).then_inc(y_filled, 1)

            up(0)
            for i in range(TILES):
                if i + 1 < TILES:
                    up(i + 1)
                if i >= 1:
                    down(i - 1)
            down(TILES - 1)
def attention_heads64(nc, s, dram, layer, experts=False):
    RING = 4
    AHEAD = 3
    HD = 64
    SCALE = HD ** -0.5
    BKT = KEYS // KB
    PAIR = 2 * SEQ
    EVEN = KEYS + 1

    def first_key(b):
        return min(b * KEYS, NK - EVEN)

    def own_keys(b):
        skip = b * KEYS - first_key(b)
        return slice(skip, skip + KEYS)

    with ExitStack() as ctx:
        def sb(name, shape, dt=F32):
            return ctx.enter_context(nc.sbuf_tensor(f"a{layer}_{name}", shape, dt))

        sem = ctx.enter_context(phase_semaphores(nc, f"a{layer}_"))

        w = HeadBuffers(sb, "head", 2 * VRING)
        prob = sb("prob", [P, RING, 2 * KEYS])
        xn = prob[:].rearrange("p r k -> p (r k)")[:, 0:TILES * D].rearrange("p (t d) -> p t d", d=D)
        o = sb("o", [P, TOK])
        pH = sb("pH", [KB, 2, BKT, PAIR], F32R)
        pL = sb("pL", [KB, 2, BKT, PAIR], F32R)
        y = sb("y", [P, TILES, D])
        bias = sb("bias", [P, D])
        nmax = sb("nmax", [SEQ, RING, 2])
        rsum = sb("rsum", [SEQ, RING, 2])
        rinv = sb("rinv", [SEQ, RING, 2])
        ln = layer_norm_buffers(sb, "ln")
        ql = layer_norm_semaphores(sem, "ln")
        q = HeadSemaphores(sem, "head")
        s_filled, max_ready, exp_done = sem("s_filled"), sem("max_ready"), sem("exp_done")
        rinv_ready, p_normed = sem("rinv_ready"), sem("p_normed")
        t_filled, t_high, t_done, pv_done = sem("t_filled"), sem("t_high"), sem("t_done"), sem("pv_done")
        out_filled, out_done = sem("out_filled"), sem("out_done")
        expert_loaded = sem("expert_loaded")
        if experts:
            expert = sb("expert", [P, 2 * EXPERTS, D])
        B = s.banks
        SB = [B[0:2], B[2:4]]
        LNB = B[2:6]
        TB = [B[4:6], B[6:8]]
        GB = [SB[0][0], *TB[1], SB[0][1], *TB[1], *SB[0], *(TB[0] + TB[1]) * (VUSES // 4)]
        OLATE = 6
        OPARTS = [slice(0, OLATE * SEQ), slice(OLATE * SEQ, TOK)]
        OUT = slice(PAIR, 2 * PAIR)
        EACH = QKV + (1 if experts else 0)
        PARTS_AT = {VUSES - 2 * (GROUPS - g): g for g in range(GROUPS)}

        def base(h):
            return EACH * h

        def part_tiles(g):
            return slice(2 * g, min(2 * g + 2, TILES))

        def probs(b, i):
            return prob[0:SEQ, b % RING, i * KEYS:(i + 1) * KEYS]

        block = ctx.enter_context(nc.Block())

        @block.sync
        def _(sp):
            sp.dma_start(bias[:], dram[f"a{layer}_bias"]).then_inc(q.bias_loaded, 16)
            head_loads(sp, w, q, dram[f"a{layer}_w"], dram[f"a{layer}_wo"])

        @block.gpsimd
        def _(pool):
            def norm(h, b):
                both = prob[0:SEQ, b % RING, :].rearrange("p (i k) -> p i k", i=2)
                pool.wait_ge(rinv_ready, BATCH * h + b + 1)
                pool.tensor_tensor(both, both, rinv[:, b % RING, :].unsqueeze(2).to_broadcast([SEQ, 2, KEYS]),
                                   ALU.mult).then_inc(p_normed, 1)

            def low_outputs(h, n):
                tok = OPARTS[n]
                pool.wait_ge(q.o_high, 2 * h + n + 1)
                pool.tensor_tensor(w.oL[:, tok], o[:, tok], w.oH[:, tok].bitcast(F32), ALU.subtract).then_inc(q.o_cut, 1)

            def low_queries_keys_weights(h, n):
                pool.wait_ge(q.qk_high, h + 1)
                part = slice(2 * n, 2 * n + 2)
                last = pool.tensor_tensor(w.wL[:, part, :], w.w_raw[:, part, :], w.wH[:, part, :].bitcast(F32), ALU.subtract)
                if n == 1:
                    last.then_inc(q.qk_cut, 1)

            def low_values_weights(h):
                pool.wait_ge(q.wv_high, h + 1)
                pool.tensor_tensor(w.wv[:, :, 1, :], w.w_raw[:, 4:6, :], w.wv[:, :, 0, :].bitcast(F32), ALU.subtract)\
                    .then_inc(q.wv_cut, 1)

            def low_output_weights(h):
                pool.wait_ge(q.wo_high, h + 1)
                pool.tensor_tensor(w.woL[:], w.wo_raw[:], w.woH[:].bitcast(F32), ALU.subtract).then_inc(q.wo_cut, 1)

            def add_part(h, g):
                tiles = part_tiles(g)
                pool.wait_ge(out_done, GROUPS * (h - 1) + g + 1)
                pool.tensor_tensor(s.x[:, tiles, :], s.x[:, tiles, :], y[:, tiles, :], ALU.add).then_inc(q.bias_added, 1)

            def pair(h, first, last):
                if not first:
                    low_outputs(h - 1, 1)
                norm(h, 0)
                norm(h, 1)
                low_values(pool, w, q, h)
                for b in range(2, BATCH):
                    norm(h, b)
                    if not last and b in (4, 5):
                        low_queries_keys_weights(h + 1, b - 4)
                    if last and b >= BATCH - GROUPS:
                        add_part(h, b - (BATCH - GROUPS))
                low_output_weights(h)
                if not last:
                    low_values_weights(h + 1)
                    if not first:
                        for g in range(GROUPS):
                            add_part(h, g)
                low_outputs(h, 0)

            for n in range(2):
                low_queries_keys_weights(0, n)
            low_values_weights(0)
            add_bias(pool, s, q, ql, bias, GROUPS)
            pool.wait_ge(q.bias_added, GROUPS)
            pair(0, True, False)
            with pool.Fori(1, HEADS - 1) as h:
                pair(h, False, False)
            pair(HEADS - 1, False, True)
            low_outputs(HEADS - 1, 1)

        @block.tensor
        def _(pe):
            def scores(h, b):
                n = BATCH * h + b
                need(pe, exp_done, n - 1)
                tok, keys = slice(b * SEQ, (b + 1) * SEQ), slice(first_key(b), first_key(b) + EVEN)
                for n, (q_part, k_part) in enumerate(((w.qH, w.kH), (w.qH, w.kL), (w.qL, w.kH))):
                    for i in range(2):
                        rows = slice(i * HD, (i + 1) * HD)
                        last = pe.matmul(SB[b % 2][i][0:SEQ, 0:EVEN], q_part[rows, tok], k_part[rows, keys],
                                         start=n == 0, stop=n == 2)
                last.then_inc(s_filled, 1)

            def turn(h, b):
                n = BATCH * h + b
                pe.wait_ge(p_normed, n + 1)
                need(pe, q.o_written, n - 1)
                for k in range(BKT):
                    for i in range(2):
                        at = (k % 2) * PAIR + i * SEQ
                        last = pe.transpose(TB[b % 2][k // 2][0:KB, at:at + SEQ],
                                            probs(b, i)[:, k * KB:(k + 1) * KB], s.ident[0:SEQ, 0:SEQ])
                last.then_inc(t_filled, 1)

            def mix(h, b):
                pe.wait_ge(t_done, BATCH * h + b + 1)
                terms = []
                for k in range(BKT):
                    t = BKT * b + k
                    terms += [(w.vH[:, t, :], pH[:, b % 2, k, :]), (w.vL[:, t, :], pH[:, b % 2, k, :]),
                              (w.vH[:, t, :], pL[:, b % 2, k, :])]
                split_products(pe, TB[b % 2][1][:, OUT], terms).then_inc(pv_done, 1)

            def add_up(h, g):
                if g == 0:
                    pe.wait_ge(q.o_cut, 2 * h)
                    pe.wait_ge(q.wo_cut, h)
                    pe.wait_ge(exp_done, BATCH * h + 2)
                if g >= 2:
                    pe.wait_ge(out_done, GROUPS * (h - 1) + g - 1)
                tiles = part_tiles(g)
                for i in range(tiles.start, tiles.stop):
                    tok = slice(i * P, (i + 1) * P)
                    last = split_products(pe, SB[1][g % 2][:, (i % 2) * D:(i % 2 + 1) * D], [
                        (w.oH[:, tok], w.woH[:]), (w.oH[:, tok], w.woL[:]), (w.oL[:, tok], w.woH[:])])
                last.then_inc(out_filled, 1)

            def last_part(g):
                tiles = part_tiles(g)
                for i in range(tiles.start, tiles.stop):
                    tok = slice(i * P, (i + 1) * P)
                    last = split_products(pe, B[g][:, (i % 2) * D:(i % 2 + 1) * D], [
                        (w.oH[:, tok], w.woH[:]), (w.oH[:, tok], w.woL[:]), (w.oL[:, tok], w.woH[:])])
                last.then_inc(q.filled, 1)

            def combine(h, use):
                pe.wait_ge(expert_loaded, 16 * h + 16)
                pe.wait_ge(q.done, use)
                for j in range(KT):
                    last = split_products(pe, TB[1][0][:, j * D:(j + 1) * D], [
                        (expert[:, k, j * P:(j + 1) * P], expert[:, EXPERTS + k, :]) for k in range(EXPERTS)])
                last.then_inc(q.filled, 1)

            def pair(h, first):
                use = base(h)
                if first:
                    project_keys(pe, s, w, q, GB, h, use, range(2))
                    turn_tensor(pe, ql, xn, LNB, s.ident[:])
                    project_keys(pe, s, w, q, GB, h, use, range(2, CHUNKS))
                    pe.wait_ge(ql.done, GROUPS)
                else:
                    project_keys(pe, s, w, q, GB, h, use, [0], {0: (exp_done, BATCH * h - 1)})
                    turn(h - 1, BATCH - 2)
                    mix(h - 1, BATCH - 3)
                    project_keys(pe, s, w, q, GB, h, use, range(1, CHUNKS), {2: (q.o_written, BATCH * h - 2)})
                project_queries(pe, s, w, q, GB, use)
                if not first:
                    pe.wait_ge(q.done, use + CHUNKS)
                    turn(h - 1, BATCH - 1)
                    mix(h - 1, BATCH - 2)
                pe.wait_ge(q.done, use + HIGHS)
                scores(h, 0)
                if not first:
                    mix(h - 1, BATCH - 1)
                scores(h, 1)
                if not first:
                    pe.wait_ge(q.o_written, BATCH * h - 1)
                between = {5: lambda: scores(h, 2)}
                if not first:
                    between.update({n: lambda g=g: add_up(h, g) for n, g in PARTS_AT.items()})
                    between[2] = lambda: pe.wait_ge(q.o_written, BATCH * h)
                project_values(pe, s, w, q, GB, h, use, between)
                use = use + QKV
                pe.wait_ge(q.done, use - 2)
                turn(h, 0)
                if experts:
                    combine(h, use - 1)
                if not first:
                    pe.wait_ge(out_done, GROUPS * h)
                scores(h, AHEAD)
                pe.wait_ge(q.done, base(h) + EACH)
                turn(h, 1)
                pe.wait_ge(q.v_cut, VUSES * (h + 1))
                mix(h, 0)
                for b in range(1, BATCH - AHEAD):
                    scores(h, b + AHEAD)
                    turn(h, b + 1)
                    mix(h, b)

            pair(0, True)
            with pe.Fori(1, HEADS) as h:
                pair(h, False)
            turn(HEADS - 1, BATCH - 2)
            mix(HEADS - 1, BATCH - 3)
            turn(HEADS - 1, BATCH - 1)
            mix(HEADS - 1, BATCH - 2)
            pe.wait_ge(q.wo_cut, HEADS)
            pe.wait_ge(q.o_cut, 2 * HEADS - 1)
            last_part(0)
            last_part(1)
            mix(HEADS - 1, BATCH - 1)
            pe.wait_ge(q.o_cut, 2 * HEADS)
            last_part(2)
            last_part(3)

        @block.scalar
        def _(act):
            def exps(h, b):
                act.wait_ge(max_ready, BATCH * h + b + 1)
                for i in range(2):
                    last = act.activation(probs(b, i), SB[b % 2][i][0:SEQ, own_keys(b)], ACT.Exp,
                                          bias=nmax[:, b % RING, i:i + 1], accum_out=rsum[:, b % RING, i:i + 1])
                last.then_inc(exp_done, 1)

            def highs(h, b):
                act.wait_ge(t_filled, BATCH * h + b + 1)
                act.activation(pH[:, b % 2, 0:2, :], TB[b % 2][0][0:KB, 0:2 * PAIR].rearrange("p (k c) -> p k c", k=2),
                               ACT.Copy).then_inc(t_high, 1)
                act.activation(pH[:, b % 2, 2, :], TB[b % 2][1][0:KB, 0:PAIR], ACT.Copy).then_inc(t_high, 1)

            def high_outputs(h, n):
                tok = OPARTS[n]
                act.wait_ge(q.o_written, BATCH * h + (OLATE, BATCH)[n])
                act.activation(w.oH[:, tok], o[:, tok], ACT.Copy).then_inc(q.o_high, 1)

            def high_queries_keys_weights(h, used):
                act.wait_ge(q.loaded, 16 * h + 16)
                need(act, q.filled, used)
                act.activation(w.wH[:], w.w_raw[:, 0:4, :], ACT.Copy).then_inc(q.qk_high, 1)

            def high_values_weights(h, used):
                need(act, q.filled, used)
                act.activation(w.wv[:, :, 0, :], w.w_raw[:, 4:6, :], ACT.Copy).then_inc(q.wv_high, 1)

            def high_output_weights(h):
                act.wait_ge(q.wo_loaded, 16 * h + 16)
                need(act, out_filled, GROUPS * h)
                act.activation(w.woH[:], w.wo_raw[:], ACT.Copy).then_inc(q.wo_high, 1)

            def part_out(h, g):
                if g == 0:
                    act.wait_ge(q.bias_added, GROUPS * h)
                tiles = part_tiles(g)
                wide = (tiles.stop - tiles.start) * D
                act.wait_ge(out_filled, GROUPS * (h - 1) + g + 1)
                act.activation(y[:, tiles, :], SB[1][g % 2][:, 0:wide].rearrange("p (t d) -> p t d", d=D),
                               ACT.Copy).then_inc(out_done, 1)

            def turned():
                turn_scalar(act, ql, LNB, s.xnTH)
                load_table(act, s, ACT.Exp)

            def pair(h, first, last):
                use = base(h)
                if not first:
                    highs(h - 1, BATCH - 2)
                high_keys(act, w, q, GB, use, {2: turned if first else lambda: high_outputs(h - 1, 0)})
                high_queries(act, w, q, GB, use, SCALE)
                if not first:
                    highs(h - 1, BATCH - 1)
                exps(h, 0)
                if not first:
                    high_outputs(h - 1, 1)
                exps(h, 1)
                between = {n: lambda g=g: part_out(h, g) for n, g in PARTS_AT.items()} if not first else {}
                between[7] = lambda: exps(h, 2)
                high_values(act, w, q, h, use, between)
                highs(h, 0)
                for b in range(BATCH - AHEAD):
                    highs(h, b + 1)
                    exps(h, b + AHEAD)
                    if b == 0 and not last:
                        high_queries_keys_weights(h + 1, use + HIGHS)
                    if b == 1 and not last:
                        high_values_weights(h + 1, use + QKV)
                    if b == 2:
                        high_output_weights(h)

            def next_expert(h):
                if experts:
                    act.wait_ge(q.filled, base(h))
                    act.dma_start(expert[:], dram["f2_w"][bass.ds(h, 1)].rearrange("o p t c -> p (o t) c"))\
                       .then_inc(expert_loaded, 16)

            layer_norm_scalar(act, ln, ql)
            high_queries_keys_weights(0, 0)
            high_values_weights(0, 0)
            if experts:
                act.dma_start(expert[:], dram["f2_w"][0]).then_inc(expert_loaded, 16)
            pair(0, True, False)
            with act.Fori(1, HEADS - 1) as h:
                next_expert(h)
                pair(h, False, False)
            next_expert(HEADS - 1)
            pair(HEADS - 1, False, True)
            highs(HEADS - 1, BATCH - 2)
            high_outputs(HEADS - 1, 0)
            highs(HEADS - 1, BATCH - 1)
            high_outputs(HEADS - 1, 1)

        @block.vector
        def _(dve):
            def maxima(h, b):
                dve.wait_ge(s_filled, BATCH * h + b + 1)
                for i in range(2):
                    last = dve.tensor_reduce(nmax[:, b % RING, i:i + 1], SB[b % 2][i][0:SEQ, own_keys(b)], AX.X, ALU.max, negate=True)
                last.then_inc(max_ready, 1)

            def one_over_sums(h, b):
                dve.wait_ge(exp_done, BATCH * h + b + 1)
                dve.reciprocal(rinv[:, b % RING, :], rsum[:, b % RING, :]).then_inc(rinv_ready, 1)

            def lows(h, b, between=None):
                n = 2 * (BATCH * h + b)
                dve.wait_ge(t_high, n + 1)
                dve.tensor_tensor(pL[:, b % 2, 0:2, :], TB[b % 2][0][0:KB, 0:2 * PAIR].rearrange("p (k c) -> p k c", k=2),
                                  pH[:, b % 2, 0:2, :].bitcast(F32), ALU.subtract)
                if between is not None:
                    outputs(*between)
                dve.wait_ge(t_high, n + 2)
                dve.tensor_tensor(pL[:, b % 2, 2, :], TB[b % 2][1][0:KB, 0:PAIR], pH[:, b % 2, 2, :].bitcast(F32),
                                  ALU.subtract).then_inc(t_done, 1)

            def outputs(h, b):
                tok = slice(b * SEQ, (b + 1) * SEQ)
                dve.wait_ge(pv_done, BATCH * h + b + 1)
                for i in range(2):
                    rows = slice(i * HD, (i + 1) * HD)
                    last = dve.tensor_copy(o[rows, tok], TB[b % 2][1][rows, PAIR + i * SEQ:PAIR + (i + 1) * SEQ])
                last.then_inc(q.o_written, 1)

            def pair(h, first):
                use = base(h)
                if not first:
                    lows(h - 1, BATCH - 2, (h - 1, BATCH - 3))
                low_keys(dve, w, q, GB, h, {2: lambda: turn_vector(dve, ql, LNB, s.xnTH, s.xnTL)} if first else {})
                low_queries(dve, w, q, GB, h, SCALE)
                if not first:
                    lows(h - 1, BATCH - 1, (h - 1, BATCH - 2))
                maxima(h, 0)
                if not first:
                    outputs(h - 1, BATCH - 1)
                maxima(h, 1)
                sum_values(dve, w, q, GB, h, use, {
                    1: lambda: one_over_sums(h, 0), 3: lambda: one_over_sums(h, 1),
                    6: lambda: maxima(h, 2), 9: lambda: one_over_sums(h, 2)})
                lows(h, 0)
                if experts:
                    dve.wait_ge(q.filled, use + EACH)
                    dve.tensor_copy(s.combined[:, h:h + 1, :] if first else s.combined[:, bass.ds(h, 1), :],
                                    TB[1][0][:, :].unsqueeze(1)).then_inc(q.done, 1)
                for b in range(BATCH - AHEAD):
                    maxima(h, b + AHEAD)
                    lows(h, b + 1, (h, b))
                    one_over_sums(h, b + AHEAD)

            layer_norm_vector(dve, ln, ql, s.x, xn)
            pair(0, True)
            with dve.Fori(1, HEADS) as h:
                pair(h, False)
            lows(HEADS - 1, BATCH - 2, (HEADS - 1, BATCH - 3))
            lows(HEADS - 1, BATCH - 1, (HEADS - 1, BATCH - 2))
            outputs(HEADS - 1, BATCH - 1)
            dve.wait_ge(q.bias_added, GROUPS * HEADS)
            add_outputs(dve, s, q, B[0:4], base(HEADS))


def layer2_ffn(nc, s, dram):
    PAIRS = EXPERTS // 2
    with ExitStack() as ctx:
        def sb(name, shape, dt=F32):
            return ctx.enter_context(nc.sbuf_tensor(f"f2_{name}", shape, dt))

        sem = ctx.enter_context(phase_semaphores(nc, "f2_"))
        xn = sb("xn", [P, TILES, D])
        cH = sb("cH", [P, KT, PAIRS, 2 * D], F32R)
        cL = sb("cL", [P, KT, PAIRS, 2 * D], F32R)
        gates = sb("gates", [P, PAIRS, 2, TILES])
        ln = layer_norm_buffers(sb, "ln")
        r = router_buffers(sb, "r")
        ql = layer_norm_semaphores(sem, "ln")
        q = router_semaphores(sem, "r")
        c_high, c_cut = sem("c_high"), sem("c_cut")
        y_filled, first_added, x_added = sem("y_filled"), sem("first_added"), sem("x_added")
        B = s.banks
        block = ctx.enter_context(nc.Block())

        @block.sync
        def _(sp):
            sp.dma_start(r.raw[:], dram["f2_gate"]).then_inc(q.loaded, 16)

        @block.gpsimd
        def _(pool):
            router_cut(pool, r, q)
            for e in range(EXPERTS):
                whole = s.combined[:, e, :].rearrange("p (k d) -> p k d", k=KT)
                mine = slice((e % 2) * D, (e % 2) * D + D)
                pool.tensor_tensor(cH[:, :, e // 2, mine], whole, s.ones[:, 0:1].unsqueeze(2).to_broadcast([P, KT, D]), ALU.mult).then_inc(c_high, 1)
                pool.wait_ge(c_high, e + 1)
                pool.tensor_tensor(cL[:, :, e // 2, mine], whole, cH[:, :, e // 2, mine].bitcast(F32),
                                   ALU.subtract).then_inc(c_cut, 1)

        @block.vector
        def _(dve):
            def add_pair(p):
                for i in range(TILES):
                    n = TILES * p + i
                    dve.wait_ge(y_filled, n + 1)
                    for j in range(2):
                        gate = gates[:, p:p + 1, j, i:i + 1] if isinstance(p, int) else gates[:, bass.ds(p, 1), j, i:i + 1]
                        if j == 1:
                            dve.wait_ge(first_added, n + 1)
                        dve.scalar_tensor_tensor(s.x[:, i, :], B[i][:, j * D:(j + 1) * D], gate.rearrange("p a b -> p (a b)"),
                                                 s.x[:, i, :], ALU.mult, ALU.add).then_inc(x_added if j else first_added, 1)

            layer_norm_vector(dve, ln, ql, s.x, xn)
            turn_vector(dve, ql, B[3:7], s.xnTH, s.xnTL)
            at = router_exps(dve, r, q, B[7])
            at = router_ranks(dve, s, r, q, r.logits[:], at)
            dve.wait_ge(q.exps, 1)
            router_keep_two(dve, r, q, at, r.exps[:], gates[:].rearrange("p a b t -> p t (a b)"), 0.0)
            dve.wait_ge(q.kept, 1)
            add_pair(0)
            with dve.Fori(1, PAIRS) as p:
                add_pair(p)

        @block.scalar
        def _(act):
            layer_norm_scalar(act, ln, ql)
            turn_scalar(act, ql, B[3:7], s.xnTH)
            router_scalar(act, r, q, B[3:7])

        @block.tensor
        def _(pe):
            def two_experts(p):
                pe.wait_ge(c_cut, 2 * p + 2)
                here = slice(p, p + 1) if isinstance(p, int) else bass.ds(p, 1)
                for i in range(TILES):
                    tok = slice(i * P, (i + 1) * P)
                    need(pe, x_added, TILES * (p - 1) + i + 1)
                    split_products(pe, B[i][:, :], [
                        pair for k in range(KT) for pair in (
                            (s.xnTH[:, k, tok], cH[:, k, here, :].rearrange("p a d -> p (a d)")),
                            (s.xnTH[:, k, tok], cL[:, k, here, :].rearrange("p a d -> p (a d)")),
                            (s.xnTL[:, k, tok], cH[:, k, here, :].rearrange("p a d -> p (a d)")))]).then_inc(y_filled, 1)

            turn_and_route(pe, s, ql, xn, B[3:7], r, q, B[7])
            two_experts(0)
            with pe.Fori(1, PAIRS) as p:
                two_experts(p)


def layer3_ffn(nc, s, dram, out):
    ALL = EXPERTS + 1
    WIDE = KT * D
    HALF = TOK // 2
    with ExitStack() as ctx:
        def sb(name, shape, dt=F32):
            return ctx.enter_context(nc.sbuf_tensor(f"f3_{name}", shape, dt))

        sem = ctx.enter_context(phase_semaphores(nc, "f3_"))
        xn = sb("xn", [P, TILES, D])
        raw = [sb(f"raw{n}", [P, 2 * WIDE + KT]) for n in range(2)]
        uH = [sb(f"u{n}H", [P, KT, D], F32R) for n in range(2)]
        uL = [sb(f"u{n}L", [P, KT, D], F32R) for n in range(2)]
        dH = [sb(f"d{n}H", [P, KT, D], F32R) for n in range(2)]
        dL = [sb(f"d{n}L", [P, KT, D], F32R) for n in range(2)]
        hid = sb("hid", [P, 2, HALF])
        hH = [sb(f"h{n}H", [P, KT, TOK], F32R) for n in range(2)]
        hL = [sb(f"h{n}L", [P, KT, TOK], F32R) for n in range(2)]
        comb = sb("comb", [P, ALL, TILES])
        combT = sb("combT", [ALL, TOK])
        down_b = sb("down_b", [ALL, D])
        ln = layer_norm_buffers(sb, "ln")
        r = router_buffers(sb, "r")
        ql = layer_norm_semaphores(sem, "ln")
        q = router_semaphores(sem, "r")
        w_loaded = [sem(f"w_loaded{n}") for n in range(2)]
        down_b_loaded, shared_set = sem("down_b_loaded"), sem("shared_set")
        w_high, w_cut = sem("w_high"), sem("w_cut")
        up_filled, silu_done, h_high, h_cut = sem("up_filled"), sem("silu_done"), sem("h_high"), sem("h_cut")
        y_filled, x_added = sem("y_filled"), sem("x_added")
        c_turned, c_out, b_filled, b_added = sem("c_turned"), sem("c_out"), sem("b_filled"), sem("b_added")
        B = s.banks
        UB, YB = B[0:4], B[4:8]
        UPS = KT * 2
        block = ctx.enter_context(nc.Block())

        def one(e):
            return slice(e, e + 1) if isinstance(e, int) else bass.ds(e, 1)

        @block.sync
        def _(sp):
            sp.dma_start(r.raw[:], dram["f3_gate"]).then_inc(q.loaded, 16)
            for e in range(2):
                sp.dma_start(raw[e][:], dram["f3_w"][e]).then_inc(w_loaded[e], 16)
            sp.dma_start(down_b[:], dram["f3_down_b"]).then_inc(down_b_loaded, 16)

            def load(e, n):
                sp.wait_ge(w_cut, 2 * e - 2)
                sp.wait_ge(silu_done, UPS * e - UPS)
                source = dram["f3_w"][e] if isinstance(e, int) else dram["f3_w"][bass.ds(e, 1)].rearrange("a p c -> p (a c)")
                sp.dma_start(raw[n][:], source).then_inc(w_loaded[n], 16)

            load(2, 0)
            with sp.Fori(2, EXPERTS // 2 + 1) as pair:
                load(2 * pair - 1, 1)
                load(2 * pair, 0)
            for i in range(TILES):
                sp.wait_ge(x_added, TILES * (ALL - 1) + i + 1)
                sp.dma_start(out[i * P:(i + 1) * P, :], s.x[:, i, :]).then_inc(s.stored, 16)
            sp.wait_ge(s.stored, 16 * TILES)

        @block.gpsimd
        def _(pool):
            def cut(e, n):
                pool.wait_ge(w_loaded[n], 8 * (e - n) + 16)
                for at, (high, low) in enumerate(((uH[n], uL[n]), (dH[n], dL[n]))):
                    whole = raw[n][:, at * WIDE:(at + 1) * WIDE].rearrange("p (k d) -> p k d", k=KT)
                    step = 2 * e + at + 1
                    need(pool, *((up_filled, UPS * (e - 1)), (y_filled, TILES * (e - 1)))[at])
                    pool.tensor_tensor(high[:], whole, s.ones[:, 0:1].unsqueeze(2).to_broadcast([P, KT, D]),
                                       ALU.mult).then_inc(w_high, 1)
                    pool.wait_ge(w_high, step)
                    pool.tensor_tensor(low[:], whole, high[:].bitcast(F32), ALU.subtract).then_inc(w_cut, 1)

            router_cut(pool, r, q)
            pool.tensor_copy(comb[:, EXPERTS, :], s.ones[:, 0:TILES]).then_inc(shared_set, 1)
            cut(0, 0)
            cut(1, 1)
            cut(2, 0)
            with pool.Fori(2, EXPERTS // 2 + 1) as pair:
                cut(2 * pair - 1, 1)
                cut(2 * pair, 0)

        @block.tensor
        def _(pe):
            def up(e, n):
                pe.wait_ge(w_cut, 2 * e + 1)
                for u in range(UPS):
                    j, half = u // 2, HALVES[u % 2]
                    cols = slice(j * P, (j + 1) * P)
                    need(pe, silu_done, UPS * (e - 1) + u + 1)
                    split_products(pe, UB[u][:, 0:HALF], [
                        pair for k in range(KT) for pair in (
                            (uH[n][:, k, cols], s.xnTH[:, k, half]), (uH[n][:, k, cols], s.xnTL[:, k, half]),
                            (uL[n][:, k, cols], s.xnTH[:, k, half]))]).then_inc(up_filled, 1)

            def down(e, n, last=False):
                pe.wait_ge(h_cut, UPS * (e + 1))
                pe.wait_ge(w_cut, 2 * e + 2)
                for i in range(TILES):
                    tok = slice(i * P, (i + 1) * P)
                    before = i - 4 if i >= 4 else (i + 4 if i + 4 < TILES else i) - TILES
                    need(pe, x_added, TILES * e + before + 1)
                    if isinstance(e, int) and e == 0 and i in (2, 3):
                        pe.wait_ge(c_out, i - 1)
                    terms = [pair for k in range(KT) for pair in (
                        (hH[n][:, k, tok], dH[n][:, k, :]), (hH[n][:, k, tok], dL[n][:, k, :]),
                        (hL[n][:, k, tok], dH[n][:, k, :]))]
                    if last:
                        terms += [(combT[:, tok], down_b[:])]
                    split_products(pe, YB[i % 4][:, 0:D], terms).then_inc(y_filled, 1)

            turn_and_route(pe, s, ql, xn, B[0:4], r, q, B[7])
            up(0, 0)
            up(1, 1)
            pe.wait_ge(q.kept, 1)
            pe.wait_ge(shared_set, 1)
            for i in range(TILES):
                last = pe.transpose(YB[2 + i // 4][0:ALL, (i % 4) * P:(i % 4 + 1) * P], comb[:, :, i], s.ident[:])
                if i in (3, TILES - 1):
                    last.then_inc(c_turned, 1)
            down(0, 0)
            up(2, 0)
            down(1, 1)
            with pe.Fori(2, EXPERTS // 2 + 1) as pair:
                up(2 * pair - 1, 1)
                down(2 * pair - 2, 0)
                up(2 * pair, 0)
                down(2 * pair - 1, 1)
            pe.wait_ge(down_b_loaded, 16)
            down(EXPERTS, 0, True)

        @block.scalar
        def _(act):
            def hidden(e, n):
                act.wait_ge(w_loaded[n], 8 * (e - n) + 16)
                for u in range(UPS):
                    step = UPS * e + u
                    act.wait_ge(up_filled, step + 1)
                    need(act, h_cut, step - 1)
                    col = raw[n][:, 2 * WIDE + u // 2:2 * WIDE + u // 2 + 1]
                    act.activation(hid[:, u % 2, :], UB[u][:, 0:HALF], ACT.Silu, bias=col).then_inc(silu_done, 1)

            layer_norm_scalar(act, ln, ql)
            turn_scalar(act, ql, B[0:4], s.xnTH)
            router_scalar(act, r, q, B[0:4])
            hidden(0, 0)
            hidden(1, 1)
            for n in range(2):
                cols = slice(4 * P * n, min(4 * P * (n + 1), TOK))
                act.wait_ge(c_turned, n + 1)
                act.activation(combT[:, cols], YB[2 + n][0:ALL, 0:cols.stop - cols.start], ACT.Copy).then_inc(c_out, 1)
            hidden(2, 0)
            with act.Fori(2, EXPERTS // 2 + 1) as pair:
                hidden(2 * pair - 1, 1)
                hidden(2 * pair, 0)

        @block.vector
        def _(dve):
            def cut_hidden(e, n):
                for u in range(UPS):
                    step = UPS * e + u
                    at = (slice(None), u // 2, HALVES[u % 2])
                    dve.wait_ge(silu_done, step + 1)
                    dve.tensor_copy(hH[n][at], hid[:, u % 2, :]).then_inc(h_high, 1)
                    dve.wait_ge(h_high, step + 1)
                    dve.tensor_tensor(hL[n][at], hid[:, u % 2, :], hH[n][at].bitcast(F32), ALU.subtract).then_inc(h_cut, 1)

            def add(e):
                for i in range(TILES):
                    n = TILES * e + i
                    col = comb[:, one(e), i:i + 1].rearrange("p a b -> p (a b)")
                    dve.wait_ge(y_filled, n + 1)
                    need(dve, x_added, n - TILES + 1)
                    dve.scalar_tensor_tensor(s.x[:, i, :], YB[i % 4][:, 0:D], col, s.x[:, i, :],
                                             ALU.mult, ALU.add).then_inc(x_added, 1)

            layer_norm_vector(dve, ln, ql, s.x, xn)
            turn_vector(dve, ql, B[0:4], s.xnTH, s.xnTL)
            at = router_exps(dve, r, q, B[7])
            at = router_softmax(dve, r, q, at)
            at = router_ranks(dve, s, r, q, r.probs[:], at)
            router_keep_two(dve, r, q, at, r.probs[:], comb[:, 0:EXPERTS, :].rearrange("p e t -> p t e"), 1e-20)
            dve.wait_ge(q.kept, 1)
            dve.wait_ge(shared_set, 1)
            cut_hidden(0, 0)
            cut_hidden(1, 1)
            add(0)
            cut_hidden(2, 0)
            add(1)
            with dve.Fori(2, EXPERTS // 2 + 1) as pair:
                cut_hidden(2 * pair - 1, 1)
                add(2 * pair - 2)
                cut_hidden(2 * pair, 0)
                add(2 * pair - 1)
            add(EXPERTS)


def build(nc, dram, out):
    with ExitStack() as ctx:
        s = Names()
        s.x = ctx.enter_context(nc.sbuf_tensor("x_stream", [P, TILES, D], F32))
        s.ident = ctx.enter_context(nc.sbuf_tensor("ident", [P, P], F32))
        s.primed = ctx.enter_context(nc.sbuf_tensor("primed", [P, 1], F32))
        s.ones = ctx.enter_context(nc.sbuf_tensor("ones", [P, P], F32))
        s.earlier = ctx.enter_context(nc.sbuf_tensor("earlier", [P, EXPERTS, EXPERTS], F32))
        s.ctxH = ctx.enter_context(nc.sbuf_tensor("ctxH", [P, NK], F32R))
        s.ctxL = ctx.enter_context(nc.sbuf_tensor("ctxL", [P, NK], F32R))
        s.ctxT = ctx.enter_context(nc.sbuf_tensor("ctxT", [P, NK], F32R))
        s.banks = [ctx.enter_context(nc.psum_tensor(f"bank{n}", [P, 512], F32)) for n in range(8)]
        s.stored = ctx.enter_context(nc.semaphore("stored"))
        layer0_attention(nc, s, dram)
        s.xnTH = ctx.enter_context(nc.sbuf_tensor("xnTH", [P, KT, TOK], F32R))
        s.xnTL = ctx.enter_context(nc.sbuf_tensor("xnTL", [P, KT, TOK], F32R))
        with ExitStack() as quantised:
            s.w_quant = quantised.enter_context(nc.sbuf_tensor("w_quant", [P, 3, 2048], BF16))
            s.w_mean = quantised.enter_context(nc.sbuf_tensor("w_mean", [P, 3], F32))
            layer0_ffn(nc, s, dram)
            layer1_attention(nc, s, dram)
            layer1_ffn(nc, s, dram)
        with ExitStack() as combined:
            s.combined = combined.enter_context(nc.sbuf_tensor("combined", [P, EXPERTS, KT * D], F32))
            attention_heads64(nc, s, dram, 2, experts=True)
            layer2_ffn(nc, s, dram)
        attention_heads64(nc, s, dram, 3)
        layer3_ffn(nc, s, dram, out)


def tiled(np, w):
    return w.reshape(-1, P, w.shape[1]).transpose(1, 0, 2)


def attention_weights(np, wq, wk, wv):
    packs = []
    for h in range(HEADS):
        c = slice(h * P, (h + 1) * P)
        parts = [wq[0:P, c], wq[P:D, c]]
        for w in (wk, wv):
            parts += [w[0:P, c], np.concatenate([w[P:DC, c], w[P:DC, c]], axis=0)]
        packs.append(np.stack(parts, axis=1))
    return np.stack(packs, axis=0)


def repeated(np, row, rows=P):
    return np.broadcast_to(row, (rows,) + row.shape)


def laid_out(np, i):
    def column_pair(v):
        return [v[0:P], np.concatenate([v[P:], v[P:]]) if v.shape[0] == DC else v[P:]]

    a = {"x": i["x"].reshape(TOK, D)}
    rows = i["ctx_768"].reshape(NK, DC)
    a["ctx_rows"], a["ctx_cols"] = rows, rows.T
    a["ident"] = np.eye(P, dtype=np.float32)
    a["ones"] = np.ones((P, P), np.float32)
    a["earlier"] = repeated(np, np.tril(np.ones((EXPERTS, EXPERTS), np.float32), -1))
    a["a0_cols"] = np.stack([c for n in ("ln1_g", "ln1_b", "ln2_g", "ln2_b", "bq", "bk", "bv")
                             for c in column_pair(i["L0_xattn_" + n])], axis=1)
    a["a0_rows"] = repeated(np, i["L0_xattn_bo"])
    a["a0_wkv"] = np.stack([np.stack([w[0:P], np.concatenate([w[P:DC], w[P:DC]], axis=0)], axis=1)
                            for w in (i["L0_xattn_Wk"], i["L0_xattn_Wv"])], axis=1)
    for n in "qo":
        a["a0_w" + n] = i["L0_xattn_W" + n]
    a["f0_gate"] = tiled(np, i["L0_ffn_gate_w"])
    a["f0_w"] = tiled(np, np.concatenate([i["L0_ffn_w0"].T, i["L0_ffn_w1"].T], axis=1))
    a["f0_bias"] = np.concatenate([i["L0_ffn_b0"], i["L0_ffn_b1"]])[None]
    a["f1_w"] = np.stack([tiled(np, i["L1_ffn_" + n].T).reshape(P, 2048) for n in ("w_gate", "w_up", "w_down")], axis=1)
    for l, o, b in ((1, "Wout", "bout"), (2, "Wo", "bo"), (3, "Wo", "bo")):
        p = f"L{l}_xattn_"
        a[f"a{l}_w"] = attention_weights(np, i[p + "Wq"], i[p + "Wk"], i[p + "Wv"])
        a[f"a{l}_wo"] = i[p + o].reshape(HEADS, P, D)
        a[f"a{l}_bias"] = repeated(np, i[p + b])
    a["f2_gate"] = tiled(np, i["L2_ffn_w_gate"].T)
    a["f2_w"] = np.stack([np.concatenate([tiled(np, i["L2_ffn_w_in"][e]), tiled(np, i["L2_ffn_w_out"][e].T)], axis=1)
                          for e in range(EXPERTS)])
    a["f3_gate"] = tiled(np, i["L3_ffn_gate_w"].T)
    up = [*i["L3_ffn_up_w"], i["L3_ffn_sh_up_w"]]
    down = [*i["L3_ffn_down_w"], i["L3_ffn_sh_down_w"]]
    up_b = [*i["L3_ffn_up_b"], i["L3_ffn_sh_up_b"]]
    a["f3_w"] = np.stack([np.concatenate([tiled(np, u).reshape(P, -1), tiled(np, d).reshape(P, -1), b.reshape(KT, P).T], axis=1)
                          for u, d, b in zip(up, down, up_b)])
    a["f3_down_b"] = np.concatenate([i["L3_ffn_down_b"], i["L3_ffn_sh_down_b"][None]], axis=0)
    return {n: np.ascontiguousarray(v) for n, v in a.items()}


def kernel(**inputs):
    import numpy as np
    import concourse.bacc as bacc
    from concourse.bass_utils import run_bass_kernel_spmd

    nc = bacc.Bacc("TRN2", target_bir_lowering=False, num_devices=1)
    arrays = laid_out(np, {n: np.asarray(v) for n, v in inputs.items()})
    dram = {n: nc.dram_tensor(f"in_{n}", v.shape, mybir.dt.from_np(v.dtype), kind="ExternalInput").ap()
            for n, v in arrays.items()}
    out = nc.dram_tensor("out_x", (TOK, D), F32, kind="ExternalOutput").ap()
    build(nc, dram, out)
    result = run_bass_kernel_spmd(nc, [{f"in_{n}": v for n, v in arrays.items()}], core_ids=[0])
    return result.results[0]["out_x"].reshape(BATCH, SEQ, D)
```
